# Optimizing a Trainium2 kernel written in Bass

```python
import numpy as np
import jax
import jax.numpy as jnp

def _softmax(x, axis=-1):
    return jax.nn.softmax(x, axis=axis)

def _gelu(x):
    return jax.nn.gelu(x, approximate=True)

def _silu(x):
    return jax.nn.silu(x)

def _sigmoid(x):
    return jax.nn.sigmoid(x)

def _layernorm(x, axis=-1, eps=1e-05):
    m = jnp.mean(x, axis=axis, keepdims=True)
    v = jnp.var(x, axis=axis, keepdims=True)
    return (x - m) / jnp.sqrt(v + eps)

def _scatter_add(tgt, idx, src, axis=0):
    return tgt.at[idx].add(src)

def _segment_sum(src, seg, n):
    return jax.ops.segment_sum(src, seg, n)
kernel_name = 'mk_seq_postln_d1_jaxref_r8_3a94c8'

def setup_inputs(seed: int=0):
    np.random.seed(seed)
    _w = jnp.asarray

    def _L0_attn_setup():
        import jax, jax.numpy as jnp
        import numpy as np
        B, T, C = (4, 128, 128)
        HEAD_SIZE = 64
        H = C // HEAD_SIZE
        N_LAYER, LAYER_ID = (24, 12)
        D_MIX_LORA, D_DECAY_LORA = (32, 64)
        HEAD_SIZE_DIVISOR = 8
        LN_EPS = 1e-05 * HEAD_SIZE_DIVISOR ** 2

        def _wkv6(r, k, v, w, u):

            def step(S, inp):
                r_t, k_t, v_t, w_t = inp
                y = jnp.einsum('bhj,bhji->bhi', r_t, S) + jnp.sum(r_t * u * k_t, axis=-1, keepdims=True) * v_t
                decay = jnp.exp(-jnp.exp(w_t))
                S = decay[..., None] * S + k_t[..., None] * v_t[..., None, :]
                return (S, y)
            to_t = lambda a: jnp.transpose(a, (1, 0, 2, 3))
            S0 = jnp.zeros(r.shape[:1] + (r.shape[2], r.shape[3], r.shape[3]), r.dtype)
            _, ys = jax.lax.scan(step, S0, (to_t(r), to_t(k), to_t(v), to_t(w)))
            return jnp.transpose(ys, (1, 0, 2, 3))
        key = jax.random.key(seed)
        ks = jax.random.split(key, 16)
        x = jax.random.normal(ks[0], (B, T, C), jnp.float32)
        r01 = LAYER_ID / (N_LAYER - 1)
        r10 = 1.0 - LAYER_ID / N_LAYER
        ddd = np.arange(C, dtype=np.float64) / C
        time_maa_x = jnp.asarray((1.0 - ddd ** r10).astype(np.float32))
        time_maa_w = jnp.asarray((1.0 - ddd ** r10).astype(np.float32))
        time_maa_k = jnp.asarray((1.0 - ddd ** r10).astype(np.float32))
        time_maa_v = jnp.asarray((1.0 - (ddd ** r10 + 0.3 * r01)).astype(np.float32))
        time_maa_r = jnp.asarray((1.0 - ddd ** (0.5 * r10)).astype(np.float32))
        time_maa_g = jnp.asarray((1.0 - ddd ** (0.5 * r10)).astype(np.float32))
        n = np.arange(C, dtype=np.float64)
        time_decay = jnp.asarray((-6.0 + 5.0 * (n / (C - 1)) ** (0.7 + 1.3 * r01)).astype(np.float32))
        zigzag = ((n + 1) % 3 - 1) * 0.1
        time_faaaa = jnp.asarray((r01 * (1.0 - n / (C - 1)) + zigzag).astype(np.float32)).reshape(H, HEAD_SIZE)
        u = lambda k, shp: jax.random.uniform(k, shp, jnp.float32, -0.01, 0.01)
        time_maa_w1 = u(ks[1], (C, D_MIX_LORA * 5))
        time_maa_w2 = u(ks[2], (5, D_MIX_LORA, C))
        time_decay_w1 = u(ks[3], (C, D_DECAY_LORA))
        time_decay_w2 = u(ks[4], (D_DECAY_LORA, C))
        s = 1.0 / np.sqrt(C)
        Wr = jax.random.normal(ks[5], (C, C), jnp.float32) * s
        Wk = jax.random.normal(ks[6], (C, C), jnp.float32) * s
        Wv = jax.random.normal(ks[7], (C, C), jnp.float32) * s
        Wg = jax.random.normal(ks[8], (C, C), jnp.float32) * s
        Wo = jax.random.normal(ks[9], (C, C), jnp.float32) * s
        ln_w = jnp.ones((C,), jnp.float32)
        ln_b = jnp.zeros((C,), jnp.float32)
        return dict(x=x, time_maa_x=time_maa_x, time_maa_w=time_maa_w, time_maa_k=time_maa_k, time_maa_v=time_maa_v, time_maa_r=time_maa_r, time_maa_g=time_maa_g, time_maa_w1=time_maa_w1, time_maa_w2=time_maa_w2, time_decay=time_decay, time_decay_w1=time_decay_w1, time_decay_w2=time_decay_w2, time_faaaa=time_faaaa, Wr=Wr, Wk=Wk, Wv=Wv, Wg=Wg, Wo=Wo, ln_w=ln_w, ln_b=ln_b)
    _L0_attn_in = _L0_attn_setup()

    def _L0_ffn_setup():
        import jax, jax.numpy as jnp
        import numpy as np
        DIM = 128
        DEPTH = 6
        HEADS = 16
        DIM_HEAD = 64
        WINDOW = 32
        INNER = HEADS * DIM_HEAD
        DIM_INNER = int(DIM * 4 * 2 / 3)
        QK_SCALE = 8.0

        def shift_tokens(t):
            a, s = jnp.split(t, 2, -1)
            s = jnp.pad(s, ((0, 0), (1, 0), (0, 0)))[:, :-1]
            return jnp.concatenate([a, s], -1)

        def l2norm(t):
            return t / jnp.maximum(jnp.linalg.norm(t, axis=-1, keepdims=True), 1e-12)

        def rotate_half(x):
            x1, x2 = jnp.split(x, 2, -1)
            return jnp.concatenate([-x2, x1], -1)

        def rotary_tables(n):
            half = jnp.arange(0, DIM_HEAD, 2, dtype=jnp.float32)
            inv_freq = 1.0 / 10000.0 ** (half / DIM_HEAD)
            t = jnp.arange(n, dtype=jnp.float32)
            freqs = t[:, None] * inv_freq[None, :]
            freqs = jnp.concatenate([freqs, freqs], -1)
            base_scale = (half + 0.4 * DIM_HEAD) / (1.4 * DIM_HEAD)
            power = (t - n // 2) / (WINDOW // 2)
            scale = base_scale[None, :] ** power[:, None]
            scale = jnp.concatenate([scale, scale], -1)
            return (freqs, scale)

        def local_attention(q, k, v):
            b, h, n, d = q.shape
            w = WINDOW
            nw = n // w
            bq = q.reshape(b, h, nw, w, d)
            bk = k.reshape(b, h, nw, w, d)
            bv = v.reshape(b, h, nw, w, d)

            def look(t):
                p = jnp.pad(t, ((0, 0), (0, 0), (1, 0), (0, 0), (0, 0)))
                return jnp.concatenate([p[:, :, :nw], p[:, :, 1:]], axis=3)
            bk2, bv2 = (look(bk), look(bv))
            seq = jnp.arange(n).reshape(nw, w)
            seq_p = jnp.pad(seq, ((1, 0), (0, 0)), constant_values=-1)
            jt = jnp.concatenate([seq_p[:nw], seq_p[1:]], axis=1)
            it = seq[:, :, None]
            jb = jt[:, None, :]
            mask = (it < jb) | (it > jb + w) | (jb == -1)
            sim = jnp.einsum('bhwie,bhwje->bhwij', bq, bk2) * QK_SCALE
            sim = jnp.where(mask, -jnp.finfo(sim.dtype).max, sim)
            attn = jax.nn.softmax(sim, -1)
            out = jnp.einsum('bhwij,bhwje->bhwie', attn, bv2)
            return out.reshape(b, h, n, d)

        def attn_layer(x, Wqkv, qs, ksc, Wo):
            b, n, _ = x.shape
            qkv = x @ Wqkv
            q, k, v = jnp.split(qkv, 3, -1)
            sh = lambda t: t.reshape(b, n, HEADS, DIM_HEAD).transpose(0, 2, 1, 3)
            q, k, v = (sh(q), sh(k), sh(v))
            q = l2norm(q) * qs
            k = l2norm(k) * ksc
            freqs, scale = rotary_tables(n)
            cos, sin = (jnp.cos(freqs), jnp.sin(freqs))
            q = q * cos * scale + rotate_half(q) * sin * scale
            inv = 1.0 / scale
            k = k * cos * inv + rotate_half(k) * sin * inv
            out = local_attention(q, k, v)
            out = out.transpose(0, 2, 1, 3).reshape(b, n, INNER)
            return out @ Wo

        def ffn_layer(x, g, bln, W1, b1, W2, b2):
            mu = x.mean(-1, keepdims=True)
            var = ((x - mu) ** 2).mean(-1, keepdims=True)
            xn = (x - mu) / jnp.sqrt(var + 1e-05) * g + bln
            hg = xn @ W1 + b1
            a, gate = jnp.split(hg, 2, -1)
            return a * jax.nn.gelu(gate, approximate=False) @ W2 + b2
        key = jax.random.key(seed)
        ks = jax.random.split(key, 8)
        B, N = (2, 256)
        init = lambda k, shape: jax.random.normal(k, shape, jnp.float32) * 0.02
        return {'x': jax.random.normal(ks[0], (B, N, DIM), jnp.float32), 'Wqkv': init(ks[1], (DEPTH, DIM, 3 * INNER)), 'q_scale': jnp.ones((DEPTH, DIM_HEAD), jnp.float32), 'k_scale': jnp.ones((DEPTH, DIM_HEAD), jnp.float32), 'Wo': init(ks[2], (DEPTH, INNER, DIM)), 'ln_g': jnp.ones((DEPTH, DIM), jnp.float32), 'ln_b': jnp.zeros((DEPTH, DIM), jnp.float32), 'W1': init(ks[3], (DEPTH, DIM, 2 * DIM_INNER)), 'b1': jnp.zeros((DEPTH, 2 * DIM_INNER), jnp.float32), 'W2': init(ks[4], (DEPTH, DIM_INNER, DIM)), 'b2': jnp.zeros((DEPTH, DIM), jnp.float32)}
    _L0_ffn_in = _L0_ffn_setup()
    _d = {'L0_attn_x': _L0_attn_in['x'], 'L0_attn_time_maa_x': _L0_attn_in['time_maa_x'], 'L0_attn_time_maa_w': _L0_attn_in['time_maa_w'], 'L0_attn_time_maa_k': _L0_attn_in['time_maa_k'], 'L0_attn_time_maa_v': _L0_attn_in['time_maa_v'], 'L0_attn_time_maa_r': _L0_attn_in['time_maa_r'], 'L0_attn_time_maa_g': _L0_attn_in['time_maa_g'], 'L0_attn_time_maa_w1': _L0_attn_in['time_maa_w1'], 'L0_attn_time_maa_w2': _L0_attn_in['time_maa_w2'], 'L0_attn_time_decay': _L0_attn_in['time_decay'], 'L0_attn_time_decay_w1': _L0_attn_in['time_decay_w1'], 'L0_attn_time_decay_w2': _L0_attn_in['time_decay_w2'], 'L0_attn_time_faaaa': _L0_attn_in['time_faaaa'], 'L0_attn_Wr': _L0_attn_in['Wr'], 'L0_attn_Wk': _L0_attn_in['Wk'], 'L0_attn_Wv': _L0_attn_in['Wv'], 'L0_attn_Wg': _L0_attn_in['Wg'], 'L0_attn_Wo': _L0_attn_in['Wo'], 'L0_attn_ln_w': _L0_attn_in['ln_w'], 'L0_attn_ln_b': _L0_attn_in['ln_b'], 'L0_ffn_Wqkv': _L0_ffn_in['Wqkv'], 'L0_ffn_q_scale': _L0_ffn_in['q_scale'], 'L0_ffn_k_scale': _L0_ffn_in['k_scale'], 'L0_ffn_Wo': _L0_ffn_in['Wo'], 'L0_ffn_ln_g': _L0_ffn_in['ln_g'], 'L0_ffn_ln_b': _L0_ffn_in['ln_b'], 'L0_ffn_W1': _L0_ffn_in['W1'], 'L0_ffn_b1': _L0_ffn_in['b1'], 'L0_ffn_W2': _L0_ffn_in['W2'], 'L0_ffn_b2': _L0_ffn_in['b2']}
    _x0 = _d['L0_attn_x']
    _d['L0_attn_x'] = jax.random.normal(jax.random.fold_in(jax.random.key(seed), 1), (1, 2048, 128), dtype=_x0.dtype)
    del _x0
    return _d

def reference(L0_attn_x, L0_attn_time_maa_x, L0_attn_time_maa_w, L0_attn_time_maa_k, L0_attn_time_maa_v, L0_attn_time_maa_r, L0_attn_time_maa_g, L0_attn_time_maa_w1, L0_attn_time_maa_w2, L0_attn_time_decay, L0_attn_time_decay_w1, L0_attn_time_decay_w2, L0_attn_time_faaaa, L0_attn_Wr, L0_attn_Wk, L0_attn_Wv, L0_attn_Wg, L0_attn_Wo, L0_attn_ln_w, L0_attn_ln_b, L0_ffn_Wqkv, L0_ffn_q_scale, L0_ffn_k_scale, L0_ffn_Wo, L0_ffn_ln_g, L0_ffn_ln_b, L0_ffn_W1, L0_ffn_b1, L0_ffn_W2, L0_ffn_b2):

    def _L0_attn_ref(x, time_maa_x, time_maa_w, time_maa_k, time_maa_v, time_maa_r, time_maa_g, time_maa_w1, time_maa_w2, time_decay, time_decay_w1, time_decay_w2, time_faaaa, Wr, Wk, Wv, Wg, Wo, ln_w, ln_b):
        import jax, jax.numpy as jnp
        import numpy as np
        B, T, C = (4, 128, 128)
        HEAD_SIZE = 64
        H = C // HEAD_SIZE
        N_LAYER, LAYER_ID = (24, 12)
        D_MIX_LORA, D_DECAY_LORA = (32, 64)
        HEAD_SIZE_DIVISOR = 8
        LN_EPS = 1e-05 * HEAD_SIZE_DIVISOR ** 2

        def _wkv6(r, k, v, w, u):

            def step(S, inp):
                r_t, k_t, v_t, w_t = inp
                y = jnp.einsum('bhj,bhji->bhi', r_t, S) + jnp.sum(r_t * u * k_t, axis=-1, keepdims=True) * v_t
                decay = jnp.exp(-jnp.exp(w_t))
                S = decay[..., None] * S + k_t[..., None] * v_t[..., None, :]
                return (S, y)
            to_t = lambda a: jnp.transpose(a, (1, 0, 2, 3))
            S0 = jnp.zeros(r.shape[:1] + (r.shape[2], r.shape[3], r.shape[3]), r.dtype)
            _, ys = jax.lax.scan(step, S0, (to_t(r), to_t(k), to_t(v), to_t(w)))
            return jnp.transpose(ys, (1, 0, 2, 3))
        b, t, c = x.shape
        h, n = (H, HEAD_SIZE)
        xx = jnp.concatenate([jnp.zeros_like(x[:, :1]), x[:, :-1]], axis=1) - x
        xxx = x + xx * time_maa_x
        mix = jnp.tanh(xxx @ time_maa_w1).reshape(b, t, 5, D_MIX_LORA)
        m = jnp.einsum('btsd,sdc->sbtc', mix, time_maa_w2)
        xw = x + xx * (time_maa_w + m[0])
        xk = x + xx * (time_maa_k + m[1])
        xv = x + xx * (time_maa_v + m[2])
        xr = x + xx * (time_maa_r + m[3])
        xg = x + xx * (time_maa_g + m[4])
        r = xr @ Wr
        k = xk @ Wk
        v = xv @ Wv
        g = jax.nn.silu(xg @ Wg)
        w = time_decay + jnp.tanh(xw @ time_decay_w1) @ time_decay_w2
        y = _wkv6(r.reshape(b, t, h, n), k.reshape(b, t, h, n), v.reshape(b, t, h, n), w.reshape(b, t, h, n), time_faaaa)
        mu = y.mean(-1, keepdims=True)
        var = y.var(-1, keepdims=True)
        yn = ((y - mu) / jnp.sqrt(var + LN_EPS)).reshape(b, t, c) * ln_w + ln_b
        return yn * g @ Wo

    def _L0_ffn_ref(x, Wqkv, q_scale, k_scale, Wo, ln_g, ln_b, W1, b1, W2, b2):
        import jax, jax.numpy as jnp
        import numpy as np
        DIM = 128
        DEPTH = 6
        HEADS = 16
        DIM_HEAD = 64
        WINDOW = 32
        INNER = HEADS * DIM_HEAD
        DIM_INNER = int(DIM * 4 * 2 / 3)
        QK_SCALE = 8.0

        def shift_tokens(t):
            a, s = jnp.split(t, 2, -1)
            s = jnp.pad(s, ((0, 0), (1, 0), (0, 0)))[:, :-1]
            return jnp.concatenate([a, s], -1)

        def l2norm(t):
            return t / jnp.maximum(jnp.linalg.norm(t, axis=-1, keepdims=True), 1e-12)

        def rotate_half(x):
            x1, x2 = jnp.split(x, 2, -1)
            return jnp.concatenate([-x2, x1], -1)

        def rotary_tables(n):
            half = jnp.arange(0, DIM_HEAD, 2, dtype=jnp.float32)
            inv_freq = 1.0 / 10000.0 ** (half / DIM_HEAD)
            t = jnp.arange(n, dtype=jnp.float32)
            freqs = t[:, None] * inv_freq[None, :]
            freqs = jnp.concatenate([freqs, freqs], -1)
            base_scale = (half + 0.4 * DIM_HEAD) / (1.4 * DIM_HEAD)
            power = (t - n // 2) / (WINDOW // 2)
            scale = base_scale[None, :] ** power[:, None]
            scale = jnp.concatenate([scale, scale], -1)
            return (freqs, scale)

        def local_attention(q, k, v):
            b, h, n, d = q.shape
            w = WINDOW
            nw = n // w
            bq = q.reshape(b, h, nw, w, d)
            bk = k.reshape(b, h, nw, w, d)
            bv = v.reshape(b, h, nw, w, d)

            def look(t):
                p = jnp.pad(t, ((0, 0), (0, 0), (1, 0), (0, 0), (0, 0)))
                return jnp.concatenate([p[:, :, :nw], p[:, :, 1:]], axis=3)
            bk2, bv2 = (look(bk), look(bv))
            seq = jnp.arange(n).reshape(nw, w)
            seq_p = jnp.pad(seq, ((1, 0), (0, 0)), constant_values=-1)
            jt = jnp.concatenate([seq_p[:nw], seq_p[1:]], axis=1)
            it = seq[:, :, None]
            jb = jt[:, None, :]
            mask = (it < jb) | (it > jb + w) | (jb == -1)
            sim = jnp.einsum('bhwie,bhwje->bhwij', bq, bk2) * QK_SCALE
            sim = jnp.where(mask, -jnp.finfo(sim.dtype).max, sim)
            attn = jax.nn.softmax(sim, -1)
            out = jnp.einsum('bhwij,bhwje->bhwie', attn, bv2)
            return out.reshape(b, h, n, d)

        def attn_layer(x, Wqkv, qs, ksc, Wo):
            b, n, _ = x.shape
            qkv = x @ Wqkv
            q, k, v = jnp.split(qkv, 3, -1)
            sh = lambda t: t.reshape(b, n, HEADS, DIM_HEAD).transpose(0, 2, 1, 3)
            q, k, v = (sh(q), sh(k), sh(v))
            q = l2norm(q) * qs
            k = l2norm(k) * ksc
            freqs, scale = rotary_tables(n)
            cos, sin = (jnp.cos(freqs), jnp.sin(freqs))
            q = q * cos * scale + rotate_half(q) * sin * scale
            inv = 1.0 / scale
            k = k * cos * inv + rotate_half(k) * sin * inv
            out = local_attention(q, k, v)
            out = out.transpose(0, 2, 1, 3).reshape(b, n, INNER)
            return out @ Wo

        def ffn_layer(x, g, bln, W1, b1, W2, b2):
            mu = x.mean(-1, keepdims=True)
            var = ((x - mu) ** 2).mean(-1, keepdims=True)
            xn = (x - mu) / jnp.sqrt(var + 1e-05) * g + bln
            hg = xn @ W1 + b1
            a, gate = jnp.split(hg, 2, -1)
            return a * jax.nn.gelu(gate, approximate=False) @ W2 + b2
        for i in range(DEPTH):
            x = attn_layer(shift_tokens(x), Wqkv[i], q_scale[i], k_scale[i], Wo[i]) + x
            x = ffn_layer(shift_tokens(x), ln_g[i], ln_b[i], W1[i], b1[i], W2[i], b2[i]) + x
        return x
    x = L0_attn_x
    x = _layernorm(x + _L0_attn_ref(x, L0_attn_time_maa_x, L0_attn_time_maa_w, L0_attn_time_maa_k, L0_attn_time_maa_v, L0_attn_time_maa_r, L0_attn_time_maa_g, L0_attn_time_maa_w1, L0_attn_time_maa_w2, L0_attn_time_decay, L0_attn_time_decay_w1, L0_attn_time_decay_w2, L0_attn_time_faaaa, L0_attn_Wr, L0_attn_Wk, L0_attn_Wv, L0_attn_Wg, L0_attn_Wo, L0_attn_ln_w, L0_attn_ln_b), axis=-1)
    x = _layernorm(x + _L0_ffn_ref(x, L0_ffn_Wqkv, L0_ffn_q_scale, L0_ffn_k_scale, L0_ffn_Wo, L0_ffn_ln_g, L0_ffn_ln_b, L0_ffn_W1, L0_ffn_b1, L0_ffn_W2, L0_ffn_b2), axis=-1)
    return x

_drawn_inputs = setup_inputs


def setup_inputs(seed=0):
    import zlib

    import numpy as np

    out = dict(_drawn_inputs(seed))
    spreads = {'L0_attn_ln_w': (1.0, 0.2),
     'L0_attn_ln_b': (0.0, 0.1),
     'L0_ffn_q_scale': (1.0, 0.6),
     'L0_ffn_k_scale': (1.0, 0.6),
     'L0_ffn_ln_g': (1.0, 0.6),
     'L0_ffn_ln_b': (0.0, 0.8),
     'L0_ffn_b1': (0.0, 0.8),
     'L0_ffn_b2': (0.0, 0.1)}
    factors = {'L0_attn_time_maa_x': 8.0,
     'L0_attn_time_maa_w': 42.122,
     'L0_attn_time_maa_w1': 8.0,
     'L0_attn_time_maa_w2': 8.0,
     'L0_attn_time_decay_w1': 35.313,
     'L0_attn_time_decay_w2': 35.205,
     'L0_attn_time_faaaa': 3.378,
     'L0_ffn_W1': 3.674,
     'L0_ffn_W2': 3.62}
    for name, (base, spread) in spreads.items():
        noise = np.random.default_rng([zlib.crc32(name.encode()), seed]).standard_normal(out[name].shape)
        drawn = base * np.exp(spread * noise) if base else spread * noise
        out[name] = jnp.asarray(drawn.astype(out[name].dtype))
    for name, factor in factors.items():
        out[name] = (out[name] * factor).astype(out[name].dtype)
    return out
```

```python
from contextlib import ExitStack

import numpy as np

import concourse.bass as bass
from concourse import mybir

F32 = mybir.dt.float32
BF16 = mybir.dt.bfloat16
ALU = mybir.AluOpType
ACT = mybir.ActivationFunctionType
AX = mybir.AxisListType

TOKENS, DIM = 2048, 128
TILE = 128
TILES = TOKENS // TILE
HEADS, HEAD = 16, 64
PAIRS = HEADS // 2
INNER = HEADS * HEAD
DEPTH = 6
WINDOW = 32
BLOCKS = TILE // WINDOW
FFN = int(DIM * 4 * 2 / 3)
CHUNKS = [(0, 128), (128, 128), (256, FFN - 256)]
NC_ = len(CHUNKS)
STEPS = DEPTH * TILES
QK_SCALE = 8.0
LN_EPS = 1e-5
GROUP_EPS = 1e-5 * 8 ** 2
R_HEADS, R_HEAD = 2, 64
MIXES, LORA, DECAY_LORA = 5, 32, 64
MASKED = [0, 1, 2, 4, 8, 16]
MASKED_BIT = -1e30

V_MAA_X, V_MAA, V_DECAY, V_BONUS = 0, 1, 6, 7
F_W1, F_W2 = 0, 2 * FFN
F_G = F_W2 + NC_ * DIM
F_B, F_B1A, F_B1G, F_B2 = F_G + 1, F_G + 2, F_G + 2 + NC_, F_G + 2 + 2 * NC_
F_COLS = F_B2 + 1


def after(engine, semaphore, count):
    if not isinstance(count, int) or count > 0:
        engine.wait_ge(semaphore, count)


def stand_alone(engine, passed):
    engine.sem_inc(passed, 1)


def tile_of(n):
    return n % TILES


def layer_of(n):
    return n // TILES


def columns(n):
    return bass.ds(tile_of(n) * TILE + 1, TILE)


def columns_before(n):
    return bass.ds(tile_of(n) * TILE, TILE)


def build(nc, x, vectors, mix_w1, mix_w2, decay_w1, decay_w2, r_weights, r_norm, wqkv, wo, ffn, qk_scales,
          positions, carry, ident, band, level_masks, out):
    with ExitStack() as ctx:
        def sb(name, shape, dtype=F32):
            return ctx.enter_context(nc.sbuf_tensor(name, shape, dtype))

        def sem(name):
            return ctx.enter_context(nc.semaphore(name))

        xa = sb("xa", [128, TOKENS + 1])
        xb = sb("xb", [128, TOKENS + 1])
        x_tok = sb("x_tok", [128, TILES, DIM])
        identity = sb("identity", [128, 128])
        identity_bf = sb("identity_bf", [128, 128], BF16)
        band_f = sb("band_f", [128, 2, 2 * WINDOW])
        band_bf = sb("band_bf", [128, 2, 2 * WINDOW], BF16)
        averager = sb("averager", [128, 128])
        minus_half = sb("minus_half", [128, 128])

        proj_a = ctx.enter_context(nc.psum_tensor("proj_a", [128, 2, 512], F32))
        proj_b = ctx.enter_context(nc.psum_tensor("proj_b", [128, 2, 512], F32))
        att = ctx.enter_context(nc.psum_tensor("att", [128, 2, 512], F32))
        turn = ctx.enter_context(nc.psum_tensor("turn", [128, 2, 512], F32))

        constants_in = sem("constants_in")
        passed = sem("passed")
        constants_made = sem("constants_made")
        x_in = [sem(f"x_in{g}") for g in range(4)]

        time_mix(nc, ctx, locals())
        layers(nc, ctx, locals())
        last_norm(nc, ctx, locals())


def time_mix(nc, ctx, given):
    x, vectors, mix_w1, mix_w2, decay_w1, decay_w2, r_weights, r_norm, ident, band, level_masks = (
        given[k] for k in ("x", "vectors", "mix_w1", "mix_w2", "decay_w1", "decay_w2", "r_weights", "r_norm",
                           "ident", "band", "level_masks"))
    xa, xb, x_tok, identity, identity_bf, band_f, band_bf, averager, minus_half = (
        given[k] for k in ("xa", "xb", "x_tok", "identity", "identity_bf", "band_f", "band_bf", "averager",
                           "minus_half"))
    proj_a, proj_b, att, turn = (given[k] for k in ("proj_a", "proj_b", "att", "turn"))
    constants_in, constants_made, x_in, passed = (
        given[k] for k in ("constants_in", "constants_made", "x_in", "passed"))

    with ExitStack() as own:
        def sb(name, shape, dtype=F32):
            return own.enter_context(nc.sbuf_tensor(name, shape, dtype))

        def sem(name):
            return ctx.enter_context(nc.semaphore(name))

        vec = sb("vec", [128, 8])
        w1 = sb("w1", [128, MIXES * LORA])
        w2_wide = sb("w2_wide", [128, MIXES, DIM])
        dw1 = sb("dw1", [128, DECAY_LORA])
        dw2 = sb("dw2", [DECAY_LORA, DIM])
        wr = sb("wr", [128, 5, DIM])
        norm_rows = sb("norm_rows", [128, 2, DIM])
        masks = sb("masks", [128, len(MASKED), WINDOW])

        xx = sb("xx", [128, TILE])
        x_mixed = sb("x_mixed", [128, TILE])
        mix = sb("mix", [128, TILE])
        mix_last = sb("mix_last", [LORA, TILE])
        shifted = sb("shifted", [128, MIXES, TILE])
        shifted2 = sb("shifted2", [128, MIXES, TILE])
        streams = sb("streams", [128, MIXES, TILE])
        low = sb("low", [DECAY_LORA, TILE])
        rate = sb("rate", [128, TILE])
        decay = [sb(f"decay{i}", [128, TILE >> i]) for i in range(8)]
        rf = sb("rf", [128, TILE])
        rf_bonus = sb("rf_bonus", [128, TILE])
        kf = sb("kf", [128, TILE])
        v_tok = sb("v_tok", [128, DIM])
        gate_t = sb("gate_t", [128, DIM])
        gate_s = sb("gate_s", [128, DIM])
        gate = sb("gate", [128, DIM])
        cut = sb("cut", [128, R_HEADS, len(MASKED), WINDOW])
        coef = sb("coef", [128, R_HEADS, TILE])
        k_tok = sb("k_tok", [128, DIM])
        state = sb("state", [128, DIM])
        stats = sb("stats", [128, R_HEADS, 6])
        moments = sb("moments", [128, R_HEADS, 2])
        var_eps = sb("var_eps", [128, R_HEADS])
        rstd = sb("rstd", [128, R_HEADS])
        y_n = sb("y_n", [128, DIM])
        y_w = sb("y_w", [128, DIM])
        y_b = sb("y_b", [128, DIM])
        y_g = sb("y_g", [128, DIM])
        y_t = sb("y_t", [128, TILE])
        res = sb("res", [128, DIM])
        stats2 = sb("stats2", [128, 6])
        moments2 = sb("moments2", [128, 2])
        var_eps2 = sb("var_eps2", [128, 1])
        rstd2 = sb("rstd2", [128, 1])
        x_one = sb("x_one", [128, DIM])

        weights_in = sem("weights_in")
        zeroed, converted, cleared = sem("zeroed"), sem("converted"), sem("cleared_r")
        w2_in = sem("w2_in")
        x_turned, x_laid = sem("x_turned"), sem("x_laid")
        s_xx, s_xmix = sem("s_xx"), sem("s_xmix")
        s_low_mix, s_mix, s_mix_up = sem("s_low_mix"), sem("s_mix"), sem("s_mix_up")
        s_add, s_mul, s_streams = sem("s_add"), sem("s_mul"), sem("s_streams")
        s_lora1, s_lora_t, s_lora2 = sem("s_lora1"), sem("s_lora_t"), sem("s_lora2")
        s_rate, s_decay = sem("s_rate"), sem("s_decay")
        s_rk, s_vg = sem("s_rk"), sem("s_vg")
        s_r, s_rb, s_k, s_v = sem("s_r"), sem("s_rb"), sem("s_k"), sem("s_v")
        s_gt, s_gs, s_gate = sem("s_gt"), sem("s_gs"), sem("s_gate")
        s_level, s_scaled = sem("s_level"), sem("s_scaled")
        s_cut, s_coef, s_coef_far = sem("s_cut"), sem("s_coef"), sem("s_coef_far")
        s_kturn, s_ktok, s_y, s_su, s_state = (sem(k) for k in ("s_kturn", "s_ktok", "s_y", "s_su", "s_state"))
        s_stat, s_mom, s_ve, s_pow, s_yn, s_yw, s_yb, s_yg = (
            sem(k) for k in ("s_stat", "s_mom", "s_ve", "s_pow", "s_yn", "s_yw", "s_yb", "s_yg"))
        s_yturn, s_yt, s_out, s_res = (sem(k) for k in ("s_yturn", "s_yt", "s_out", "s_res"))
        s_stat2, s_mom2, s_ve2, s_pow2, s_one, s_keep, s_oturn, s_done = (
            sem(k) for k in ("s_stat2", "s_mom2", "s_ve2", "s_pow2", "s_one", "s_keep", "s_oturn", "s_done"))
        LEVELS = 7

        def levels_of(buffer, b):
            return buffer[:, :].rearrange("p (m two b) -> p m two b", two=2, b=b)

        with nc.Block() as block:
            @block.sync
            def _(sp):
                for g in range(4):
                    sp.dma_start(x_tok[:, 4 * g:4 * g + 4, :],
                                 x[0, 512 * g:512 * g + 512, :].rearrange("(t p) c -> p t c", p=TILE)).then_inc(x_in[g], 16)
                sp.dma_start(vec[:, :], vectors).then_inc(weights_in, 16)
                sp.dma_start(w1[:, :], mix_w1).then_inc(weights_in, 16)
                sp.dma_start(dw1[:, :], decay_w1).then_inc(weights_in, 16)
                sp.dma_start(dw2[:, :], decay_w2).then_inc(weights_in, 16)
                sp.dma_start(wr[:, :, :], r_weights.rearrange("w i o -> i w o")).then_inc(weights_in, 16)
                sp.dma_start(norm_rows[:, :, :], r_norm.partition_broadcast(128)).then_inc(weights_in, 16)
                sp.dma_start(masks[:, :, :], level_masks).then_inc(weights_in, 16)
                sp.wait_ge(zeroed, 1)
                for s in range(MIXES):
                    row = LORA * (s % 4)
                    sp.dma_start(w2_wide[row:row + LORA, s, :], mix_w2[s]).then_inc(w2_in, 16)

            @block.gpsimd
            def _(pool):
                pool.memset(w2_wide[:, :, :], 0.0).then_inc(zeroed, 1)
                pool.memset(averager[:, :], 1.0 / DIM).then_inc(constants_made, 1)
                pool.memset(minus_half[:, :], -0.5).then_inc(constants_made, 1)
                pool.wait_ge(constants_made, 2)
                with pool.Fori(0, TILES) as c:
                    pool.wait_ge(s_ve, c * 2 + 2)
                    pool.tensor_tensor(rstd[:, :], var_eps[:, :], minus_half[:, 0:R_HEADS], ALU.pow).then_inc(s_pow, 1)
                    pool.wait_ge(s_ve2, c + 1)
                    pool.tensor_tensor(rstd2[:, :], var_eps2[:, :], minus_half[:, 0:1], ALU.pow).then_inc(s_pow2, 1)

            @block.scalar
            def _(act):
                act.dma_start(identity[:, :], ident).then_inc(constants_in, 16)
                act.dma_start(band_f[:, :, :], band).then_inc(constants_in, 16)
                for g in range(4):
                    act.wait_ge(x_turned, g + 1)
                    act.copy(xb[:, 1 + 512 * g:1 + 512 * g + 512], turn[:, g % 2, :]).then_inc(x_laid, 1)
                act.wait_ge(weights_in, 16 * 7)
                with act.Fori(0, TILES) as c:
                    act.wait_ge(s_low_mix, c + 1)
                    act.activation(mix[:, :], turn[:, 0, 0:TILE], ACT.Tanh).then_inc(s_mix, 1)
                    act.activation(mix_last[:, :], turn[0:LORA, 0, TILE:2 * TILE], ACT.Tanh).then_inc(s_mix, 1)
                    act.wait_ge(s_lora1, c + 1)
                    act.activation(low[:, :], turn[0:DECAY_LORA, 1, 0:TILE], ACT.Tanh).then_inc(s_lora_t, 1)
                    act.wait_ge(s_lora2, c + 1)
                    act.activation(rate[:, :], turn[:, 1, TILE:2 * TILE], ACT.Exp,
                                   bias=vec[:, V_DECAY:V_DECAY + 1]).then_inc(s_rate, 1)
                    act.wait_ge(s_rate, c + 1)
                    act.activation(decay[0][:, :], rate[:, :], ACT.Exp, scale=-1.0).then_inc(s_decay, 1)
                    act.wait_ge(s_vg, c + 1)
                    act.copy(v_tok[:, :], proj_b[:, 1, 0:DIM]).then_inc(s_v, 1)
                    act.activation(gate_t[:, :], proj_b[:, 1, DIM:2 * DIM], ACT.Tanh, scale=0.5).then_inc(s_gt, 1)
                    act.wait_ge(s_level, c * 8 + 8)
                    act.wait_ge(s_cut, c + 1)
                    act.copy(coef[0:32, :, 32:64], att[0:32, :, 192:224]).then_inc(s_coef_far, 1)
                    act.copy(coef[64:96, :, 96:128], att[64:96, :, 192:224]).then_inc(s_coef_far, 1)
                    act.copy(coef[0:64, :, 64:128], att[0:64, :, 256:320]).then_inc(s_coef_far, 1)
                    act.wait_ge(s_kturn, c + 1)
                    act.copy(k_tok[:, :], turn[:, 0, 0:DIM]).then_inc(s_ktok, 1)
                    act.wait_ge(s_yturn, c + 1)
                    act.copy(y_t[:, :], turn[:, 1, 0:TILE]).then_inc(s_yt, 1)
                    act.wait_ge(s_oturn, c + 1)
                    act.copy(xa[:, bass.ds(c * TILE + 1, TILE)], turn[:, 0, 0:TILE]).then_inc(s_done, 1)

            @block.vector
            def _(dve):
                dve.memset(xa[:, 0:1], 0.0).then_inc(cleared, 1)
                dve.memset(xb[:, 0:1], 0.0).then_inc(cleared, 1)
                dve.memset(coef[:, :, :], 0.0).then_inc(cleared, 1)
                dve.memset(state[:, :], 0.0).then_inc(cleared, 1)
                dve.wait_ge(constants_in, 32)
                dve.tensor_copy(identity_bf[:, :], identity[:, :]).then_inc(converted, 1)
                dve.tensor_copy(band_bf[:, :, :], band_f[:, :, :]).then_inc(converted, 1)
                dve.wait_ge(weights_in, 16 * 7)
                dve.wait_ge(cleared, 4)
                dve.wait_ge(x_laid, 4)
                maa = vec[:, V_MAA:V_MAA + MIXES].unsqueeze(2).broadcast_to([128, MIXES, TILE])
                with dve.Fori(0, TILES) as c:
                    here = xb[:, bass.ds(c * TILE + 1, TILE)]
                    dve.tensor_tensor(xx[:, :], xb[:, bass.ds(c * TILE, TILE)], here, ALU.subtract).then_inc(s_xx, 1)
                    dve.wait_ge(s_xx, c + 1)
                    dve.scalar_tensor_tensor(x_mixed[:, :], xx[:, :], vec[:, V_MAA_X:V_MAA_X + 1], here,
                                             ALU.mult, ALU.add).then_inc(s_xmix, 1)
                    dve.wait_ge(s_mix_up, c + 1)
                    wide = proj_a[:, :, :].rearrange("p a b -> p (a b)")[:, 0:MIXES * TILE].rearrange(
                        "p (s t) -> p s t", s=MIXES)
                    dve.tensor_tensor(shifted[:, :, :], wide, maa, ALU.add).then_inc(s_add, 1)
                    dve.wait_ge(s_add, c + 1)
                    dve.tensor_tensor(shifted2[:, :, :], shifted[:, :, :],
                                      xx[:, :].unsqueeze(1).broadcast_to([128, MIXES, TILE]),
                                      ALU.mult).then_inc(s_mul, 1)
                    dve.wait_ge(s_mul, c + 1)
                    dve.tensor_tensor(streams[:, :, :], shifted2[:, :, :],
                                      here.unsqueeze(1).broadcast_to([128, MIXES, TILE]),
                                      ALU.add).then_inc(s_streams, 1)
                    dve.wait_ge(s_rk, c + 1)
                    dve.tensor_copy(rf[:, :], proj_b[:, 0, 0:TILE]).then_inc(s_r, 1)
                    dve.tensor_scalar(rf_bonus[:, :], proj_b[:, 0, 0:TILE], vec[:, V_BONUS:V_BONUS + 1], None,
                                      ALU.mult).then_inc(s_rb, 1)
                    dve.tensor_copy(kf[:, :], proj_b[:, 0, TILE:2 * TILE]).then_inc(s_k, 1)
                    dve.wait_ge(s_gt, c + 1)
                    dve.tensor_scalar(gate_s[:, :], gate_t[:, :], 0.5, 0.5, ALU.mult, ALU.add).then_inc(s_gs, 1)
                    dve.wait_ge(s_gs, c + 1)
                    dve.tensor_tensor(gate[:, :], gate_s[:, :], proj_b[:, 1, DIM:2 * DIM], ALU.mult).then_inc(s_gate, 1)
                    dve.wait_ge(s_decay, c + 1)
                    for i in range(LEVELS):
                        b = 1 << i
                        r_v, k_v = levels_of(rf, b), levels_of(kf, b)
                        pairs = TILE // (2 * b)
                        d_v = decay[i][:, :].rearrange("p (m two) -> p m two", two=2)
                        dve.wait_ge(s_level, c * 8 + i + 2)
                        if i:
                            dve.wait_ge(s_scaled, c * 3 * LEVELS + 3 * i)
                        dve.tensor_tensor(r_v[:, :, 1, :], r_v[:, :, 1, :],
                                          d_v[:, :, 0:1].broadcast_to([128, pairs, b]), ALU.mult).then_inc(s_scaled, 1)
                        dve.tensor_tensor(k_v[:, :, 0, :], k_v[:, :, 0, :],
                                          d_v[:, :, 1:2].broadcast_to([128, pairs, b]), ALU.mult).then_inc(s_scaled, 1)
                        dve.tensor_tensor(decay[i + 1][:, :], d_v[:, :, 0], d_v[:, :, 1], ALU.mult).then_inc(s_scaled, 1)
                    dve.tensor_tensor(cut[:, :, :, :],
                                      att[:, :, 0:192].rearrange("p h (l t) -> p h l t", t=WINDOW),
                                      masks[:, :, :].unsqueeze(1).broadcast_to([128, R_HEADS, len(MASKED), WINDOW]),
                                      ALU.mult).then_inc(s_cut, 1)
                    dve.wait_ge(s_cut, c + 1)
                    for q in range(BLOCKS):
                        p = slice(WINDOW * q, WINDOW * q + WINDOW)
                        dve.tensor_reduce(coef[p, :, p], cut[p, :, :, :].rearrange("p h l t -> p h t l"),
                                          AX.X, ALU.add).then_inc(s_coef, 1)
                    dve.wait_ge(s_su, c + 1)
                    dve.wait_ge(s_scaled, c * 3 * LEVELS + 3 * LEVELS)
                    for h in range(R_HEADS):
                        p = slice(R_HEAD * h, R_HEAD * h + R_HEAD)
                        dve.scalar_tensor_tensor(state[p, p], state[p, p], decay[LEVELS][p, 0:1],
                                                 turn[p, 1, TILE + R_HEAD * h:TILE + R_HEAD * h + R_HEAD],
                                                 ALU.mult, ALU.add).then_inc(s_state, 1)
                    for h in range(R_HEADS):
                        dve.bn_stats(stats[:, h, :], proj_a[:, 0, R_HEAD * h:R_HEAD * h + R_HEAD]).then_inc(s_stat, 1)
                    dve.wait_ge(s_stat, c * 2 + 2)
                    stand_alone(dve, passed)
                    for h in range(R_HEADS):
                        dve.bn_aggr(moments[:, h, :], stats[:, h, :]).then_inc(s_mom, 1)
                    for h in range(R_HEADS):
                        dve.wait_ge(s_mom, c * 2 + h + 1)
                        dve.tensor_scalar(var_eps[:, h:h + 1], moments[:, h, 1:2], GROUP_EPS, None,
                                          ALU.add).then_inc(s_ve, 1)
                    dve.wait_ge(s_pow, c + 1)
                    for h in range(R_HEADS):
                        p = slice(R_HEAD * h, R_HEAD * h + R_HEAD)
                        dve.tensor_scalar(y_n[:, p], proj_a[:, 0, p], moments[:, h, 0:1], rstd[:, h:h + 1],
                                          ALU.subtract, ALU.mult).then_inc(s_yn, 1)
                    dve.wait_ge(s_yn, c * 2 + 2)
                    dve.tensor_tensor(y_w[:, :], y_n[:, :], norm_rows[:, 0, :], ALU.mult).then_inc(s_yw, 1)
                    dve.wait_ge(s_yw, c + 1)
                    dve.tensor_tensor(y_b[:, :], y_w[:, :], norm_rows[:, 1, :], ALU.add).then_inc(s_yb, 1)
                    dve.wait_ge(s_yb, c + 1)
                    dve.wait_ge(s_gate, c + 1)
                    dve.tensor_tensor(y_g[:, :], y_b[:, :], gate[:, :], ALU.mult).then_inc(s_yg, 1)
                    dve.wait_ge(s_out, c + 1)
                    dve.tensor_tensor(res[:, :], proj_a[:, 1, 0:DIM], x_tok[:, c, :], ALU.add).then_inc(s_res, 1)
                    dve.wait_ge(s_res, c + 1)
                    dve.bn_stats(stats2[:, :], res[:, :]).then_inc(s_stat2, 1)
                    dve.wait_ge(s_stat2, c + 1)
                    stand_alone(dve, passed)
                    dve.bn_aggr(moments2[:, :], stats2[:, :]).then_inc(s_mom2, 1)
                    dve.wait_ge(s_mom2, c + 1)
                    dve.tensor_scalar(var_eps2[:, :], moments2[:, 1:2], LN_EPS, None, ALU.add).then_inc(s_ve2, 1)
                    dve.wait_ge(s_pow2, c + 1)
                    dve.tensor_scalar(x_one[:, :], res[:, :], moments2[:, 0:1], rstd2[:, 0:1],
                                      ALU.subtract, ALU.mult).then_inc(s_one, 1)
                    dve.wait_ge(s_one, c + 1)
                    stand_alone(dve, passed)
                    dve.tensor_copy(x_tok[:, c, :], x_one[:, :]).then_inc(s_keep, 1)

            @block.tensor
            def _(pe):
                pe.wait_ge(constants_in, 32)
                for g in range(4):
                    pe.wait_ge(x_in[g], 16)
                    if g >= 2:
                        pe.wait_ge(x_laid, g - 1)
                    for j in range(4):
                        mm = pe.transpose(turn[:, g % 2, TILE * j:TILE * j + TILE], x_tok[:, 4 * g + j, :], identity[:, :])
                    mm.then_inc(x_turned, 1)
                pe.wait_ge(x_laid, 4)
                pe.wait_ge(weights_in, 16 * 7)
                pe.wait_ge(w2_in, 16 * MIXES)

                def level(c, i, r_buffer):
                    for h in range(R_HEADS):
                        rows = slice(R_HEAD * h, R_HEAD * h + R_HEAD)
                        for q in range(BLOCKS):
                            cols = slice(WINDOW * q, WINDOW * q + WINDOW)
                            mm = pe.matmul(att[cols, h, WINDOW * i:WINDOW * i + WINDOW], kf[rows, cols],
                                           r_buffer[rows, cols], start=True, stop=True)
                    mm.then_inc(s_level, 1)

                with pe.Fori(0, TILES) as c:
                    pe.wait_ge(s_xmix, c + 1)
                    pe.matmul(turn[:, 0, 0:TILE], w1[:, 0:128], x_mixed[:, :], start=True, stop=True)
                    pe.matmul(turn[0:LORA, 0, TILE:2 * TILE], w1[:, 128:160], x_mixed[:, :],
                              start=True, stop=True).then_inc(s_low_mix, 1)
                    pe.wait_ge(s_mix, c * 2 + 2)
                    for s in range(4):
                        pe.matmul(proj_a[:, 0, TILE * s:TILE * s + TILE], w2_wide[:, s, :], mix[:, :],
                                  start=True, stop=True)
                    pe.matmul(proj_a[:, 1, 0:TILE], w2_wide[0:LORA, 4, :], mix_last[:, :],
                              start=True, stop=True).then_inc(s_mix_up, 1)
                    pe.wait_ge(s_streams, c + 1)
                    pe.matmul(turn[0:DECAY_LORA, 1, 0:TILE], dw1[:, :], streams[:, 0, :],
                              start=True, stop=True).then_inc(s_lora1, 1)
                    pe.matmul(proj_b[:, 0, 0:TILE], wr[:, 0, :], streams[:, 3, :], start=True, stop=True)
                    pe.matmul(proj_b[:, 0, TILE:2 * TILE], wr[:, 1, :], streams[:, 1, :],
                              start=True, stop=True).then_inc(s_rk, 1)
                    pe.matmul(proj_b[:, 1, 0:DIM], streams[:, 2, :], wr[:, 2, :], start=True, stop=True)
                    pe.matmul(proj_b[:, 1, DIM:2 * DIM], streams[:, 4, :], wr[:, 3, :],
                              start=True, stop=True).then_inc(s_vg, 1)
                    pe.wait_ge(s_lora_t, c + 1)
                    pe.matmul(turn[:, 1, TILE:2 * TILE], dw2[:, :], low[:, :], start=True, stop=True).then_inc(s_lora2, 1)
                    pe.wait_ge(s_rb, c + 1)
                    pe.wait_ge(s_k, c + 1)
                    stand_alone(pe, passed)
                    level(c, 0, rf_bonus)
                    for i in range(5):
                        if i:
                            pe.wait_ge(s_scaled, c * 3 * LEVELS + 3 * i)
                        else:
                            pe.wait_ge(s_r, c + 1)
                        stand_alone(pe, passed)
                        level(c, i + 1, rf)
                    pe.wait_ge(s_scaled, c * 3 * LEVELS + 15)
                    stand_alone(pe, passed)
                    for h in range(R_HEADS):
                        rows = slice(R_HEAD * h, R_HEAD * h + R_HEAD)
                        for q in (0, 2):
                            mm = pe.matmul(att[WINDOW * q:WINDOW * q + WINDOW, h, 192:224],
                                           kf[rows, WINDOW * q:WINDOW * q + WINDOW],
                                           rf[rows, WINDOW * q + WINDOW:WINDOW * q + 2 * WINDOW], start=True, stop=True)
                    mm.then_inc(s_level, 1)
                    pe.wait_ge(s_scaled, c * 3 * LEVELS + 18)
                    stand_alone(pe, passed)
                    for h in range(R_HEADS):
                        rows = slice(R_HEAD * h, R_HEAD * h + R_HEAD)
                        mm = pe.matmul(att[0:64, h, 256:320], kf[rows, 0:64], rf[rows, 64:128], start=True, stop=True)
                    mm.then_inc(s_level, 1)
                    pe.wait_ge(s_scaled, c * 3 * LEVELS + 21)
                    pe.transpose(turn[:, 0, 0:DIM], kf[:, :], identity[:, :]).then_inc(s_kturn, 1)
                    pe.wait_ge(s_coef, c * 4 + 4)
                    pe.wait_ge(s_coef_far, c * 3 + 3)
                    pe.wait_ge(s_v, c + 1)
                    pe.matmul(proj_a[:, 0, 0:DIM], rf[:, :], state[:, :], start=True, stop=False)
                    for h in range(R_HEADS):
                        p = slice(R_HEAD * h, R_HEAD * h + R_HEAD)
                        mm = pe.matmul(proj_a[:, 0, p], coef[:, h, :], v_tok[:, p], start=False, stop=(h == 1))
                    mm.then_inc(s_y, 1)
                    pe.wait_ge(s_ktok, c + 1)
                    pe.matmul(turn[:, 1, TILE:2 * TILE], k_tok[:, :], v_tok[:, :], start=True, stop=True).then_inc(s_su, 1)
                    pe.wait_ge(s_yg, c + 1)
                    pe.transpose(turn[:, 1, 0:TILE], y_g[:, :], identity[:, :]).then_inc(s_yturn, 1)
                    pe.wait_ge(s_yt, c + 1)
                    pe.matmul(proj_a[:, 1, 0:DIM], y_t[:, :], wr[:, 4, :], start=True, stop=True).then_inc(s_out, 1)
                    pe.wait_ge(s_one, c + 1)
                    pe.transpose(turn[:, 0, 0:TILE], x_one[:, :], identity[:, :]).then_inc(s_oturn, 1)
                    pe.wait_ge(s_done, c + 1)


def layers(nc, ctx, given):
    wqkv, wo, ffn, qk_scales, positions, carry = (
        given[k] for k in ("wqkv", "wo", "ffn", "qk_scales", "positions", "carry"))
    xa, xb, identity, identity_bf, band_bf, averager, minus_half = (
        given[k] for k in ("xa", "xb", "identity", "identity_bf", "band_bf", "averager", "minus_half"))
    proj_a, proj_b, att, turn = (given[k] for k in ("proj_a", "proj_b", "att", "turn"))
    constants_in, passed = given["constants_in"], given["passed"]

    with ExitStack() as own:
        def sb(name, shape, dtype=F32):
            return own.enter_context(nc.sbuf_tensor(name, shape, dtype))

        def sem(name):
            return ctx.enter_context(nc.semaphore(name))

        w_qkv = sb("w_qkv", [128, 3 * INNER])
        w_o = sb("w_o", [128, PAIRS, DIM])
        w_ffn = sb("w_ffn", [128, F_COLS])
        scales = sb("scales", [128, DEPTH, 4, HEAD])
        where = sb("where", [128, TILES, 4, HEAD])
        carry_scale = sb("carry_scale", [128, 1])

        shift_a = [sb(f"shift_a{i}", [128, TILE]) for i in range(2)]
        turns = [sb(f"turns{i}", [128, 4, HEAD]) for i in range(2)]
        squares = [sb(f"squares{i}", [128, HEADS, HEAD]) for i in range(2)]
        sums = sb("sums", [128, 2, HEADS])
        sums_min = sb("sums_min", [128, 2, HEADS])
        inv_norm = sb("inv_norm", [128, 2, HEADS])
        unit = [sb(f"unit{i}", [128, HEADS, HEAD]) for i in range(2)]
        along = [sb(f"along{i}", [128, HEADS, HEAD]) for i in range(2)]
        across = [sb(f"across{i}", [128, HEADS, HEAD]) for i in range(2)]
        rotated = [sb(f"rotated{i}", [128, HEADS, HEAD]) for i in range(2)]
        q_t = sb("q_t", [128, PAIRS, TILE])
        k_t = sb("k_t", [128, PAIRS, WINDOW + TILE])
        v_tok = [sb(f"val{i}", [128, 2, PAIRS, HEAD]) for i in range(2)]
        v_win = sb("v_win", [128, BLOCKS, PAIRS * HEAD])
        row_max = sb("row_max", [128, HEADS])
        logits = sb("logits", [128, 2, PAIRS, 2 * WINDOW])
        probs = sb("probs", [128, PAIRS, 2, 2 * WINDOW])
        mass = sb("mass", [128, HEADS])
        inv_mass = sb("inv_mass", [128, HEADS])
        p_t = sb("p_t", [128, PAIRS, TILE])
        heads_out = sb("heads_out", [128, PAIRS, 2, HEAD])
        o_t = sb("o_t", [128, PAIRS, TILE])
        shift_f = sb("shift_f", [128, TILE])
        dev = sb("dev", [128, TILE])
        dev_sq = sb("dev_sq", [128, TILE])
        var_f = sb("var_f", [128, TILE])
        rstd_f = sb("rstd_f", [128, TILE])
        norm_g = sb("norm_g", [128, TILE])
        normed = sb("normed", [128, TILE])
        gelu = sb("gelu", [128, NC_, TILE])
        hidden = sb("hidden", [128, NC_, TILE])

        tables_in = sem("tables_in")
        qkv_in, wo_in, ffn_in = sem("qkv_in"), sem("wo_in"), sem("ffn_in")
        cleared = sem("cleared")
        shifted = sem("shifted")
        table_made = sem("table_made")
        q_projected, k_projected, v_projected = sem("q_projected"), sem("k_projected"), sem("v_projected")
        squared = [sem("q_squared"), sem("k_squared")]
        summed = [sem("q_summed"), sem("k_summed")]
        bounded = [sem("q_bounded"), sem("k_bounded")]
        inverted = [sem("q_inverted"), sem("k_inverted")]
        united = [sem("q_united"), sem("k_united")]
        alonged = [sem("q_alonged"), sem("k_alonged")]
        acrossed = [sem("q_acrossed"), sem("k_acrossed")]
        turned_in = [sem("q_rotated"), sem("k_rotated")]
        q_turned, q_laid = sem("q_turned"), sem("q_laid")
        k_turned, k_laid, k_carried = sem("k_turned"), sem("k_laid"), sem("k_carried")
        v_laid, v_spread = sem("v_laid"), sem("v_spread")
        scored, maxed, centred, weighed = sem("scored"), sem("maxed"), sem("centred"), sem("weighed")
        massed, mass_inverted = sem("massed"), sem("mass_inverted")
        p_turned, p_laid, mixed, scaled_out = sem("p_turned"), sem("p_laid"), sem("mixed"), sem("scaled_out")
        o_turned, o_laid, attended, xb_ready = sem("o_turned"), sem("o_laid"), sem("attended"), sem("xb_ready")
        f_shifted, mean_made, deviated, dev_squared = (
            sem(k) for k in ("f_shifted", "mean_made", "deviated", "dev_squared"))
        var_made, var_kept, rstd_made, scaled_f, normed_f = (
            sem(k) for k in ("var_made", "var_kept", "rstd_made", "scaled_f", "normed_f"))
        widened, gelued, gated, narrowed, xa_ready = (
            sem(k) for k in ("widened", "gelued", "gated", "narrowed", "xa_ready"))

        slots = [proj_a, proj_b]

        def by_head(slot):
            return slot[:, :, :].rearrange("p a (h e) -> p (a h) e", e=HEAD)

        def halves(buffer):
            return buffer[:, :, :].rearrange("p h (two e) -> p h two e", two=2)

        def run(engine, step):
            step(-1, 1, False, True, False)
            step(0, 0, True, True, False)
            with engine.Fori(0, (STEPS - 2) // 2) as i:
                step(i * 2 + 1, 1, True, True, True)
                step(i * 2 + 2, 0, True, True, True)
            step(STEPS - 1, 1, True, False, True)
            step(STEPS, 0, False, False, True)

        with nc.Block() as block:
            @block.sync
            def _(sp):
                def load_qkv(layer):
                    sp.dma_start(w_qkv[:, :], wqkv[layer]).then_inc(qkv_in, 16)

                def load_wo(layer):
                    sp.dma_start(w_o[:, :, :], wo[layer].rearrange("(p i) o -> i p o", i=128)).then_inc(wo_in, 16)

                def load_ffn(layer):
                    sp.dma_start(w_ffn[:, :], ffn[layer]).then_inc(ffn_in, 16)

                def spread(m, odd):
                    now, old = v_tok[odd], v_tok[1 - odd]
                    sp.wait_ge(v_laid, m + 1)
                    after(sp, mixed, m)
                    for par in range(2):
                        base = 2 * WINDOW * par
                        own_rows = slice(base + WINDOW, base + 2 * WINDOW)
                        flat = [v[:, par, :, :].rearrange("p a e -> p (a e)") for v in (now, old)]
                        for w in range(BLOCKS):
                            sp.dma_start(v_win[own_rows, w, :],
                                         flat[0][WINDOW * w:WINDOW * w + WINDOW, :]).then_inc(v_spread, 16)
                            before = flat[0][WINDOW * (w - 1):WINDOW * w, :] if w else flat[1][TILE - WINDOW:TILE, :]
                            sp.dma_start(v_win[base:base + WINDOW, w, :], before).then_inc(v_spread, 16)

                def spread_pairs(first, last, base):
                    with sp.Fori(first // 2, last // 2) as i:
                        spread(base + i * 2, 0)
                        spread(base + i * 2 + 1, 1)

                load_qkv(0)
                sp.dma_start(carry_scale[:, :], carry).then_inc(tables_in, 16)
                sp.dma_start(where[:, :, :, :], positions).then_inc(tables_in, 16)
                sp.dma_start(scales[:, :, :, :], qk_scales.partition_broadcast(128)).then_inc(tables_in, 16)
                load_wo(0)
                load_ffn(0)
                sp.wait_ge(cleared, 3)
                spread_pairs(0, TILES, 0)
                with sp.Fori(1, DEPTH) as layer:
                    first = layer * TILES
                    sp.wait_ge(v_projected, first)
                    load_qkv(layer)
                    spread(first, 0)
                    sp.wait_ge(attended, first)
                    load_wo(layer)
                    spread(first + 1, 1)
                    sp.wait_ge(xa_ready, first)
                    load_ffn(layer)
                    spread_pairs(2, TILES, first)

            @block.gpsimd
            def _(pool):
                pool.wait_ge(tables_in, 48)

                def step(n, odd, attend, project, feed):
                    m, p = n + 1, 1 - odd
                    if feed:
                        pool.wait_ge(var_kept, n)
                        pool.tensor_tensor(rstd_f[:, :], var_f[:, :], minus_half[:, :], ALU.pow).then_inc(rstd_made, 1)
                    if not project:
                        return
                    after(pool, alonged[1], m - 1)
                    after(pool, acrossed[1], 2 * (m - 1))
                    pool.tensor_tensor(turns[p][:, :, :], where[:, tile_of(m), :, :], scales[:, layer_of(m), :, :],
                                       ALU.mult).then_inc(table_made, 1)
                    pool.wait_ge(table_made, m + 1)
                    for j in range(2):
                        pool.wait_ge(bounded[j], m + 1)
                        pool.tensor_tensor(inv_norm[:, j, :], sums_min[:, j, :], minus_half[:, 0:HEADS],
                                           ALU.pow).then_inc(inverted[j], 1)
                    for j in range(2):
                        pool.wait_ge(united[j], m + 1)
                        after(pool, turned_in[j], m)
                        u, a = halves(unit[j]), halves(across[j])
                        for half in range(2):
                            table = turns[p][:, 2 * j + 1, 32 * half:32 * half + 32].unsqueeze(1).broadcast_to(
                                [128, HEADS, 32])
                            pool.tensor_tensor(a[:, :, 1 - half, :], u[:, :, half, :], table,
                                               ALU.mult).then_inc(acrossed[j], 1)
                        pool.wait_ge(alonged[j], m + 1)
                        pool.wait_ge(acrossed[j], 2 * m + 2)
                        after(pool, (q_turned, k_turned)[j], 2 * m)
                        pool.tensor_tensor(rotated[j][:, :, :], along[j][:, :, :], across[j][:, :, :],
                                           ALU.add).then_inc(turned_in[j], 1)

                run(pool, step)

            @block.scalar
            def _(act):
                def step(n, odd, attend, project, feed):
                    m, p, f = n + 1, 1 - odd, n - 1
                    if attend:
                        for j in range(2):
                            act.wait_ge(q_turned, 2 * n + j + 1)
                            after(act, scored, n)
                            act.copy(q_t[:, 4 * j:4 * j + 4, :], turn[:, j, :].rearrange("p (a t) -> p a t", t=TILE))\
                                .then_inc(q_laid, 1)
                        for j in range(2):
                            act.wait_ge(k_turned, 2 * n + j + 1)
                            act.wait_ge(k_carried, n + 1)
                            act.copy(k_t[:, 4 * j:4 * j + 4, WINDOW:], turn[:, j, :].rearrange("p (a t) -> p a t", t=TILE))\
                                .then_inc(k_laid, 1)
                        act.wait_ge(centred, n + 1)
                        after(act, p_turned, 2 * n)
                        after(act, massed, n)
                        act.activation(probs[:, :, :, :].rearrange("p a b c -> p b a c"), logits[:, :, :, :], ACT.Exp).then_inc(weighed, 1)
                    if project:
                        for j in range(2):
                            act.wait_ge((q_projected, k_projected)[j], m + 1)
                            after(act, summed[j], m)
                            act.activation(squares[j][:, :, :], by_head(slots[j]), ACT.Square).then_inc(squared[j], 1)
                    if attend:
                        for j in range(2):
                            act.wait_ge(p_turned, 2 * n + j + 1)
                            after(act, mixed, n)
                            act.copy(p_t[:, 4 * j:4 * j + 4, :], att[:, j, :].rearrange("p (a t) -> p a t", t=TILE))\
                                .then_inc(p_laid, 1)
                    if project:
                        act.wait_ge(v_projected, m + 1)
                        after(act, v_spread, 256 * m)
                        act.copy(v_tok[p][:, :, :, :], proj_a[:, :, :].rearrange("p a (h e) -> p a h e", e=HEAD))\
                            .then_inc(v_laid, 1)
                    if feed:
                        act.wait_ge(widened, f + 1)
                        act.wait_ge(ffn_in, (layer_of(f) + 1) * 16)
                        after(act, gated, NC_ * f)
                        for i, (_, size) in enumerate(CHUNKS):
                            act.activation(gelu[0:size, i, :], turn[0:size, 1, TILE * i:TILE * i + TILE], ACT.Gelu,
                                           bias=w_ffn[0:size, F_B1G + i:F_B1G + i + 1]).then_inc(gelued, 1)
                    if attend:
                        for j in (1, 0):
                            act.wait_ge(o_turned, 2 * n + 2 - j)
                            after(act, attended, n)
                            act.copy(o_t[:, 4 * (1 - j):4 * (1 - j) + 4, :],
                                     turn[:, j, :].rearrange("p (a t) -> p a t", t=TILE)).then_inc(o_laid, 1)

                run(act, step)

            @block.vector
            def _(dve):
                dve.memset(k_t[:, :, :], 0.0).then_inc(cleared, 1)
                dve.memset(v_tok[0][:, :, :, :], 0.0).then_inc(cleared, 1)
                dve.memset(v_tok[1][:, :, :, :], 0.0).then_inc(cleared, 1)
                dve.wait_ge(cleared, 3)
                dve.wait_ge(tables_in, 48)

                def step(n, odd, attend, project, feed):
                    m, p, f = n + 1, 1 - odd, n - 1
                    if attend:
                        after(dve, scored, n)
                        after(dve, k_laid, 2 * n)
                        dve.tensor_scalar(k_t[:, :, 0:WINDOW], k_t[:, :, TILE:TILE + WINDOW], carry_scale[:, 0:1], None,
                                          ALU.mult).then_inc(k_carried, 1)
                    if feed:
                        after(dve, xb_ready, f + 1)
                        after(dve, deviated, f)
                        stand_alone(dve, passed)
                        dve.tensor_copy(shift_f[0:64, :], xb[0:64, columns(f)]).then_inc(f_shifted, 1)
                        dve.tensor_copy(shift_f[64:128, :], xb[64:128, columns_before(f)]).then_inc(f_shifted, 1)
                    if project:
                        after(dve, v_projected, m - 1)
                        after(dve, xa_ready, n - 1)
                        stand_alone(dve, passed)
                        dve.tensor_copy(shift_a[p][0:64, :], xa[0:64, columns(m)]).then_inc(shifted, 1)
                        dve.tensor_copy(shift_a[p][64:128, :], xa[64:128, columns_before(m)]).then_inc(shifted, 1)
                    if feed:
                        dve.wait_ge(mean_made, f + 1)
                        dve.wait_ge(f_shifted, 2 * f + 2)
                        after(dve, scaled_f, f)
                        dve.tensor_tensor(dev[:, :], shift_f[:, :], proj_a[:, 0, 0:TILE], ALU.subtract).then_inc(deviated, 1)
                        dve.wait_ge(deviated, f + 1)
                        dve.tensor_tensor(dev_sq[:, :], dev[:, :], dev[:, :], ALU.mult).then_inc(dev_squared, 1)
                        dve.wait_ge(var_made, f + 1)
                        dve.tensor_scalar(var_f[:, :], proj_a[:, 1, 0:TILE], LN_EPS, None, ALU.add).then_inc(var_kept, 1)
                    if attend:
                        dve.wait_ge(scored, n + 1)
                        dve.tensor_reduce(row_max[:, :], by_head(att), AX.X, ALU.max).then_inc(maxed, 1)
                        dve.wait_ge(maxed, n + 1)
                        after(dve, weighed, n)
                        dve.tensor_tensor(logits[:, :, :, :].rearrange("p a h c -> p (a h) c"), by_head(att),
                                          row_max[:, :].unsqueeze(2).broadcast_to([128, HEADS, 2 * WINDOW]),
                                          ALU.subtract).then_inc(centred, 1)
                    if feed:
                        dve.wait_ge(rstd_made, f + 1)
                        dve.wait_ge(ffn_in, (layer_of(f) + 1) * 16)
                        dve.scalar_tensor_tensor(norm_g[:, :], dev[:, :], w_ffn[:, F_G:F_G + 1], rstd_f[:, :],
                                                 ALU.mult, ALU.mult).then_inc(scaled_f, 1)
                        dve.wait_ge(scaled_f, f + 1)
                        after(dve, widened, f)
                        dve.tensor_scalar(normed[:, :], norm_g[:, :], w_ffn[:, F_B:F_B + 1], None,
                                          ALU.add).then_inc(normed_f, 1)
                    if project:
                        for j in range(2):
                            dve.wait_ge(squared[j], m + 1)
                            dve.tensor_reduce(sums[:, j, :], squares[j][:, :, :], AX.X, ALU.add).then_inc(summed[j], 1)
                            dve.wait_ge(summed[j], m + 1)
                            after(dve, inverted[j], m)
                            dve.tensor_scalar(sums_min[:, j, :], sums[:, j, :], 1e-24, None, ALU.max).then_inc(bounded[j], 1)
                        for j in range(2):
                            dve.wait_ge(inverted[j], m + 1)
                            after(dve, alonged[j], m)
                            after(dve, acrossed[j], 2 * m)
                            dve.tensor_tensor(unit[j][:, :, :], by_head(slots[j]),
                                              inv_norm[:, j, :].unsqueeze(2).broadcast_to([128, HEADS, HEAD]),
                                              ALU.mult).then_inc(united[j], 1)
                    if attend:
                        dve.wait_ge(weighed, n + 1)
                        dve.tensor_reduce(mass[:, :], probs[:, :, :, :].rearrange("p a b c -> p (a b) c"), AX.X,
                                          ALU.add).then_inc(massed, 1)
                        dve.wait_ge(massed, n + 1)
                        after(dve, scaled_out, n)
                        dve.reciprocal(inv_mass[:, :], mass[:, :]).then_inc(mass_inverted, 1)
                    if project:
                        for j in range(2):
                            dve.wait_ge(table_made, m + 1)
                            dve.wait_ge(united[j], m + 1)
                            after(dve, turned_in[j], m)
                            dve.tensor_tensor(along[j][:, :, :], unit[j][:, :, :],
                                              turns[p][:, 2 * j, :].unsqueeze(1).broadcast_to([128, HEADS, HEAD]),
                                              ALU.mult).then_inc(alonged[j], 1)
                    if feed:
                        for i, (_, size) in enumerate(CHUNKS):
                            dve.wait_ge(gelued, NC_ * f + i + 1)
                            after(dve, narrowed, f)
                            dve.scalar_tensor_tensor(hidden[0:size, i, :], turn[0:size, 0, TILE * i:TILE * i + TILE],
                                                     w_ffn[0:size, F_B1A + i:F_B1A + i + 1], gelu[0:size, i, :],
                                                     ALU.add, ALU.mult).then_inc(gated, 1)
                    if attend:
                        dve.wait_ge(mixed, n + 1)
                        dve.wait_ge(mass_inverted, n + 1)
                        after(dve, o_turned, 2 * n)
                        dve.tensor_tensor(heads_out[:, :, :, :].rearrange("p a b e -> p b a e"),
                                          att[:, :, :].rearrange("p b (a e) -> p b a e", e=HEAD),
                                          inv_mass[:, :].rearrange("p (a b) -> p b a", b=2).unsqueeze(3).broadcast_to(
                                              [128, 2, PAIRS, HEAD]), ALU.mult).then_inc(scaled_out, 1)
                    if feed:
                        dve.wait_ge(narrowed, f + 1)
                        dve.scalar_tensor_tensor(xa[:, columns(f)], turn[:, 0, 0:TILE], w_ffn[:, F_B2:F_B2 + 1],
                                                 xb[:, columns(f)], ALU.add, ALU.add).then_inc(xa_ready, 1)
                    if attend:
                        dve.wait_ge(attended, n + 1)
                        dve.tensor_tensor(xb[:, columns(n)], att[:, 0, 0:TILE], xa[:, columns(n)], ALU.add)\
                            .then_inc(xb_ready, 1)

                run(dve, step)

            @block.tensor
            def _(pe):
                mask_first, mask_other = 0, 1

                def transposes(bank, source, count, signal):
                    for j in range(4):
                        mm = pe.transpose(bank[:, TILE * j:TILE * j + TILE], source(count * 4 + j), identity[:, :])
                    mm.then_inc(signal, 1)

                def step(n, odd, attend, project, feed):
                    m, p, f = n + 1, 1 - odd, n - 1

                    def pair(buffer):
                        return lambda a: buffer[:, 2 * a:2 * a + 2, :].rearrange("p h e -> p (h e)")

                    if attend:
                        for j in range(2):
                            pe.wait_ge(turned_in[0], n + 1)
                            after(pe, o_laid, 2 * n)
                            transposes(turn[:, j, :], pair(rotated[0]), j, q_turned)
                    if feed:
                        pe.wait_ge(f_shifted, 2 * f + 2)
                        pe.wait_ge(v_laid, n + 1 if not isinstance(n, int) or n < STEPS else STEPS)
                        pe.matmul(proj_a[:, 0, 0:TILE], averager[:, :], shift_f[:, :], start=True, stop=True)\
                            .then_inc(mean_made, 1)
                    if attend:
                        for j in range(2):
                            pe.wait_ge(turned_in[1], n + 1)
                            pe.wait_ge(q_laid, 2 * n + j + 1)
                            transposes(turn[:, j, :], pair(rotated[1]), j, k_turned)
                        which = (mask_first if n == 0 else mask_other) if isinstance(n, int) else (tile_of(n) + 15) // 16
                        band = band_bf[:, which, :].unsqueeze(1).broadcast_to([128, PAIRS, 2 * WINDOW])
                        for par in range(2):
                            pe.wait_ge(k_laid, 2 * n + 2)
                            after(pe, xb_ready, n)
                            rows = slice(HEAD * par, HEAD * par + HEAD)
                            pe.matmul(att[:, par, :].rearrange("p (a c) -> p a c", a=PAIRS), identity_bf[:, :], band,
                                      start=True, stop=False, skip_group_check=True)
                            for a in range(PAIRS):
                                for w in range(BLOCKS):
                                    mm = pe.matmul(att[WINDOW * w:WINDOW * w + WINDOW, par, HEAD * a:HEAD * a + HEAD],
                                                   q_t[rows, a, WINDOW * w:WINDOW * w + WINDOW],
                                                   k_t[rows, a, WINDOW * w:WINDOW * w + 2 * WINDOW],
                                                   start=False, stop=True, skip_group_check=True)
                            if par == 0 and feed:
                                pe.wait_ge(dev_squared, f + 1)
                                pe.matmul(proj_a[:, 1, 0:TILE], averager[:, :], dev_sq[:, :], start=True, stop=True)\
                                    .then_inc(var_made, 1)
                        mm.then_inc(scored, 1)
                    elif feed:
                        pe.wait_ge(dev_squared, f + 1)
                        pe.matmul(proj_a[:, 1, 0:TILE], averager[:, :], dev_sq[:, :], start=True, stop=True)\
                            .then_inc(var_made, 1)
                    if project:
                        pe.wait_ge(shifted, 2 * m + 2)
                        pe.wait_ge(qkv_in, (layer_of(m) + 1) * 16)
                        if feed:
                            pe.wait_ge(var_kept, f + 1)
                        for j in range(2):
                            if j:
                                after(pe, united[1], m)
                            for half in range(2):
                                base = INNER * j + 512 * half
                                mm = pe.matmul(slots[j][:, half, :], shift_a[p][:, :], w_qkv[:, base:base + 512],
                                               start=True, stop=True)
                            mm.then_inc((q_projected, k_projected)[j], 1)
                    if feed:
                        pe.wait_ge(normed_f, f + 1)
                        if attend:
                            pe.wait_ge(k_laid, 2 * n + 2)
                        else:
                            pe.wait_ge(o_laid, 2 * n)
                        pe.wait_ge(ffn_in, (layer_of(f) + 1) * 16)
                        for half in range(2):
                            for i, (at, size) in enumerate(CHUNKS):
                                col = F_W1 + FFN * half + at
                                mm = pe.matmul(turn[0:size, half, TILE * i:TILE * i + TILE], w_ffn[:, col:col + size],
                                               normed[:, :], start=True, stop=True)
                        mm.then_inc(widened, 1)
                    if attend:
                        pe.wait_ge(weighed, n + 1)
                        for j in range(2):
                            transposes(att[:, j, :], lambda a: probs[:, a, :, :].rearrange("p b c -> p (b c)"), j, p_turned)
                    if project:
                        pe.wait_ge(united[0], m + 1)
                        values = w_qkv[:, 2 * INNER:].rearrange("i (a b e) -> i b a e", a=PAIRS, b=2)
                        for par in range(2):
                            mm = pe.matmul(proj_a[:, par, :].rearrange("p (a e) -> p a e", a=PAIRS), shift_a[p][:, :],
                                           values[:, par, :, :], start=True, stop=True)
                        mm.then_inc(v_projected, 1)
                    if attend:
                        pe.wait_ge(p_laid, 2 * n + 2)
                        pe.wait_ge(v_spread, 256 * n + 256)
                        stand_alone(pe, passed)
                        for par in range(2):
                            rows = slice(HEAD * par, HEAD * par + HEAD)
                            for a in range(PAIRS):
                                for w in range(BLOCKS):
                                    mm = pe.matmul(att[WINDOW * w:WINDOW * w + WINDOW, par, HEAD * a:HEAD * a + HEAD],
                                                   p_t[rows, a, WINDOW * w:WINDOW * w + WINDOW],
                                                   v_win[rows, w, HEAD * a:HEAD * a + HEAD], start=True, stop=True)
                        mm.then_inc(mixed, 1)
                    if feed:
                        pe.wait_ge(gated, NC_ * f + NC_)
                        for i, (_, size) in enumerate(CHUNKS):
                            mm = pe.matmul(turn[:, 0, 0:TILE], w_ffn[0:size, F_W2 + DIM * i:F_W2 + DIM * i + DIM],
                                           hidden[0:size, i, :], start=(i == 0), stop=(i == NC_ - 1))
                        mm.then_inc(narrowed, 1)
                    if attend:
                        pe.wait_ge(scaled_out, n + 1)
                        turned = lambda a: heads_out[:, a, :, :].rearrange("p b e -> p (b e)")
                        if not feed:
                            pe.wait_ge(k_laid, 2 * n + 2)
                        transposes(turn[:, 1, :], turned, 0, o_turned)
                        if feed:
                            pe.wait_ge(xa_ready, f + 1)
                        transposes(turn[:, 0, :], turned, 1, o_turned)
                        pe.wait_ge(o_laid, 2 * n + 2)
                        pe.wait_ge(wo_in, (layer_of(n) + 1) * 16)
                        for a in range(PAIRS):
                            mm = pe.matmul(att[:, 0, 0:TILE], w_o[:, a, :], o_t[:, a, :],
                                           start=(a == 0), stop=(a == PAIRS - 1))
                        mm.then_inc(attended, 1)

                run(pe, step)


def last_norm(nc, ctx, given):
    xa, x_tok, identity, out, att, turn = (given[k] for k in ("xa", "x_tok", "identity", "out", "att", "turn"))
    minus_half = given["minus_half"]
    GROUP = 4
    with ExitStack() as own:
        def sb(name, shape, dtype=F32):
            return own.enter_context(nc.sbuf_tensor(name, shape, dtype))

        def sem(name):
            return ctx.enter_context(nc.semaphore(name))

        total = sb("total", [128, TILES, DIM])
        stat = sb("stat", [128, TILES, 6])
        moment = sb("moment", [128, TILES, 2])
        var_l = sb("var_l", [128, TILES])
        rstd_l = sb("rstd_l", [128, TILES])
        final = sb("final", [128, TILES, DIM])
        l_turned, l_added, l_stat, l_moment, l_var, l_rstd, l_final, stored = (
            sem(k) for k in ("l_turned", "l_added", "l_stat", "l_moment", "l_var", "l_rstd", "l_final", "stored"))
        banks = [turn[:, 0, :], turn[:, 1, :], att[:, 0, :], att[:, 1, :]]
        with nc.Block() as block:
            @block.tensor
            def _(pe):
                for g in range(TILES // GROUP):
                    for j in range(GROUP):
                        t = GROUP * g + j
                        mm = pe.transpose(banks[g][:, DIM * j:DIM * j + DIM], xa[:, 1 + TILE * t:1 + TILE * t + TILE],
                                          identity[:, :])
                    mm.then_inc(l_turned, 1)

            @block.vector
            def _(dve):
                for g in range(TILES // GROUP):
                    tiles = slice(GROUP * g, GROUP * g + GROUP)
                    dve.wait_ge(l_turned, g + 1)
                    dve.tensor_tensor(total[:, tiles, :], banks[g].rearrange("p (t c) -> p t c", t=GROUP),
                                      x_tok[:, tiles, :], ALU.add).then_inc(l_added, 1)
                    dve.wait_ge(l_added, g + 1)
                    for t in range(GROUP * g, GROUP * g + GROUP):
                        dve.bn_stats(stat[:, t, :], total[:, t, :]).then_inc(l_stat, 1)
                    for t in range(GROUP * g, GROUP * g + GROUP):
                        dve.wait_ge(l_stat, t + 1)
                        dve.bn_aggr(moment[:, t, :], stat[:, t, :]).then_inc(l_moment, 1)
                    dve.wait_ge(l_moment, GROUP * g + GROUP)
                    dve.tensor_scalar(var_l[:, tiles], moment[:, tiles, 1], LN_EPS, None, ALU.add).then_inc(l_var, 1)
                for g in range(TILES // GROUP):
                    dve.wait_ge(l_rstd, g + 1)
                    for t in range(GROUP * g, GROUP * g + GROUP):
                        dve.tensor_scalar(final[:, t, :], total[:, t, :], moment[:, t, 0:1], rstd_l[:, t:t + 1],
                                          ALU.subtract, ALU.mult).then_inc(l_final, 1)

            @block.gpsimd
            def _(pool):
                for g in range(TILES // GROUP):
                    tiles = slice(GROUP * g, GROUP * g + GROUP)
                    pool.wait_ge(l_var, g + 1)
                    pool.tensor_tensor(rstd_l[:, tiles], var_l[:, tiles], minus_half[:, 0:GROUP], ALU.pow)\
                        .then_inc(l_rstd, 1)

            @block.sync
            def _(sp):
                for g in range(TILES // GROUP):
                    tiles = slice(GROUP * g, GROUP * g + GROUP)
                    sp.wait_ge(l_final, GROUP * g + GROUP)
                    sp.dma_start(out[0, 512 * g:512 * g + 512, :].rearrange("(t p) c -> p t c", p=TILE),
                                 final[:, tiles, :]).then_inc(stored, 16)
                sp.wait_ge(stored, 16 * (TILES // GROUP))


def position_tables():
    half = np.arange(0, HEAD, 2, dtype=np.float64)
    freq = 1.0 / 10000.0 ** (half / HEAD)
    t = np.arange(TOKENS, dtype=np.float64)
    angle = t[:, None] * freq[None, :]
    base = (half + 0.4 * HEAD) / (1.4 * HEAD)
    power = ((t % TILE) - TILE // 2) / (WINDOW // 2)
    scale = base[None, :] ** power[:, None]
    cos, sin = np.cos(angle), np.sin(angle)
    sign = np.concatenate([np.ones(HEAD // 2), -np.ones(HEAD // 2)])
    both = lambda a: np.concatenate([a, a], -1)
    tables = np.stack([both(cos * scale) * QK_SCALE, both(sin * scale) * sign * QK_SCALE,
                       both(cos / scale), both(sin / scale) * sign], 1)
    tables = tables.reshape(TILES, TILE, 4, HEAD).transpose(1, 0, 2, 3)
    carry = np.tile(np.concatenate([base, base]) ** (TILE // (WINDOW // 2)), 2)[:, None]
    return np.ascontiguousarray(tables, np.float32), np.ascontiguousarray(carry, np.float32)


def band_masks():
    a = np.arange(TILE)[:, None]
    c = np.arange(2 * WINDOW)[None, :]
    i = a % WINDOW
    hidden = (c - WINDOW > i) | (i > c)
    first = hidden | ((a < WINDOW) & (c < WINDOW))
    return np.stack([first, hidden], 1).astype(np.float32) * np.float32(MASKED_BIT)


def level_cuts():
    s = (np.arange(128) % WINDOW)[:, None]
    t = np.arange(WINDOW)[None, :]
    cuts = [(s == t) if b == 0 else ((t // b) % 2 == 1) & (s // b == t // b - 1) for b in MASKED]
    return np.stack(cuts, 1).astype(np.float32)


def kernel(**inputs):
    import concourse.bacc as bacc
    from concourse.bass_utils import run_bass_kernel_spmd

    a = {k.removeprefix("L0_"): np.ascontiguousarray(v) for k, v in inputs.items()}
    maa = [a["attn_time_maa_" + k] for k in "xwkvrg"]
    vectors = np.stack(maa + [a["attn_time_decay"], a["attn_time_faaaa"].reshape(-1)], 1)
    r_weights = np.stack([a["attn_W" + k] for k in "rkvgo"])
    r_norm = np.stack([a["attn_ln_w"], a["attn_ln_b"]])
    qk = np.stack([a["ffn_q_scale"], a["ffn_q_scale"], a["ffn_k_scale"], a["ffn_k_scale"]], 1)

    def rows(v, lead):
        wide = np.zeros((DEPTH, NC_ * 128) + v.shape[2:], v.dtype)
        wide[:, :FFN] = v
        return wide.reshape((DEPTH, NC_, 128) + v.shape[2:]).swapaxes(1, 2)

    ffn = np.concatenate([
        a["ffn_W1"],
        rows(a["ffn_W2"], DIM).reshape(DEPTH, 128, NC_ * DIM),
        a["ffn_ln_g"][:, :, None], a["ffn_ln_b"][:, :, None],
        rows(a["ffn_b1"][:, :FFN], 1), rows(a["ffn_b1"][:, FFN:], 1),
        a["ffn_b2"][:, :, None]], 2)
    tables, carry = position_tables()
    arrays = {
        "x": a["attn_x"], "vectors": vectors, "mix_w1": a["attn_time_maa_w1"], "mix_w2": a["attn_time_maa_w2"],
        "decay_w1": a["attn_time_decay_w1"], "decay_w2": a["attn_time_decay_w2"], "r_weights": r_weights,
        "r_norm": r_norm, "wqkv": a["ffn_Wqkv"], "wo": a["ffn_Wo"], "ffn": ffn, "qk_scales": qk,
        "positions": tables, "carry": carry, "ident": np.eye(128, dtype=np.float32), "band": band_masks(),
        "level_masks": level_cuts(),
    }
    arrays = {k + "_dram": np.ascontiguousarray(v) for k, v in arrays.items()}

    nc = bacc.Bacc("TRN2", target_bir_lowering=False, num_devices=1)
    args = [nc.dram_tensor(k, v.shape, mybir.dt.from_np(v.dtype), kind="ExternalInput").ap() for k, v in arrays.items()]
    out = nc.dram_tensor("out_dram", (1, TOKENS, DIM), F32, kind="ExternalOutput").ap()
    build(nc, *args, out)
    result = run_bass_kernel_spmd(nc, [arrays], core_ids=[0])
    return result.results[0]["out_dram"]
```

```python
from contextlib import ExitStack

import numpy as np

import concourse.bass as bass
from concourse import mybir

F32 = mybir.dt.float32
BF16 = mybir.dt.bfloat16
I32 = mybir.dt.int32
ALU = mybir.AluOpType
ACT = mybir.ActivationFunctionType
AX = mybir.AxisListType

TOKENS, DIM = 2048, 128
TILE = 128
TILES = TOKENS // TILE
HEADS, HEAD = 16, 64
PAIRS = HEADS // 2
INNER = HEADS * HEAD
DEPTH = 6
WINDOW = 32
BLOCKS = TILE // WINDOW
FFN = int(DIM * 4 * 2 / 3)
CHUNKS = [(0, 128), (128, 128), (256, FFN - 256)]
NC_ = len(CHUNKS)
STEPS = DEPTH * TILES
QK_SCALE = 8.0
LN_EPS = 1e-5
GROUP_EPS = 1e-5 * 8 ** 2
R_HEADS, R_HEAD = 2, 64
MIXES, LORA, DECAY_LORA = 5, 32, 64
MASKED = [0, 1, 2, 4, 8, 16]
MASKED_BIT = -1e30

V_MAA_X, V_MAA, V_DECAY, V_BONUS = 0, 1, 6, 7
F_W1, F_W2 = 0, 2 * FFN
F_G = F_W2 + NC_ * DIM
F_B, F_B1A, F_B1G, F_B2 = F_G + 1, F_G + 2, F_G + 2 + NC_, F_G + 2 + 2 * NC_
F_COLS = F_B2 + 1


def after(engine, semaphore, count):
    if not isinstance(count, int) or count > 0:
        engine.wait_ge(semaphore, count)


def stand_alone(engine, passed):
    engine.sem_inc(passed, 1)


ROOT_OPS = 10


def inverse_root(dve, ops, x, y, work, done, before):
    for i in ops:
        if i:
            dve.wait_ge(done, before + i)
        if i == 0:
            dve.tensor_scalar(y.bitcast(I32), x.bitcast(I32), -0.5, float(0x5F3759DF), ALU.mult, ALU.add)\
                .then_inc(done, 1)
        elif i % 3 == 1:
            dve.scalar_tensor_tensor(work[0], y, -0.5, y, ALU.mult, ALU.mult).then_inc(done, 1)
        elif i % 3 == 2:
            dve.tensor_tensor(work[1], work[0], x, ALU.mult).then_inc(done, 1)
        else:
            dve.scalar_tensor_tensor(y, work[1], 1.5, y, ALU.add, ALU.mult).then_inc(done, 1)


def tile_of(n):
    return n % TILES


def layer_of(n):
    return n // TILES


def columns(n):
    return bass.ds(tile_of(n) * TILE + 1, TILE)


def columns_before(n):
    return bass.ds(tile_of(n) * TILE, TILE)


def build(nc, x, vectors, mix_w1, mix_w2, decay_w1, decay_w2, r_weights, r_norm, wqkv, wo, ffn, qk_scales,
          positions, carry, ident, band, level_masks, out):
    with ExitStack() as ctx:
        def sb(name, shape, dtype=F32):
            return ctx.enter_context(nc.sbuf_tensor(name, shape, dtype))

        def sem(name):
            return ctx.enter_context(nc.semaphore(name))

        xa = sb("xa", [128, TOKENS + 1])
        xb = sb("xb", [128, TOKENS + 1])
        x_tok = sb("x_tok", [128, TILES, DIM])
        identity = sb("identity", [128, 128])
        identity_bf = sb("identity_bf", [128, 128], BF16)
        band_f = sb("band_f", [128, 2, 2 * WINDOW])
        band_bf = sb("band_bf", [128, 2, 2 * WINDOW], BF16)
        averager = sb("averager", [128, 128])
        ones = sb("ones", [128, 128])
        minus_half = sb("minus_half", [128, 8])

        proj_a = ctx.enter_context(nc.psum_tensor("proj_a", [128, 2, 512], F32))
        proj_b = ctx.enter_context(nc.psum_tensor("proj_b", [128, 2, 512], F32))
        att = ctx.enter_context(nc.psum_tensor("att", [128, 2, 512], F32))
        turn = ctx.enter_context(nc.psum_tensor("turn", [128, 2, 512], F32))

        constants_in = sem("constants_in")
        passed = sem("passed")
        constants_made = sem("constants_made")
        x_in = [sem(f"x_in{g}") for g in range(4)]

        time_mix(nc, ctx, locals())
        layers(nc, ctx, locals())
        last_norm(nc, ctx, locals())


def time_mix(nc, ctx, given):
    x, vectors, mix_w1, mix_w2, decay_w1, decay_w2, r_weights, r_norm, ident, band, level_masks = (
        given[k] for k in ("x", "vectors", "mix_w1", "mix_w2", "decay_w1", "decay_w2", "r_weights", "r_norm",
                           "ident", "band", "level_masks"))
    xa, xb, x_tok, identity, identity_bf, band_f, band_bf, averager, ones, minus_half = (
        given[k] for k in ("xa", "xb", "x_tok", "identity", "identity_bf", "band_f", "band_bf", "averager",
                           "ones", "minus_half"))
    proj_a, proj_b, att, turn = (given[k] for k in ("proj_a", "proj_b", "att", "turn"))
    constants_in, constants_made, x_in, passed = (
        given[k] for k in ("constants_in", "constants_made", "x_in", "passed"))

    with ExitStack() as own:
        def sb(name, shape, dtype=F32):
            return own.enter_context(nc.sbuf_tensor(name, shape, dtype))

        def sem(name):
            return ctx.enter_context(nc.semaphore(name))

        vec = sb("vec", [128, 8])
        w1 = sb("w1", [128, MIXES * LORA])
        w2_wide = sb("w2_wide", [128, MIXES, DIM])
        dw1 = sb("dw1", [128, DECAY_LORA])
        dw2 = sb("dw2", [DECAY_LORA, DIM])
        wr = sb("wr", [128, 5, DIM])
        norm_rows = sb("norm_rows", [128, 2, DIM])
        masks = sb("masks", [128, len(MASKED), WINDOW])

        xx = sb("xx", [128, TILE])
        x_mixed = sb("x_mixed", [128, TILE])
        mix = sb("mix", [128, TILE])
        mix_last = sb("mix_last", [LORA, TILE])
        shifted = sb("shifted", [128, MIXES, TILE])
        shifted2 = sb("shifted2", [128, MIXES, TILE])
        streams = sb("streams", [128, MIXES, TILE])
        low = sb("low", [DECAY_LORA, TILE])
        rate = sb("rate", [128, TILE])
        decay = [sb(f"decay{i}", [128, TILE >> i]) for i in range(8)]
        rf = sb("rf", [128, TILE])
        rf_bonus = sb("rf_bonus", [128, TILE])
        kf = sb("kf", [128, TILE])
        v_tok = sb("v_tok", [128, DIM])
        gate_t = sb("gate_t", [128, DIM])
        gate_s = sb("gate_s", [128, DIM])
        gate = sb("gate", [128, DIM])
        cut = sb("cut", [128, R_HEADS, len(MASKED), WINDOW])
        coef = sb("coef", [128, R_HEADS, TILE])
        k_tok = sb("k_tok", [128, DIM])
        state = sb("state", [128, DIM])
        stats = sb("stats", [128, R_HEADS, 6])
        moments = sb("moments", [128, R_HEADS, 2])
        var_eps = sb("var_eps", [128, R_HEADS])
        rstd = sb("rstd", [128, R_HEADS])
        y_n = sb("y_n", [128, DIM])
        y_w = sb("y_w", [128, DIM])
        y_b = sb("y_b", [128, DIM])
        y_g = sb("y_g", [128, DIM])
        y_t = sb("y_t", [128, TILE])
        res = sb("res", [128, DIM])
        stats2 = sb("stats2", [128, 6])
        moments2 = sb("moments2", [128, 2])
        var_eps2 = sb("var_eps2", [128, 1])
        rstd2 = sb("rstd2", [128, 1])
        x_one = sb("x_one", [128, DIM])

        weights_in = sem("weights_in")
        zeroed, converted, cleared = sem("zeroed"), sem("converted"), sem("cleared_r")
        w2_in = sem("w2_in")
        x_turned, x_laid = sem("x_turned"), sem("x_laid")
        s_xx, s_xmix = sem("s_xx"), sem("s_xmix")
        s_low_mix, s_mix, s_mix_up = sem("s_low_mix"), sem("s_mix"), sem("s_mix_up")
        s_add, s_mul, s_streams = sem("s_add"), sem("s_mul"), sem("s_streams")
        s_lora1, s_lora_t, s_lora2 = sem("s_lora1"), sem("s_lora_t"), sem("s_lora2")
        s_rate, s_decay = sem("s_rate"), sem("s_decay")
        s_rk, s_vg = sem("s_rk"), sem("s_vg")
        s_r, s_rb, s_k, s_v = sem("s_r"), sem("s_rb"), sem("s_k"), sem("s_v")
        s_gt, s_gs, s_gate = sem("s_gt"), sem("s_gs"), sem("s_gate")
        s_level, s_scaled = sem("s_level"), sem("s_scaled")
        s_cut, s_coef, s_coef_far = sem("s_cut"), sem("s_coef"), sem("s_coef_far")
        s_kturn, s_ktok, s_y, s_su, s_state = (sem(k) for k in ("s_kturn", "s_ktok", "s_y", "s_su", "s_state"))
        s_stat, s_mom, s_ve, s_pow, s_yn, s_yw, s_yb, s_yg = (
            sem(k) for k in ("s_stat", "s_mom", "s_ve", "s_pow", "s_yn", "s_yw", "s_yb", "s_yg"))
        s_yturn, s_yt, s_out, s_res = (sem(k) for k in ("s_yturn", "s_yt", "s_out", "s_res"))
        s_stat2, s_mom2, s_ve2, s_pow2, s_one, s_keep, s_oturn, s_done = (
            sem(k) for k in ("s_stat2", "s_mom2", "s_ve2", "s_pow2", "s_one", "s_keep", "s_oturn", "s_done"))
        LEVELS = 7

        def levels_of(buffer, b):
            return buffer[:, :].rearrange("p (m two b) -> p m two b", two=2, b=b)

        with nc.Block() as block:
            @block.sync
            def _(sp):
                for g in range(4):
                    sp.dma_start(x_tok[:, 4 * g:4 * g + 4, :],
                                 x[0, 512 * g:512 * g + 512, :].rearrange("(t p) c -> p t c", p=TILE)).then_inc(x_in[g], 16)
                sp.dma_start(vec[:, :], vectors).then_inc(weights_in, 16)
                sp.dma_start(w1[:, :], mix_w1).then_inc(weights_in, 16)
                sp.dma_start(dw1[:, :], decay_w1).then_inc(weights_in, 16)
                sp.dma_start(dw2[:, :], decay_w2).then_inc(weights_in, 16)
                sp.dma_start(wr[:, :, :], r_weights.rearrange("w i o -> i w o")).then_inc(weights_in, 16)
                sp.dma_start(norm_rows[:, :, :], r_norm.partition_broadcast(128)).then_inc(weights_in, 16)
                sp.dma_start(masks[:, :, :], level_masks).then_inc(weights_in, 16)
                sp.wait_ge(zeroed, 1)
                for s in range(MIXES):
                    row = LORA * (s % 4)
                    sp.dma_start(w2_wide[row:row + LORA, s, :], mix_w2[s]).then_inc(w2_in, 16)

            @block.gpsimd
            def _(pool):
                pool.memset(w2_wide[:, :, :], 0.0).then_inc(zeroed, 1)
                pool.memset(averager[:, :], 1.0 / DIM).then_inc(constants_made, 1)
                pool.memset(ones[:, :], 1.0).then_inc(constants_made, 1)
                pool.memset(minus_half[:, :], -0.5).then_inc(constants_made, 1)
                pool.wait_ge(constants_made, 3)
                with pool.Fori(0, TILES) as c:
                    pool.wait_ge(s_ve, c * 2 + 2)
                    pool.tensor_tensor(rstd[:, :], var_eps[:, :], minus_half[:, 0:R_HEADS], ALU.pow).then_inc(s_pow, 1)
                    pool.wait_ge(s_ve2, c + 1)
                    pool.tensor_tensor(rstd2[:, :], var_eps2[:, :], minus_half[:, 0:1], ALU.pow).then_inc(s_pow2, 1)

            @block.scalar
            def _(act):
                act.dma_start(identity[:, :], ident).then_inc(constants_in, 16)
                act.dma_start(band_f[:, :, :], band).then_inc(constants_in, 16)
                for g in range(4):
                    act.wait_ge(x_turned, g + 1)
                    act.copy(xb[:, 1 + 512 * g:1 + 512 * g + 512], turn[:, g % 2, :]).then_inc(x_laid, 1)
                act.wait_ge(weights_in, 16 * 7)
                with act.Fori(0, TILES) as c:
                    act.wait_ge(s_low_mix, c + 1)
                    act.activation(mix[:, :], turn[:, 0, 0:TILE], ACT.Tanh).then_inc(s_mix, 1)
                    act.activation(mix_last[:, :], turn[0:LORA, 0, TILE:2 * TILE], ACT.Tanh).then_inc(s_mix, 1)
                    act.wait_ge(s_lora1, c + 1)
                    act.activation(low[:, :], turn[0:DECAY_LORA, 1, 0:TILE], ACT.Tanh).then_inc(s_lora_t, 1)
                    act.wait_ge(s_lora2, c + 1)
                    act.activation(rate[:, :], turn[:, 1, TILE:2 * TILE], ACT.Exp,
                                   bias=vec[:, V_DECAY:V_DECAY + 1]).then_inc(s_rate, 1)
                    act.wait_ge(s_rate, c + 1)
                    act.activation(decay[0][:, :], rate[:, :], ACT.Exp, scale=-1.0).then_inc(s_decay, 1)
                    act.wait_ge(s_vg, c + 1)
                    act.copy(v_tok[:, :], proj_b[:, 1, 0:DIM]).then_inc(s_v, 1)
                    act.activation(gate_t[:, :], proj_b[:, 1, DIM:2 * DIM], ACT.Tanh, scale=0.5).then_inc(s_gt, 1)
                    act.wait_ge(s_level, c * 8 + 8)
                    act.wait_ge(s_cut, c + 1)
                    act.copy(coef[0:32, :, 32:64], att[0:32, :, 192:224]).then_inc(s_coef_far, 1)
                    act.copy(coef[64:96, :, 96:128], att[64:96, :, 192:224]).then_inc(s_coef_far, 1)
                    act.copy(coef[0:64, :, 64:128], att[0:64, :, 256:320]).then_inc(s_coef_far, 1)
                    act.wait_ge(s_kturn, c + 1)
                    act.copy(k_tok[:, :], turn[:, 0, 0:DIM]).then_inc(s_ktok, 1)
                    act.wait_ge(s_yturn, c + 1)
                    act.copy(y_t[:, :], turn[:, 1, 0:TILE]).then_inc(s_yt, 1)
                    act.wait_ge(s_oturn, c + 1)
                    act.copy(xa[:, bass.ds(c * TILE + 1, TILE)], turn[:, 0, 0:TILE]).then_inc(s_done, 1)

            @block.vector
            def _(dve):
                dve.memset(xa[:, 0:1], 0.0).then_inc(cleared, 1)
                dve.memset(xb[:, 0:1], 0.0).then_inc(cleared, 1)
                dve.memset(coef[:, :, :], 0.0).then_inc(cleared, 1)
                dve.memset(state[:, :], 0.0).then_inc(cleared, 1)
                dve.wait_ge(constants_in, 32)
                dve.tensor_copy(identity_bf[:, :], identity[:, :]).then_inc(converted, 1)
                dve.tensor_copy(band_bf[:, :, :], band_f[:, :, :]).then_inc(converted, 1)
                dve.wait_ge(weights_in, 16 * 7)
                dve.wait_ge(cleared, 4)
                dve.wait_ge(x_laid, 4)
                maa = vec[:, V_MAA:V_MAA + MIXES].unsqueeze(2).broadcast_to([128, MIXES, TILE])
                with dve.Fori(0, TILES) as c:
                    here = xb[:, bass.ds(c * TILE + 1, TILE)]
                    dve.tensor_tensor(xx[:, :], xb[:, bass.ds(c * TILE, TILE)], here, ALU.subtract).then_inc(s_xx, 1)
                    dve.wait_ge(s_xx, c + 1)
                    dve.scalar_tensor_tensor(x_mixed[:, :], xx[:, :], vec[:, V_MAA_X:V_MAA_X + 1], here,
                                             ALU.mult, ALU.add).then_inc(s_xmix, 1)
                    dve.wait_ge(s_mix_up, c + 1)
                    wide = proj_a[:, :, :].rearrange("p a b -> p (a b)")[:, 0:MIXES * TILE].rearrange(
                        "p (s t) -> p s t", s=MIXES)
                    dve.tensor_tensor(shifted[:, :, :], wide, maa, ALU.add).then_inc(s_add, 1)
                    dve.wait_ge(s_add, c + 1)
                    dve.tensor_tensor(shifted2[:, :, :], shifted[:, :, :],
                                      xx[:, :].unsqueeze(1).broadcast_to([128, MIXES, TILE]),
                                      ALU.mult).then_inc(s_mul, 1)
                    dve.wait_ge(s_mul, c + 1)
                    dve.tensor_tensor(streams[:, :, :], shifted2[:, :, :],
                                      here.unsqueeze(1).broadcast_to([128, MIXES, TILE]),
                                      ALU.add).then_inc(s_streams, 1)
                    dve.wait_ge(s_rk, c + 1)
                    dve.tensor_copy(rf[:, :], proj_b[:, 0, 0:TILE]).then_inc(s_r, 1)
                    dve.tensor_scalar(rf_bonus[:, :], proj_b[:, 0, 0:TILE], vec[:, V_BONUS:V_BONUS + 1], None,
                                      ALU.mult).then_inc(s_rb, 1)
                    dve.tensor_copy(kf[:, :], proj_b[:, 0, TILE:2 * TILE]).then_inc(s_k, 1)
                    dve.wait_ge(s_gt, c + 1)
                    dve.tensor_scalar(gate_s[:, :], gate_t[:, :], 0.5, 0.5, ALU.mult, ALU.add).then_inc(s_gs, 1)
                    dve.wait_ge(s_gs, c + 1)
                    dve.tensor_tensor(gate[:, :], gate_s[:, :], proj_b[:, 1, DIM:2 * DIM], ALU.mult).then_inc(s_gate, 1)
                    dve.wait_ge(s_decay, c + 1)
                    for i in range(LEVELS):
                        b = 1 << i
                        r_v, k_v = levels_of(rf, b), levels_of(kf, b)
                        pairs = TILE // (2 * b)
                        d_v = decay[i][:, :].rearrange("p (m two) -> p m two", two=2)
                        dve.wait_ge(s_level, c * 8 + i + 2)
                        if i:
                            dve.wait_ge(s_scaled, c * 3 * LEVELS + 3 * i)
                        dve.tensor_tensor(r_v[:, :, 1, :], r_v[:, :, 1, :],
                                          d_v[:, :, 0:1].broadcast_to([128, pairs, b]), ALU.mult).then_inc(s_scaled, 1)
                        dve.tensor_tensor(k_v[:, :, 0, :], k_v[:, :, 0, :],
                                          d_v[:, :, 1:2].broadcast_to([128, pairs, b]), ALU.mult).then_inc(s_scaled, 1)
                        dve.tensor_tensor(decay[i + 1][:, :], d_v[:, :, 0], d_v[:, :, 1], ALU.mult).then_inc(s_scaled, 1)
                    dve.tensor_tensor(cut[:, :, :, :],
                                      att[:, :, 0:192].rearrange("p h (l t) -> p h l t", t=WINDOW),
                                      masks[:, :, :].unsqueeze(1).broadcast_to([128, R_HEADS, len(MASKED), WINDOW]),
                                      ALU.mult).then_inc(s_cut, 1)
                    dve.wait_ge(s_cut, c + 1)
                    for q in range(BLOCKS):
                        p = slice(WINDOW * q, WINDOW * q + WINDOW)
                        dve.tensor_reduce(coef[p, :, p], cut[p, :, :, :].rearrange("p h l t -> p h t l"),
                                          AX.X, ALU.add).then_inc(s_coef, 1)
                    dve.wait_ge(s_su, c + 1)
                    dve.wait_ge(s_scaled, c * 3 * LEVELS + 3 * LEVELS)
                    for h in range(R_HEADS):
                        p = slice(R_HEAD * h, R_HEAD * h + R_HEAD)
                        dve.scalar_tensor_tensor(state[p, p], state[p, p], decay[LEVELS][p, 0:1],
                                                 turn[p, 1, TILE + R_HEAD * h:TILE + R_HEAD * h + R_HEAD],
                                                 ALU.mult, ALU.add).then_inc(s_state, 1)
                    for h in range(R_HEADS):
                        dve.bn_stats(stats[:, h, :], proj_a[:, 0, R_HEAD * h:R_HEAD * h + R_HEAD]).then_inc(s_stat, 1)
                    dve.wait_ge(s_stat, c * 2 + 2)
                    stand_alone(dve, passed)
                    for h in range(R_HEADS):
                        dve.bn_aggr(moments[:, h, :], stats[:, h, :]).then_inc(s_mom, 1)
                    for h in range(R_HEADS):
                        dve.wait_ge(s_mom, c * 2 + h + 1)
                        dve.tensor_scalar(var_eps[:, h:h + 1], moments[:, h, 1:2], GROUP_EPS, None,
                                          ALU.add).then_inc(s_ve, 1)
                    dve.wait_ge(s_pow, c + 1)
                    for h in range(R_HEADS):
                        p = slice(R_HEAD * h, R_HEAD * h + R_HEAD)
                        dve.tensor_scalar(y_n[:, p], proj_a[:, 0, p], moments[:, h, 0:1], rstd[:, h:h + 1],
                                          ALU.subtract, ALU.mult).then_inc(s_yn, 1)
                    dve.wait_ge(s_yn, c * 2 + 2)
                    dve.tensor_tensor(y_w[:, :], y_n[:, :], norm_rows[:, 0, :], ALU.mult).then_inc(s_yw, 1)
                    dve.wait_ge(s_yw, c + 1)
                    dve.tensor_tensor(y_b[:, :], y_w[:, :], norm_rows[:, 1, :], ALU.add).then_inc(s_yb, 1)
                    dve.wait_ge(s_yb, c + 1)
                    dve.wait_ge(s_gate, c + 1)
                    dve.tensor_tensor(y_g[:, :], y_b[:, :], gate[:, :], ALU.mult).then_inc(s_yg, 1)
                    dve.wait_ge(s_out, c + 1)
                    dve.tensor_tensor(res[:, :], proj_a[:, 1, 0:DIM], x_tok[:, c, :], ALU.add).then_inc(s_res, 1)
                    dve.wait_ge(s_res, c + 1)
                    dve.bn_stats(stats2[:, :], res[:, :]).then_inc(s_stat2, 1)
                    dve.wait_ge(s_stat2, c + 1)
                    stand_alone(dve, passed)
                    dve.bn_aggr(moments2[:, :], stats2[:, :]).then_inc(s_mom2, 1)
                    dve.wait_ge(s_mom2, c + 1)
                    dve.tensor_scalar(var_eps2[:, :], moments2[:, 1:2], LN_EPS, None, ALU.add).then_inc(s_ve2, 1)
                    dve.wait_ge(s_pow2, c + 1)
                    dve.tensor_scalar(x_one[:, :], res[:, :], moments2[:, 0:1], rstd2[:, 0:1],
                                      ALU.subtract, ALU.mult).then_inc(s_one, 1)
                    dve.wait_ge(s_one, c + 1)
                    stand_alone(dve, passed)
                    dve.tensor_copy(x_tok[:, c, :], x_one[:, :]).then_inc(s_keep, 1)

            @block.tensor
            def _(pe):
                pe.wait_ge(constants_in, 32)
                for g in range(4):
                    pe.wait_ge(x_in[g], 16)
                    if g >= 2:
                        pe.wait_ge(x_laid, g - 1)
                    for j in range(4):
                        mm = pe.transpose(turn[:, g % 2, TILE * j:TILE * j + TILE], x_tok[:, 4 * g + j, :], identity[:, :])
                    mm.then_inc(x_turned, 1)
                pe.wait_ge(x_laid, 4)
                pe.wait_ge(weights_in, 16 * 7)
                pe.wait_ge(w2_in, 16 * MIXES)

                def level(c, i, r_buffer):
                    for h in range(R_HEADS):
                        rows = slice(R_HEAD * h, R_HEAD * h + R_HEAD)
                        for q in range(BLOCKS):
                            cols = slice(WINDOW * q, WINDOW * q + WINDOW)
                            mm = pe.matmul(att[cols, h, WINDOW * i:WINDOW * i + WINDOW], kf[rows, cols],
                                           r_buffer[rows, cols], start=True, stop=True)
                    mm.then_inc(s_level, 1)

                with pe.Fori(0, TILES) as c:
                    pe.wait_ge(s_xmix, c + 1)
                    pe.matmul(turn[:, 0, 0:TILE], w1[:, 0:128], x_mixed[:, :], start=True, stop=True)
                    pe.matmul(turn[0:LORA, 0, TILE:2 * TILE], w1[:, 128:160], x_mixed[:, :],
                              start=True, stop=True).then_inc(s_low_mix, 1)
                    pe.wait_ge(s_mix, c * 2 + 2)
                    for s in range(4):
                        pe.matmul(proj_a[:, 0, TILE * s:TILE * s + TILE], w2_wide[:, s, :], mix[:, :],
                                  start=True, stop=True)
                    pe.matmul(proj_a[:, 1, 0:TILE], w2_wide[0:LORA, 4, :], mix_last[:, :],
                              start=True, stop=True).then_inc(s_mix_up, 1)
                    pe.wait_ge(s_streams, c + 1)
                    pe.matmul(turn[0:DECAY_LORA, 1, 0:TILE], dw1[:, :], streams[:, 0, :],
                              start=True, stop=True).then_inc(s_lora1, 1)
                    pe.matmul(proj_b[:, 0, 0:TILE], wr[:, 0, :], streams[:, 3, :], start=True, stop=True)
                    pe.matmul(proj_b[:, 0, TILE:2 * TILE], wr[:, 1, :], streams[:, 1, :],
                              start=True, stop=True).then_inc(s_rk, 1)
                    pe.matmul(proj_b[:, 1, 0:DIM], streams[:, 2, :], wr[:, 2, :], start=True, stop=True)
                    pe.matmul(proj_b[:, 1, DIM:2 * DIM], streams[:, 4, :], wr[:, 3, :],
                              start=True, stop=True).then_inc(s_vg, 1)
                    pe.wait_ge(s_lora_t, c + 1)
                    pe.matmul(turn[:, 1, TILE:2 * TILE], dw2[:, :], low[:, :], start=True, stop=True).then_inc(s_lora2, 1)
                    pe.wait_ge(s_rb, c + 1)
                    pe.wait_ge(s_k, c + 1)
                    stand_alone(pe, passed)
                    level(c, 0, rf_bonus)
                    for i in range(5):
                        if i:
                            pe.wait_ge(s_scaled, c * 3 * LEVELS + 3 * i)
                        else:
                            pe.wait_ge(s_r, c + 1)
                        stand_alone(pe, passed)
                        level(c, i + 1, rf)
                    pe.wait_ge(s_scaled, c * 3 * LEVELS + 15)
                    stand_alone(pe, passed)
                    for h in range(R_HEADS):
                        rows = slice(R_HEAD * h, R_HEAD * h + R_HEAD)
                        for q in (0, 2):
                            mm = pe.matmul(att[WINDOW * q:WINDOW * q + WINDOW, h, 192:224],
                                           kf[rows, WINDOW * q:WINDOW * q + WINDOW],
                                           rf[rows, WINDOW * q + WINDOW:WINDOW * q + 2 * WINDOW], start=True, stop=True)
                    mm.then_inc(s_level, 1)
                    pe.wait_ge(s_scaled, c * 3 * LEVELS + 18)
                    stand_alone(pe, passed)
                    for h in range(R_HEADS):
                        rows = slice(R_HEAD * h, R_HEAD * h + R_HEAD)
                        mm = pe.matmul(att[0:64, h, 256:320], kf[rows, 0:64], rf[rows, 64:128], start=True, stop=True)
                    mm.then_inc(s_level, 1)
                    pe.wait_ge(s_scaled, c * 3 * LEVELS + 21)
                    pe.transpose(turn[:, 0, 0:DIM], kf[:, :], identity[:, :]).then_inc(s_kturn, 1)
                    pe.wait_ge(s_coef, c * 4 + 4)
                    pe.wait_ge(s_coef_far, c * 3 + 3)
                    pe.wait_ge(s_v, c + 1)
                    pe.matmul(proj_a[:, 0, 0:DIM], rf[:, :], state[:, :], start=True, stop=False)
                    for h in range(R_HEADS):
                        p = slice(R_HEAD * h, R_HEAD * h + R_HEAD)
                        mm = pe.matmul(proj_a[:, 0, p], coef[:, h, :], v_tok[:, p], start=False, stop=(h == 1))
                    mm.then_inc(s_y, 1)
                    pe.wait_ge(s_ktok, c + 1)
                    pe.matmul(turn[:, 1, TILE:2 * TILE], k_tok[:, :], v_tok[:, :], start=True, stop=True).then_inc(s_su, 1)
                    pe.wait_ge(s_yg, c + 1)
                    pe.transpose(turn[:, 1, 0:TILE], y_g[:, :], identity[:, :]).then_inc(s_yturn, 1)
                    pe.wait_ge(s_yt, c + 1)
                    pe.matmul(proj_a[:, 1, 0:DIM], y_t[:, :], wr[:, 4, :], start=True, stop=True).then_inc(s_out, 1)
                    pe.wait_ge(s_one, c + 1)
                    pe.transpose(turn[:, 0, 0:TILE], x_one[:, :], identity[:, :]).then_inc(s_oturn, 1)
                    pe.wait_ge(s_done, c + 1)


def layers(nc, ctx, given):
    wqkv, wo, ffn, qk_scales, positions, carry = (
        given[k] for k in ("wqkv", "wo", "ffn", "qk_scales", "positions", "carry"))
    xa, xb, identity, identity_bf, band_bf, averager, ones, minus_half = (
        given[k] for k in ("xa", "xb", "identity", "identity_bf", "band_bf", "averager", "ones", "minus_half"))
    proj_a, proj_b, att, turn = (given[k] for k in ("proj_a", "proj_b", "att", "turn"))
    constants_in, passed = given["constants_in"], given["passed"]

    with ExitStack() as own:
        def sb(name, shape, dtype=F32):
            return own.enter_context(nc.sbuf_tensor(name, shape, dtype))

        def sem(name):
            return ctx.enter_context(nc.semaphore(name))

        w_qkv = sb("w_qkv", [128, 3 * INNER])
        w_o = sb("w_o", [128, PAIRS, DIM])
        w_ffn = sb("w_ffn", [128, F_COLS])
        scales = sb("scales", [128, DEPTH, 4, HEAD])
        where = sb("where", [128, TILES, 4, HEAD])
        carry_scale = sb("carry_scale", [128, 1])

        shift_a = [sb(f"shift_a{i}", [128, TILE]) for i in range(2)]
        turns = [sb(f"turns{i}", [128, 4, HEAD]) for i in range(2)]
        squares = [sb(f"squares{i}", [128, HEADS, HEAD]) for i in range(2)]
        sums = sb("sums", [128, 2, HEADS])
        sums_min = sb("sums_min", [128, 2, HEADS])
        inv_norm = sb("inv_norm", [128, 2, HEADS])
        root_work = [sb(f"root_work{i}", [128, 2, HEADS]) for i in range(2)]
        raw = [sb(f"raw{i}", [128, HEADS, HEAD]) for i in range(2)]
        unit = [sb(f"unit{i}", [128, HEADS, HEAD]) for i in range(2)]
        along = [sb(f"along{i}", [128, HEADS, HEAD]) for i in range(2)]
        across = [sb(f"across{i}", [128, HEADS, HEAD]) for i in range(2)]
        rotated = [sb(f"rotated{i}", [128, HEADS, HEAD]) for i in range(2)]
        q_t = sb("q_t", [128, PAIRS, TILE])
        k_t = sb("k_t", [128, PAIRS, WINDOW + TILE])
        v_tok = [sb(f"val{i}", [128, 2, PAIRS, HEAD]) for i in range(2)]
        v_win = sb("v_win", [128, BLOCKS, PAIRS * HEAD])
        row_max = sb("row_max", [128, HEADS])
        logits = sb("logits", [128, 2, PAIRS, 2 * WINDOW])
        probs = sb("probs", [128, PAIRS, 2, 2 * WINDOW])
        mass = sb("mass", [128, HEADS])
        inv_mass = sb("inv_mass", [128, HEADS])
        p_t = sb("p_t", [128, PAIRS, TILE])
        heads_out = sb("heads_out", [128, PAIRS, 2, HEAD])
        o_t = sb("o_t", [128, PAIRS, TILE])
        shift_f = sb("shift_f", [128, TILE])
        dev = sb("dev", [128, TILE])
        dev_sq = sb("dev_sq", [128, TILE])
        var_f = sb("var_f", [128, 1])
        rstd_f = sb("rstd_f", [128, 1])
        rstd_diag = sb("rstd_diag", [128, TILE])
        norm_g = sb("norm_g", [128, TILE])
        normed = sb("normed", [128, TILE])
        gelu = sb("gelu", [128, NC_, TILE])
        hidden = sb("hidden", [128, NC_, TILE])

        tables_in = sem("tables_in")
        q_in, k_in, v_in, wo_in, ffn_in = (sem(k) for k in ("q_in", "k_in", "v_in", "wo_in", "ffn_in"))
        cleared = sem("cleared")
        shifted = sem("shifted")
        table_made = sem("table_made")
        q_projected, k_projected, v_projected = sem("q_projected"), sem("k_projected"), sem("v_projected")
        raw_kept = [sem("q_kept"), sem("k_kept")]
        squared = [sem("q_squared"), sem("k_squared")]
        summed = [sem("q_summed"), sem("k_summed")]
        bounded, rooted = sem("bounded"), sem("rooted")
        united = [sem("q_united"), sem("k_united")]
        alonged = [sem("q_alonged"), sem("k_alonged")]
        acrossed = [sem("q_acrossed"), sem("k_acrossed")]
        rotated_in = [sem("q_rotated"), sem("k_rotated")]
        q_turned, q_laid = sem("q_turned"), sem("q_laid")
        k_turned, k_laid, k_carried = sem("k_turned"), sem("k_laid"), sem("k_carried")
        v_laid, v_spread = sem("v_laid"), sem("v_spread")
        scored, maxed, centred, weighed = sem("scored"), sem("maxed"), sem("centred"), sem("weighed")
        massed, mass_inverted = sem("massed"), sem("mass_inverted")
        p_turned, p_laid, mixed, scaled_out = sem("p_turned"), sem("p_laid"), sem("mixed"), sem("scaled_out")
        o_turned, o_laid, attended, xb_ready = sem("o_turned"), sem("o_laid"), sem("attended"), sem("xb_ready")
        f_shifted, mean_made, deviated, dev_squared = (
            sem(k) for k in ("f_shifted", "mean_made", "deviated", "dev_squared"))
        var_made, var_kept, rstd_made, rstd_laid, rstd_spread, scaled_f, normed_f = (
            sem(k) for k in ("var_made", "var_kept", "rstd_made", "rstd_laid", "rstd_spread", "scaled_f", "normed_f"))
        widened, gelued, gated, narrowed, xa_ready = (
            sem(k) for k in ("widened", "gelued", "gated", "narrowed", "xa_ready"))

        slots = [proj_a, proj_b]

        def by_head(slot):
            return slot[:, :, :].rearrange("p a (h e) -> p (a h) e", e=HEAD)

        def halves(buffer):
            return buffer[:, :, :].rearrange("p h (two e) -> p h two e", two=2)

        def turn_along(engine, j, m, p):
            engine.wait_ge(table_made, m + 1)
            engine.wait_ge(raw_kept[j], m + 1)
            after(engine, rotated_in[j], m)
            engine.tensor_tensor(along[j][:, :, :], raw[j][:, :, :],
                              turns[p][:, 2 * j, :].unsqueeze(1).broadcast_to([128, HEADS, HEAD]),
                              ALU.mult).then_inc(alonged[j], 1)

        def run(engine, step):
            step(-1, 1, False, True, False)
            step(0, 0, True, True, False)
            with engine.Fori(0, (STEPS - 2) // 2) as i:
                step(i * 2 + 1, 1, True, True, True)
                step(i * 2 + 2, 0, True, True, True)
            step(STEPS - 1, 1, True, False, True)
            step(STEPS, 0, False, False, True)

        with nc.Block() as block:
            @block.sync
            def _(sp):
                def load_projection(layer, j):
                    part = slice(INNER * j, INNER * j + INNER)
                    sp.dma_start(w_qkv[:, part], wqkv[layer, :, part]).then_inc((q_in, k_in, v_in)[j], 16)

                def load_wo(layer):
                    sp.dma_start(w_o[:, :, :], wo[layer].rearrange("(p i) o -> i p o", i=128)).then_inc(wo_in, 16)

                def load_ffn(layer):
                    sp.dma_start(w_ffn[:, :], ffn[layer]).then_inc(ffn_in, 16)

                def spread(m, odd):
                    now, old = v_tok[odd], v_tok[1 - odd]
                    sp.wait_ge(v_laid, m + 1)
                    stand_alone(sp, passed)
                    after(sp, mixed, 2 * m)
                    stand_alone(sp, passed)
                    for par in range(2):
                        base = 2 * WINDOW * par
                        own_rows = slice(base + WINDOW, base + 2 * WINDOW)
                        flat = [v[:, par, :, :].rearrange("p a e -> p (a e)") for v in (now, old)]
                        for w in range(BLOCKS):
                            sp.dma_start(v_win[own_rows, w, :],
                                         flat[0][WINDOW * w:WINDOW * w + WINDOW, :]).then_inc(v_spread, 16)
                            before = flat[0][WINDOW * (w - 1):WINDOW * w, :] if w else flat[1][TILE - WINDOW:TILE, :]
                            sp.dma_start(v_win[base:base + WINDOW, w, :], before).then_inc(v_spread, 16)

                def spread_pairs(first, last, base):
                    with sp.Fori(first // 2, last // 2) as i:
                        spread(base + i * 2, 0)
                        spread(base + i * 2 + 1, 1)

                for j in range(3):
                    load_projection(0, j)
                sp.dma_start(carry_scale[:, :], carry).then_inc(tables_in, 16)
                sp.dma_start(where[:, :, :, :], positions).then_inc(tables_in, 16)
                sp.dma_start(scales[:, :, :, :], qk_scales.partition_broadcast(128)).then_inc(tables_in, 16)
                load_wo(0)
                load_ffn(0)
                sp.wait_ge(cleared, 3)
                spread_pairs(0, TILES - 2, 0)
                spread(TILES - 2, 0)
                with sp.Fori(1, DEPTH) as layer:
                    first = layer * TILES
                    sp.wait_ge(q_projected, first)
                    stand_alone(sp, passed)
                    load_projection(layer, 0)
                    sp.wait_ge(k_projected, first)
                    stand_alone(sp, passed)
                    load_projection(layer, 1)
                    sp.wait_ge(v_projected, 2 * first)
                    stand_alone(sp, passed)
                    load_projection(layer, 2)
                    spread(first - 1, 1)
                    sp.wait_ge(attended, first)
                    stand_alone(sp, passed)
                    load_wo(layer)
                    spread(first, 0)
                    sp.wait_ge(xa_ready, first)
                    stand_alone(sp, passed)
                    load_ffn(layer)
                    spread(first + 1, 1)
                    spread_pairs(2, TILES - 2, first)
                    spread(first + TILES - 2, 0)
                spread(STEPS - 1, 1)

            @block.gpsimd
            def _(pool):
                pool.wait_ge(tables_in, 48)

                def step(n, odd, attend, project, feed):
                    m, p = n + 1, 1 - odd

                    def invert_deviation():
                        pool.wait_ge(var_kept, n)
                        pool.tensor_tensor(rstd_f[:, :], var_f[:, :], minus_half[:, 0:1], ALU.pow).then_inc(rstd_made, 1)

                    if not project:
                        invert_deviation()
                        return
                    after(pool, alonged[1], m - 1)
                    after(pool, acrossed[1], 2 * (m - 1))
                    pool.tensor_tensor(turns[p][:, :, :], where[:, tile_of(m), :, :], scales[:, layer_of(m), :, :],
                                       ALU.mult).then_inc(table_made, 1)
                    pool.wait_ge(table_made, m + 1)
                    for j in range(2):
                        pool.wait_ge(raw_kept[j], m + 1)
                        after(pool, rotated_in[j], m)
                        u, a = halves(raw[j]), halves(across[j])
                        for half in range(2):
                            table = turns[p][:, 2 * j + 1, 32 * half:32 * half + 32].unsqueeze(1).broadcast_to(
                                [128, HEADS, 32])
                            pool.tensor_tensor(a[:, :, 1 - half, :], u[:, :, half, :], table,
                                               ALU.mult).then_inc(acrossed[j], 1)
                            if feed and j == half == 0:
                                invert_deviation()
                        if j == 0:
                            turn_along(pool, 0, m, p)
                        pool.wait_ge(alonged[j], m + 1)
                        pool.wait_ge(acrossed[j], 2 * m + 2)
                        after(pool, united[j], m)
                        pool.tensor_tensor(rotated[j][:, :, :], along[j][:, :, :], across[j][:, :, :],
                                           ALU.add).then_inc(rotated_in[j], 1)

                run(pool, step)

            @block.scalar
            def _(act):
                def step(n, odd, attend, project, feed):
                    m, p, f = n + 1, 1 - odd, n - 1
                    if attend:
                        for j in range(2):
                            act.wait_ge(q_turned, 2 * n + j + 1)
                            after(act, scored, 2 * n)
                            act.copy(q_t[:, 4 * j:4 * j + 4, :], turn[:, j, :].rearrange("p (a t) -> p a t", t=TILE))\
                                .then_inc(q_laid, 1)
                        for j in range(2):
                            act.wait_ge(k_turned, 2 * n + j + 1)
                            after(act, k_carried, n)
                            act.copy(k_t[:, 4 * j:4 * j + 4, WINDOW:], turn[:, j, :].rearrange("p (a t) -> p a t", t=TILE))\
                                .then_inc(k_laid, 1)
                    def keep_raw(j):
                        act.wait_ge((q_projected, k_projected)[j], m + 1)
                        after(act, alonged[j], m)
                        after(act, acrossed[j], 2 * m)
                        act.copy(raw[j][:, :, :], by_head(slots[j])).then_inc(raw_kept[j], 1)

                    def square(j):
                        after(act, summed[j], m)
                        act.activation(squares[j][:, :, :], by_head(slots[j]), ACT.Square).then_inc(squared[j], 1)

                    if project:
                        keep_raw(0)
                        square(0)
                    if attend:
                        for par in range(2):
                            act.wait_ge(centred, 2 * n + par + 1)
                            after(act, p_turned, 2 * n)
                            after(act, massed, n)
                            act.activation(probs[:, :, par, :], logits[:, par, :, :], ACT.Exp).then_inc(weighed, 1)
                    if project:
                        keep_raw(1)
                    if attend:
                        for j in range(2):
                            act.wait_ge(p_turned, 2 * n + j + 1)
                            after(act, mixed, 2 * n)
                            act.copy(p_t[:, 4 * j:4 * j + 4, :], att[:, j, :].rearrange("p (a t) -> p a t", t=TILE))\
                                .then_inc(p_laid, 1)
                    if project:
                        square(1)
                    if feed:
                        act.wait_ge(widened, f + 1)
                        act.wait_ge(ffn_in, (layer_of(f) + 1) * 16)
                        after(act, gated, NC_ * f)
                        for i, (_, size) in enumerate(CHUNKS):
                            act.activation(gelu[0:size, i, :], turn[0:size, 1, TILE * i:TILE * i + TILE], ACT.Gelu,
                                           bias=w_ffn[0:size, F_B1G + i:F_B1G + i + 1]).then_inc(gelued, 1)
                    if project:
                        act.wait_ge(v_projected, 2 * m + 2)
                        after(act, v_spread, 256 * m)
                        act.copy(v_tok[p][:, :, :, :], proj_a[:, :, :].rearrange("p a (h e) -> p a h e", e=HEAD))\
                            .then_inc(v_laid, 1)
                    if attend:
                        for j in range(2):
                            act.wait_ge(o_turned, 2 * n + j + 1)
                            after(act, attended, n)
                            act.copy(o_t[:, 4 * j:4 * j + 4, :],
                                     turn[:, 1 - j, :].rearrange("p (a t) -> p a t", t=TILE)).then_inc(o_laid, 1)

                run(act, step)

            @block.vector
            def _(dve):
                dve.memset(k_t[:, :, :], 0.0).then_inc(cleared, 1)
                dve.memset(v_tok[0][:, :, :, :], 0.0).then_inc(cleared, 1)
                dve.memset(v_tok[1][:, :, :, :], 0.0).then_inc(cleared, 1)
                dve.wait_ge(cleared, 3)
                dve.wait_ge(tables_in, 48)

                def unite(j, m):
                    dve.wait_ge(rotated_in[j], m + 1)
                    dve.wait_ge(rooted, ROOT_OPS * m + ROOT_OPS)
                    after(dve, (q_turned, k_turned)[j], 2 * m)
                    dve.tensor_tensor(unit[j][:, :, :], rotated[j][:, :, :],
                                      inv_norm[:, j, :].unsqueeze(2).broadcast_to([128, HEADS, HEAD]),
                                      ALU.mult).then_inc(united[j], 1)

                def root(ops, m):
                    inverse_root(dve, ops, sums_min[:, :, :], inv_norm[:, :, :], [w[:, :, :] for w in root_work],
                                 rooted, ROOT_OPS * m)

                def sum_squares(j, m):
                    dve.wait_ge(squared[j], m + 1)
                    after(dve, bounded, m)
                    dve.tensor_reduce(sums[:, j, :], squares[j][:, :, :], AX.X, ALU.add).then_inc(summed[j], 1)

                def divide_out(par, n):
                    dve.wait_ge(mixed, 2 * n + par + 1)
                    dve.wait_ge(mass_inverted, n + 1)
                    after(dve, o_turned, 2 * n)
                    dve.tensor_tensor(heads_out[:, :, par, :], att[:, par, :].rearrange("p (a e) -> p a e", e=HEAD),
                                      inv_mass[:, :].rearrange("p (a b) -> p a b", b=2)[:, :, par].unsqueeze(2)
                                      .broadcast_to([128, PAIRS, HEAD]), ALU.mult).then_inc(scaled_out, 1)

                def shift_layer_input(m, p):
                    after(dve, v_projected, 2 * (m - 1))
                    after(dve, xa_ready, m - 3)
                    stand_alone(dve, passed)
                    dve.tensor_copy(shift_a[p][0:64, :], xa[0:64, columns(m)]).then_inc(shifted, 1)
                    dve.tensor_copy(shift_a[p][64:128, :], xa[64:128, columns_before(m)]).then_inc(shifted, 1)

                def step(n, odd, attend, project, feed):
                    m, p, f = n + 1, 1 - odd, n - 1

                    def spread_rstd():
                        dve.wait_ge(rstd_made, f + 1)
                        dve.tensor_scalar(rstd_diag[:, :], identity[:, :], rstd_f[:, 0:1], None,
                                          ALU.mult).then_inc(rstd_laid, 1)

                    def keep_variance():
                        dve.wait_ge(var_made, f + 1)
                        dve.tensor_scalar(var_f[:, :], turn[:, 0, 0:1], LN_EPS, None, ALU.add).then_inc(var_kept, 1)

                    if isinstance(n, int) and n == -1:
                        shift_layer_input(0, 0)
                    if feed:
                        after(dve, xb_ready, f + 1)
                        after(dve, deviated, f)
                        stand_alone(dve, passed)
                        dve.tensor_copy(shift_f[0:64, :], xb[0:64, columns(f)]).then_inc(f_shifted, 1)
                        dve.tensor_copy(shift_f[64:128, :], xb[64:128, columns_before(f)]).then_inc(f_shifted, 1)
                        dve.wait_ge(mean_made, f + 1)
                        dve.wait_ge(f_shifted, 2 * f + 2)
                        after(dve, scaled_f, f)
                        dve.tensor_tensor(dev[:, :], shift_f[:, :], att[:, 1, 0:TILE], ALU.subtract).then_inc(deviated, 1)
                        dve.wait_ge(deviated, f + 1)
                        dve.tensor_tensor(dev_sq[:, :], dev[:, :], dev[:, :], ALU.mult).then_inc(dev_squared, 1)
                    if attend:
                        for par in range(2):
                            heads = slice(PAIRS * par, PAIRS * par + PAIRS)
                            scores = att[:, par, :].rearrange("p (a c) -> p a c", a=PAIRS)
                            dve.wait_ge(scored, 2 * n + par + 1)
                            dve.tensor_reduce(row_max[:, heads], scores, AX.X, ALU.max).then_inc(maxed, 1)
                            if feed and par == 0:
                                keep_variance()
                            dve.wait_ge(maxed, 2 * n + par + 1)
                            after(dve, weighed, 2 * n)
                            dve.tensor_tensor(logits[:, par, :, :], scores,
                                              row_max[:, heads].unsqueeze(2).broadcast_to([128, PAIRS, 2 * WINDOW]),
                                              ALU.subtract).then_inc(centred, 1)
                            if feed and par == 0:
                                spread_rstd()
                        dve.tensor_scalar(k_t[:, :, 0:WINDOW], k_t[:, :, TILE:TILE + WINDOW], carry_scale[:, 0:1], None,
                                          ALU.mult).then_inc(k_carried, 1)
                    elif feed:
                        keep_variance()
                        spread_rstd()
                    if feed:
                        dve.wait_ge(rstd_spread, f + 1)
                        dve.wait_ge(ffn_in, (layer_of(f) + 1) * 16)
                        dve.scalar_tensor_tensor(norm_g[:, :], dev[:, :], w_ffn[:, F_G:F_G + 1], turn[:, 1, 0:TILE],
                                                 ALU.mult, ALU.mult).then_inc(scaled_f, 1)
                        dve.wait_ge(scaled_f, f + 1)
                        after(dve, widened, f)
                        dve.tensor_scalar(normed[:, :], norm_g[:, :], w_ffn[:, F_B:F_B + 1], None,
                                          ALU.add).then_inc(normed_f, 1)
                    if project:
                        sum_squares(0, m)
                        turn_along(dve, 1, m, p)
                    if attend:
                        dve.wait_ge(weighed, 2 * n + 2)
                        dve.tensor_reduce(mass[:, :], probs[:, :, :, :].rearrange("p a b c -> p (a b) c"), AX.X,
                                          ALU.add).then_inc(massed, 1)
                    if project:
                        sum_squares(1, m)
                    if attend:
                        dve.wait_ge(massed, n + 1)
                        after(dve, scaled_out, 2 * n)
                        dve.reciprocal(inv_mass[:, :], mass[:, :]).then_inc(mass_inverted, 1)
                    if project:
                        for j in range(2):
                            dve.wait_ge(summed[j], m + 1)
                        dve.tensor_scalar(sums_min[:, :, :], sums[:, :, :], 1e-24, None, ALU.max).then_inc(bounded, 1)
                    if attend:
                        divide_out(0, n)
                    if project:
                        dve.wait_ge(bounded, m + 1)
                        after(dve, united[1], m)
                        root([0], m)
                    if feed:
                        for i, (_, size) in enumerate(CHUNKS):
                            dve.wait_ge(gelued, NC_ * f + i + 1)
                            after(dve, narrowed, f)
                            dve.scalar_tensor_tensor(hidden[0:size, i, :], turn[0:size, 0, TILE * i:TILE * i + TILE],
                                                     w_ffn[0:size, F_B1A + i:F_B1A + i + 1], gelu[0:size, i, :],
                                                     ALU.add, ALU.mult).then_inc(gated, 1)
                            if project:
                                root([i + 1], m)
                    if attend:
                        divide_out(1, n)
                    if project:
                        root(range(NC_ + 1 if feed else 1, ROOT_OPS), m)
                        unite(0, m)
                        shift_layer_input(m + 1, odd)
                        unite(1, m)
                    if feed:
                        dve.wait_ge(narrowed, f + 1)
                        dve.scalar_tensor_tensor(xa[:, columns(f)], att[:, 0, 0:TILE], w_ffn[:, F_B2:F_B2 + 1],
                                                 xb[:, columns(f)], ALU.add, ALU.add).then_inc(xa_ready, 1)
                    if attend:
                        dve.wait_ge(attended, n + 1)
                        dve.tensor_tensor(xb[:, columns(n)], att[:, 1, 0:TILE], xa[:, columns(n)], ALU.add)\
                            .then_inc(xb_ready, 1)

                run(dve, step)

            @block.tensor
            def _(pe):
                mask_first, mask_other = 0, 1

                def transposes(bank, source, count, signal):
                    for j in range(4):
                        mm = pe.transpose(bank[:, TILE * j:TILE * j + TILE], source(count * 4 + j), identity[:, :])
                    mm.then_inc(signal, 1)

                def project_values(par, m, p):
                    values = w_qkv[:, 2 * INNER:].rearrange("i (a b e) -> i b a e", a=PAIRS, b=2)
                    pe.matmul(proj_a[:, par, :].rearrange("p (a e) -> p a e", a=PAIRS), shift_a[p][:, :],
                              values[:, par, :, :], start=True, stop=True).then_inc(v_projected, 1)

                def step(n, odd, attend, project, feed):
                    m, p, f = n + 1, 1 - odd, n - 1

                    def pair(buffer):
                        return lambda a: buffer[:, 2 * a:2 * a + 2, :].rearrange("p h e -> p (h e)")

                    def variance():
                        pe.wait_ge(dev_squared, f + 1)
                        if attend:
                            pe.wait_ge(k_laid, 2 * n + 1)
                        pe.matmul(turn[:, 0, 0:1], dev_sq[:, :], averager[:, 0:1], start=True, stop=True)\
                            .then_inc(var_made, 1)

                    def project_half(j, half):
                        if half == 0:
                            if j == 0:
                                pe.wait_ge(shifted, 2 * m + 2)
                                pe.wait_ge(q_in, (layer_of(m) + 1) * 16)
                                after(pe, v_laid, m)
                            else:
                                pe.wait_ge(k_in, (layer_of(m) + 1) * 16)
                                after(pe, squared[1], m)
                            stand_alone(pe, passed)
                        base = INNER * j + 512 * half
                        mm = pe.matmul(slots[j][:, half, :], shift_a[p][:, :], w_qkv[:, base:base + 512],
                                       start=True, stop=True)
                        if half == 1:
                            mm.then_inc((q_projected, k_projected)[j], 1)

                    if attend:
                        pe.wait_ge(united[0], n + 1)
                        after(pe, o_laid, 2 * n)
                        for j in range(2):
                            transposes(turn[:, j, :], pair(unit[0]), j, q_turned)
                    if project:
                        project_half(0, 0)
                    if attend:
                        for j in range(2):
                            pe.wait_ge(united[1], n + 1)
                            pe.wait_ge(q_laid, 2 * n + j + 1)
                            transposes(turn[:, j, :], pair(unit[1]), j, k_turned)
                    if project:
                        project_half(0, 1)
                    if feed:
                        pe.wait_ge(f_shifted, 2 * f + 2)
                        pe.matmul(att[:, 1, 0:TILE], averager[:, :], shift_f[:, :], start=True, stop=True)\
                            .then_inc(mean_made, 1)
                    if attend:
                        which = (mask_first if n == 0 else mask_other) if isinstance(n, int) else (tile_of(n) + 15) // 16
                        band = band_bf[:, which, :].unsqueeze(1).broadcast_to([128, PAIRS, 2 * WINDOW])
                        for par in range(2):
                            pe.wait_ge(k_laid, 2 * n + 2)
                            if par == 0:
                                after(pe, xa_ready, n - 1)
                            elif feed:
                                pe.wait_ge(deviated, f + 1)
                            else:
                                after(pe, xb_ready, n)
                            rows = slice(HEAD * par, HEAD * par + HEAD)
                            pe.matmul(att[:, par, :].rearrange("p (a c) -> p a c", a=PAIRS), identity_bf[:, :], band,
                                      start=True, stop=False, skip_group_check=True)
                            for a in range(PAIRS):
                                for w in range(BLOCKS):
                                    mm = pe.matmul(att[WINDOW * w:WINDOW * w + WINDOW, par, HEAD * a:HEAD * a + HEAD],
                                                   q_t[rows, a, WINDOW * w:WINDOW * w + WINDOW],
                                                   k_t[rows, a, WINDOW * w:WINDOW * w + 2 * WINDOW],
                                                   start=False, stop=True, skip_group_check=True)
                            mm.then_inc(scored, 1)
                            if par == 0 and feed:
                                variance()
                            if par == 0 and project:
                                project_half(1, 0)
                    else:
                        if feed:
                            variance()
                        if project:
                            project_half(1, 0)
                    if project:
                        project_half(1, 1)
                    if feed:
                        pe.wait_ge(rstd_laid, f + 1)
                        pe.matmul(turn[:, 1, 0:TILE], ones[:, :], rstd_diag[:, :], start=True, stop=True)\
                            .then_inc(rstd_spread, 1)
                    if project:
                        pe.wait_ge(squared[0], m + 1)
                        pe.wait_ge(v_in, (layer_of(m) + 1) * 16)
                        project_values(0, m, p)
                    if attend:
                        pe.wait_ge(weighed, 2 * n + 2)
                        for j in range(2):
                            transposes(att[:, j, :], lambda a: probs[:, a, :, :].rearrange("p b c -> p (b c)"), j, p_turned)
                    if feed:
                        pe.wait_ge(normed_f, f + 1)
                        pe.wait_ge(ffn_in, (layer_of(f) + 1) * 16)
                        for half in (1, 0):
                            for i, (at, size) in enumerate(CHUNKS):
                                col = F_W1 + FFN * half + at
                                mm = pe.matmul(turn[0:size, half, TILE * i:TILE * i + TILE], w_ffn[:, col:col + size],
                                               normed[:, :], start=True, stop=True)
                        mm.then_inc(widened, 1)
                    if attend:
                        for par in range(2):
                            if par == 0:
                                pe.wait_ge(p_laid, 2 * n + 2)
                                pe.wait_ge(v_spread, 256 * n + 256)
                                stand_alone(pe, passed)
                            rows = slice(HEAD * par, HEAD * par + HEAD)
                            for a in range(PAIRS):
                                for w in range(BLOCKS):
                                    mm = pe.matmul(att[WINDOW * w:WINDOW * w + WINDOW, par, HEAD * a:HEAD * a + HEAD],
                                                   p_t[rows, a, WINDOW * w:WINDOW * w + WINDOW],
                                                   v_win[rows, w, HEAD * a:HEAD * a + HEAD], start=True, stop=True)
                            mm.then_inc(mixed, 1)
                            if par == 0 and project:
                                project_values(1, m, p)
                    elif project:
                        project_values(1, m, p)
                    if feed:
                        pe.wait_ge(gated, NC_ * f + NC_)
                        pe.wait_ge(scaled_out, 2 * n + 1 if attend else 2 * n)
                        for i, (_, size) in enumerate(CHUNKS):
                            mm = pe.matmul(att[:, 0, 0:TILE], w_ffn[0:size, F_W2 + DIM * i:F_W2 + DIM * i + DIM],
                                           hidden[0:size, i, :], start=(i == 0), stop=(i == NC_ - 1))
                        mm.then_inc(narrowed, 1)
                    if attend:
                        turned = lambda a: heads_out[:, a, :, :].rearrange("p b e -> p (b e)")
                        pe.wait_ge(scaled_out, 2 * n + 2)
                        if not feed:
                            pe.wait_ge(k_laid, 2 * n + 2)
                        transposes(turn[:, 1, :], turned, 0, o_turned)
                        transposes(turn[:, 0, :], turned, 1, o_turned)
                        pe.wait_ge(wo_in, (layer_of(n) + 1) * 16)
                        for a in range(PAIRS):
                            if a % 4 == 0:
                                pe.wait_ge(o_laid, 2 * n + a // 4 + 1)
                            mm = pe.matmul(att[:, 1, 0:TILE], w_o[:, a, :], o_t[:, a, :],
                                           start=(a == 0), stop=(a == PAIRS - 1))
                        mm.then_inc(attended, 1)

                run(pe, step)


def last_norm(nc, ctx, given):
    xa, x_tok, identity, out, att, turn = (given[k] for k in ("xa", "x_tok", "identity", "out", "att", "turn"))
    minus_half = given["minus_half"]
    GROUP = 4
    with ExitStack() as own:
        def sb(name, shape, dtype=F32):
            return own.enter_context(nc.sbuf_tensor(name, shape, dtype))

        def sem(name):
            return ctx.enter_context(nc.semaphore(name))

        total = sb("total", [128, TILES, DIM])
        stat = sb("stat", [128, TILES, 6])
        moment = sb("moment", [128, TILES, 2])
        var_l = sb("var_l", [128, TILES])
        rstd_l = sb("rstd_l", [128, TILES])
        final = sb("final", [128, TILES, DIM])
        l_turned, l_added, l_stat, l_moment, l_var, l_rstd, l_final, stored = (
            sem(k) for k in ("l_turned", "l_added", "l_stat", "l_moment", "l_var", "l_rstd", "l_final", "stored"))
        banks = [turn[:, 0, :], turn[:, 1, :], att[:, 0, :], att[:, 1, :]]
        with nc.Block() as block:
            @block.tensor
            def _(pe):
                for g in range(TILES // GROUP):
                    for j in range(GROUP):
                        t = GROUP * g + j
                        mm = pe.transpose(banks[g][:, DIM * j:DIM * j + DIM], xa[:, 1 + TILE * t:1 + TILE * t + TILE],
                                          identity[:, :])
                    mm.then_inc(l_turned, 1)

            @block.vector
            def _(dve):
                for g in range(TILES // GROUP):
                    tiles = slice(GROUP * g, GROUP * g + GROUP)
                    dve.wait_ge(l_turned, g + 1)
                    dve.tensor_tensor(total[:, tiles, :], banks[g].rearrange("p (t c) -> p t c", t=GROUP),
                                      x_tok[:, tiles, :], ALU.add).then_inc(l_added, 1)
                    dve.wait_ge(l_added, g + 1)
                    for t in range(GROUP * g, GROUP * g + GROUP):
                        dve.bn_stats(stat[:, t, :], total[:, t, :]).then_inc(l_stat, 1)
                    for t in range(GROUP * g, GROUP * g + GROUP):
                        dve.wait_ge(l_stat, t + 1)
                        dve.bn_aggr(moment[:, t, :], stat[:, t, :]).then_inc(l_moment, 1)
                    dve.wait_ge(l_moment, GROUP * g + GROUP)
                    dve.tensor_scalar(var_l[:, tiles], moment[:, tiles, 1], LN_EPS, None, ALU.add).then_inc(l_var, 1)
                for g in range(TILES // GROUP):
                    dve.wait_ge(l_rstd, g + 1)
                    for t in range(GROUP * g, GROUP * g + GROUP):
                        dve.tensor_scalar(final[:, t, :], total[:, t, :], moment[:, t, 0:1], rstd_l[:, t:t + 1],
                                          ALU.subtract, ALU.mult).then_inc(l_final, 1)

            @block.gpsimd
            def _(pool):
                for g in range(TILES // GROUP):
                    tiles = slice(GROUP * g, GROUP * g + GROUP)
                    pool.wait_ge(l_var, g + 1)
                    pool.tensor_tensor(rstd_l[:, tiles], var_l[:, tiles], minus_half[:, 0:GROUP], ALU.pow)\
                        .then_inc(l_rstd, 1)

            @block.sync
            def _(sp):
                for g in range(TILES // GROUP):
                    tiles = slice(GROUP * g, GROUP * g + GROUP)
                    sp.wait_ge(l_final, GROUP * g + GROUP)
                    sp.dma_start(out[0, 512 * g:512 * g + 512, :].rearrange("(t p) c -> p t c", p=TILE),
                                 final[:, tiles, :]).then_inc(stored, 16)
                sp.wait_ge(stored, 16 * (TILES // GROUP))


def position_tables():
    half = np.arange(0, HEAD, 2, dtype=np.float64)
    freq = 1.0 / 10000.0 ** (half / HEAD)
    t = np.arange(TOKENS, dtype=np.float64)
    angle = t[:, None] * freq[None, :]
    base = (half + 0.4 * HEAD) / (1.4 * HEAD)
    power = ((t % TILE) - TILE // 2) / (WINDOW // 2)
    scale = base[None, :] ** power[:, None]
    cos, sin = np.cos(angle), np.sin(angle)
    sign = np.concatenate([np.ones(HEAD // 2), -np.ones(HEAD // 2)])
    both = lambda a: np.concatenate([a, a], -1)
    tables = np.stack([both(cos * scale) * QK_SCALE, both(sin * scale) * sign * QK_SCALE,
                       both(cos / scale), both(sin / scale) * sign], 1)
    tables = tables.reshape(TILES, TILE, 4, HEAD).transpose(1, 0, 2, 3)
    carry = np.tile(np.concatenate([base, base]) ** (TILE // (WINDOW // 2)), 2)[:, None]
    return np.ascontiguousarray(tables, np.float32), np.ascontiguousarray(carry, np.float32)


def band_masks():
    a = np.arange(TILE)[:, None]
    c = np.arange(2 * WINDOW)[None, :]
    i = a % WINDOW
    hidden = (c - WINDOW > i) | (i > c)
    first = hidden | ((a < WINDOW) & (c < WINDOW))
    return np.stack([first, hidden], 1).astype(np.float32) * np.float32(MASKED_BIT)


def level_cuts():
    s = (np.arange(128) % WINDOW)[:, None]
    t = np.arange(WINDOW)[None, :]
    cuts = [(s == t) if b == 0 else ((t // b) % 2 == 1) & (s // b == t // b - 1) for b in MASKED]
    return np.stack(cuts, 1).astype(np.float32)


def kernel(**inputs):
    import concourse.bacc as bacc
    from concourse.bass_utils import run_bass_kernel_spmd

    a = {k.removeprefix("L0_"): np.ascontiguousarray(v) for k, v in inputs.items()}
    maa = [a["attn_time_maa_" + k] for k in "xwkvrg"]
    vectors = np.stack(maa + [a["attn_time_decay"], a["attn_time_faaaa"].reshape(-1)], 1)
    r_weights = np.stack([a["attn_W" + k] for k in "rkvgo"])
    r_norm = np.stack([a["attn_ln_w"], a["attn_ln_b"]])
    qk = np.stack([a["ffn_q_scale"], a["ffn_q_scale"], a["ffn_k_scale"], a["ffn_k_scale"]], 1)

    def rows(v, lead):
        wide = np.zeros((DEPTH, NC_ * 128) + v.shape[2:], v.dtype)
        wide[:, :FFN] = v
        return wide.reshape((DEPTH, NC_, 128) + v.shape[2:]).swapaxes(1, 2)

    ffn = np.concatenate([
        a["ffn_W1"],
        rows(a["ffn_W2"], DIM).reshape(DEPTH, 128, NC_ * DIM),
        a["ffn_ln_g"][:, :, None], a["ffn_ln_b"][:, :, None],
        rows(a["ffn_b1"][:, :FFN], 1), rows(a["ffn_b1"][:, FFN:], 1),
        a["ffn_b2"][:, :, None]], 2)
    tables, carry = position_tables()
    arrays = {
        "x": a["attn_x"], "vectors": vectors, "mix_w1": a["attn_time_maa_w1"], "mix_w2": a["attn_time_maa_w2"],
        "decay_w1": a["attn_time_decay_w1"], "decay_w2": a["attn_time_decay_w2"], "r_weights": r_weights,
        "r_norm": r_norm, "wqkv": a["ffn_Wqkv"], "wo": a["ffn_Wo"], "ffn": ffn, "qk_scales": qk,
        "positions": tables, "carry": carry, "ident": np.eye(128, dtype=np.float32), "band": band_masks(),
        "level_masks": level_cuts(),
    }
    arrays = {k + "_dram": np.ascontiguousarray(v) for k, v in arrays.items()}

    nc = bacc.Bacc("TRN2", target_bir_lowering=False, num_devices=1)
    args = [nc.dram_tensor(k, v.shape, mybir.dt.from_np(v.dtype), kind="ExternalInput").ap() for k, v in arrays.items()]
    out = nc.dram_tensor("out_dram", (1, TOKENS, DIM), F32, kind="ExternalOutput").ap()
    build(nc, *args, out)
    result = run_bass_kernel_spmd(nc, [arrays], core_ids=[0])
    return result.results[0]["out_dram"]
```

```python
from contextlib import ExitStack

import numpy as np

import concourse.bass as bass
from concourse import mybir

F32 = mybir.dt.float32
BF16 = mybir.dt.bfloat16
I32 = mybir.dt.int32
ALU = mybir.AluOpType
ACT = mybir.ActivationFunctionType
AX = mybir.AxisListType

TOKENS, DIM = 2048, 128
TILE = 128
TILES = TOKENS // TILE
HEADS, HEAD = 16, 64
PAIRS = HEADS // 2
INNER = HEADS * HEAD
DEPTH = 6
WINDOW = 32
BLOCKS = TILE // WINDOW
FFN = int(DIM * 4 * 2 / 3)
CHUNKS = [(0, 128), (128, 128), (256, FFN - 256)]
NC_ = len(CHUNKS)
STEPS = DEPTH * TILES
QK_SCALE = 8.0
LN_EPS = 1e-5
GROUP_EPS = 1e-5 * 8 ** 2
R_HEADS, R_HEAD = 2, 64
MIXES, LORA, DECAY_LORA = 5, 32, 64
MASKED = [0, 1, 2, 4, 8, 16]
MASKED_BIT = -1e30

V_MAA_X, V_MAA, V_DECAY, V_BONUS = 0, 1, 6, 7
F_W1, F_W2 = 0, 2 * FFN
F_G = F_W2 + NC_ * DIM
F_B, F_B1A, F_B1G, F_B2 = F_G + 1, F_G + 2, F_G + 2 + NC_, F_G + 2 + 2 * NC_
F_COLS = F_B2 + 1


def after(engine, semaphore, count):
    if not isinstance(count, int) or count > 0:
        engine.wait_ge(semaphore, count)


def stand_alone(engine, passed):
    engine.sem_inc(passed, 1)


ROOT_OPS = 10


def inverse_root(dve, ops, x, y, work, done, before):
    for i in ops:
        if i:
            dve.wait_ge(done, before + i)
        if i == 0:
            dve.tensor_scalar(y.bitcast(I32), x.bitcast(I32), -0.5, float(0x5F3759DF), ALU.mult, ALU.add)\
                .then_inc(done, 1)
        elif i % 3 == 1:
            dve.scalar_tensor_tensor(work[0], y, -0.5, y, ALU.mult, ALU.mult).then_inc(done, 1)
        elif i % 3 == 2:
            dve.tensor_tensor(work[1], work[0], x, ALU.mult).then_inc(done, 1)
        else:
            dve.scalar_tensor_tensor(y, work[1], 1.5, y, ALU.add, ALU.mult).then_inc(done, 1)


def tile_of(n):
    return n % TILES


def layer_of(n):
    return n // TILES


def columns(n):
    return bass.ds(tile_of(n) * TILE + 1, TILE)


def columns_before(n):
    return bass.ds(tile_of(n) * TILE, TILE)


def build(nc, x, vectors, mix_w1, mix_w2, decay_w1, decay_w2, r_weights, r_norm, wqkv, wo, ffn, qk_scales,
          positions, carry, ident, band, level_masks, out):
    with ExitStack() as ctx:
        def sb(name, shape, dtype=F32):
            return ctx.enter_context(nc.sbuf_tensor(name, shape, dtype))

        def sem(name):
            return ctx.enter_context(nc.semaphore(name))

        xa = sb("xa", [128, TOKENS + 1])
        xb = sb("xb", [128, TOKENS + 1])
        x_tok = sb("x_tok", [128, TILES, DIM])
        identity = sb("identity", [128, 128])
        identity_bf = sb("identity_bf", [128, 128], BF16)
        band_f = sb("band_f", [128, 2, 2 * WINDOW])
        band_bf = sb("band_bf", [128, 2, 2 * WINDOW], BF16)
        averager = sb("averager", [128, 128])
        ones = sb("ones", [128, 128])
        minus_half = sb("minus_half", [128, 8])

        w_qkv = sb("w_qkv", [128, 3 * INNER])
        w_o = sb("w_o", [128, PAIRS, DIM])
        w_ffn = sb("w_ffn", [128, F_COLS])
        scales = sb("scales", [128, DEPTH, 4, HEAD])
        where = sb("where", [128, TILES, 4, HEAD])
        carry_scale = sb("carry_scale", [128, 1])

        proj_a = ctx.enter_context(nc.psum_tensor("proj_a", [128, 2, 512], F32))
        proj_b = ctx.enter_context(nc.psum_tensor("proj_b", [128, 2, 512], F32))
        att = ctx.enter_context(nc.psum_tensor("att", [128, 2, 512], F32))
        turn = ctx.enter_context(nc.psum_tensor("turn", [128, 2, 512], F32))

        constants_in = sem("constants_in")
        passed = sem("passed")
        constants_made = sem("constants_made")
        x_in = [sem(f"x_in{g}") for g in range(4)]
        tables_in = sem("tables_in")
        q_in, k_in, v_in, wo_in, ffn_in = (sem(k) for k in ("q_in", "k_in", "v_in", "wo_in", "ffn_in"))

        def load_projection(sp, layer, j):
            part = slice(INNER * j, INNER * j + INNER)
            sp.dma_start(w_qkv[:, part], wqkv[layer, :, part]).then_inc((q_in, k_in, v_in)[j], 16)

        def load_wo(sp, layer):
            sp.dma_start(w_o[:, :, :], wo[layer].rearrange("(p i) o -> i p o", i=128)).then_inc(wo_in, 16)

        def load_ffn(sp, layer):
            sp.dma_start(w_ffn[:, :], ffn[layer]).then_inc(ffn_in, 16)

        time_mix(nc, ctx, locals())
        layers(nc, ctx, locals())
        last_norm(nc, ctx, locals())


def time_mix(nc, ctx, given):
    x, vectors, mix_w1, mix_w2, decay_w1, decay_w2, r_weights, r_norm, ident, band, level_masks = (
        given[k] for k in ("x", "vectors", "mix_w1", "mix_w2", "decay_w1", "decay_w2", "r_weights", "r_norm",
                           "ident", "band", "level_masks"))
    xa, xb, x_tok, identity, identity_bf, band_f, band_bf, averager, ones, minus_half = (
        given[k] for k in ("xa", "xb", "x_tok", "identity", "identity_bf", "band_f", "band_bf", "averager",
                           "ones", "minus_half"))
    proj_a, proj_b, att, turn = (given[k] for k in ("proj_a", "proj_b", "att", "turn"))
    constants_in, constants_made, x_in, passed = (
        given[k] for k in ("constants_in", "constants_made", "x_in", "passed"))
    positions, carry, qk_scales, where, carry_scale, scales, tables_in = (
        given[k] for k in ("positions", "carry", "qk_scales", "where", "carry_scale", "scales", "tables_in"))
    load_projection, load_wo, load_ffn = (given[k] for k in ("load_projection", "load_wo", "load_ffn"))

    with ExitStack() as own:
        def sb(name, shape, dtype=F32):
            return own.enter_context(nc.sbuf_tensor(name, shape, dtype))

        def sem(name):
            return ctx.enter_context(nc.semaphore(name))

        vec = sb("vec", [128, 8])
        w1 = sb("w1", [128, MIXES * LORA])
        w2_wide = sb("w2_wide", [128, MIXES, DIM])
        dw1 = sb("dw1", [128, DECAY_LORA])
        dw2 = sb("dw2", [DECAY_LORA, DIM])
        wr = sb("wr", [128, 5, DIM])
        norm_rows = sb("norm_rows", [128, 2, DIM])
        masks = sb("masks", [128, len(MASKED), WINDOW])

        xx = sb("xx", [128, TILE])
        x_mixed = sb("x_mixed", [128, TILE])
        mix = sb("mix", [128, TILE])
        mix_last = sb("mix_last", [LORA, TILE])
        share = sb("share", [128, MIXES, TILE])
        shift_part = sb("shift_part", [128, MIXES, TILE])
        streams = sb("streams", [128, MIXES, TILE])
        low = sb("low", [DECAY_LORA, TILE])
        rate = sb("rate", [128, TILE])
        decay_one = [sb(f"decay_one{i}", [128, TILE]) for i in range(2)]
        decay = [sb(f"decay{i}", [128, TILE >> i]) for i in range(1, 8)]
        rf = [sb(f"rf{i}", [128, TILE]) for i in range(2)]
        rf_bonus = [sb(f"rf_bonus{i}", [128, TILE]) for i in range(2)]
        kf = [sb(f"kf{i}", [128, TILE]) for i in range(2)]
        v_tok = [sb(f"v_tok{i}", [128, DIM]) for i in range(2)]
        gate_t = sb("gate_t", [128, DIM])
        gate_s = sb("gate_s", [128, DIM])
        gate = [sb(f"gate{i}", [128, DIM]) for i in range(2)]
        cut = sb("cut", [128, R_HEADS, len(MASKED), WINDOW])
        coef = sb("coef", [128, R_HEADS, TILE])
        k_tok = sb("k_tok", [128, DIM])
        state = sb("state", [128, DIM])
        stats = sb("stats", [128, R_HEADS, 6])
        moments = sb("moments", [128, R_HEADS, 2])
        var_eps = sb("var_eps", [128, R_HEADS])
        rstd = sb("rstd", [128, R_HEADS])
        y_n = sb("y_n", [128, DIM])
        y_w = sb("y_w", [128, DIM])
        y_b = sb("y_b", [128, DIM])
        y_g = sb("y_g", [128, DIM])
        y_t = sb("y_t", [128, TILE])
        res = sb("res", [128, DIM])
        stats2 = sb("stats2", [128, 6])
        moments2 = sb("moments2", [128, 2])
        var_eps2 = sb("var_eps2", [128, 1])
        rstd2 = sb("rstd2", [128, 1])
        x_one = sb("x_one", [128, DIM])

        weights_in = sem("weights_in")
        zeroed, converted, cleared = sem("zeroed"), sem("converted"), sem("cleared_r")
        w2_in = sem("w2_in")
        x_turned, x_laid = sem("x_turned"), sem("x_laid")
        s_xx, s_xmix = sem("s_xx"), sem("s_xmix")
        s_low_mix, s_mix, s_mix_up = sem("s_low_mix"), sem("s_mix"), sem("s_mix_up")
        s_add, s_mul, s_streams = sem("s_add"), sem("s_mul"), sem("s_streams")
        s_lora1, s_lora_t, s_lora2 = sem("s_lora1"), sem("s_lora_t"), sem("s_lora2")
        s_rate, s_decay = sem("s_rate"), sem("s_decay")
        s_rk, s_vg = sem("s_rk"), sem("s_vg")
        s_r, s_rb, s_k, s_v = sem("s_r"), sem("s_rb"), sem("s_k"), sem("s_v")
        s_gt, s_gs, s_gate = sem("s_gt"), sem("s_gs"), sem("s_gate")
        s_level, s_scaled = sem("s_level"), sem("s_scaled")
        s_cut, s_coef, s_coef_far = sem("s_cut"), sem("s_coef"), sem("s_coef_far")
        s_kturn, s_ktok, s_y, s_su, s_state = (sem(k) for k in ("s_kturn", "s_ktok", "s_y", "s_su", "s_state"))
        s_stat, s_mom, s_ve, s_pow, s_yn, s_yw, s_yb, s_yg = (
            sem(k) for k in ("s_stat", "s_mom", "s_ve", "s_pow", "s_yn", "s_yw", "s_yb", "s_yg"))
        s_yturn, s_yt, s_out, s_res = (sem(k) for k in ("s_yturn", "s_yt", "s_out", "s_res"))
        s_stat2, s_mom2, s_ve2, s_pow2, s_one, s_keep, s_oturn, s_done = (
            sem(k) for k in ("s_stat2", "s_mom2", "s_ve2", "s_pow2", "s_one", "s_keep", "s_oturn", "s_done"))
        LEVELS = 7

        def levels_of(buffer, b):
            return buffer[:, :].rearrange("p (m two b) -> p m two b", two=2, b=b)

        def run(engine, step):
            step(-1, 1, True, False, False)
            step(0, 0, True, True, False)
            with engine.Fori(0, (TILES - 2) // 2) as half:
                step(half * 2 + 1, 1, True, True, True)
                step(half * 2 + 2, 0, True, True, True)
            step(TILES - 1, 1, False, True, True)
            step(TILES, 0, False, False, True)

        low_mix = proj_a[:, 1, 128:256], proj_a[0:LORA, 1, 256:384]
        lora_low, lora_rate = proj_a[0:DECAY_LORA, 1, 256:384], proj_a[:, 1, 384:512]
        k_turned, state_add = att[:, 1, 384:512], turn[:, 0, 128:256]
        level_32, level_64 = turn[:, :, 384:416], turn[:, :, 416:480]
        y_sum, y_turned = turn[:, 0, 0:DIM], turn[:, 1, 0:TILE]
        projected, x_one_turned = turn[:, 1, 128:256], turn[:, 1, 256:384]

        with nc.Block() as block:
            @block.sync
            def _(sp):
                for g in range(4):
                    sp.dma_start(x_tok[:, 4 * g:4 * g + 4, :],
                                 x[0, 512 * g:512 * g + 512, :].rearrange("(t p) c -> p t c", p=TILE)).then_inc(x_in[g], 16)
                sp.dma_start(vec[:, :], vectors).then_inc(weights_in, 16)
                sp.dma_start(w1[:, :], mix_w1).then_inc(weights_in, 16)
                sp.dma_start(dw1[:, :], decay_w1).then_inc(weights_in, 16)
                sp.dma_start(dw2[:, :], decay_w2).then_inc(weights_in, 16)
                sp.dma_start(wr[:, :, :], r_weights.rearrange("w i o -> i w o")).then_inc(weights_in, 16)
                sp.dma_start(norm_rows[:, :, :], r_norm.partition_broadcast(128)).then_inc(weights_in, 16)
                sp.dma_start(masks[:, :, :], level_masks).then_inc(weights_in, 16)
                sp.wait_ge(zeroed, 1)
                for s in range(MIXES):
                    row = LORA * (s % 4)
                    sp.dma_start(w2_wide[row:row + LORA, s, :], mix_w2[s]).then_inc(w2_in, 16)
                for j in range(3):
                    load_projection(sp, 0, j)
                sp.dma_start(carry_scale[:, :], carry).then_inc(tables_in, 16)
                sp.dma_start(where[:, :, :, :], positions).then_inc(tables_in, 16)
                sp.dma_start(scales[:, :, :, :], qk_scales.partition_broadcast(128)).then_inc(tables_in, 16)
                load_wo(sp, 0)
                load_ffn(sp, 0)

            @block.gpsimd
            def _(pool):
                pool.memset(w2_wide[:, :, :], 0.0).then_inc(zeroed, 1)
                pool.memset(averager[:, :], 1.0 / DIM).then_inc(constants_made, 1)
                pool.memset(ones[:, :], 1.0).then_inc(constants_made, 1)
                pool.memset(minus_half[:, :], -0.5).then_inc(constants_made, 1)
                pool.wait_ge(constants_made, 3)
                with pool.Fori(0, TILES) as c:
                    pool.wait_ge(s_ve, c * 2 + 2)
                    pool.tensor_tensor(rstd[:, :], var_eps[:, :], minus_half[:, 0:R_HEADS], ALU.pow).then_inc(s_pow, 1)
                    pool.wait_ge(s_ve2, c + 1)
                    pool.tensor_tensor(rstd2[:, :], var_eps2[:, :], minus_half[:, 0:1], ALU.pow).then_inc(s_pow2, 1)

            @block.scalar
            def _(act):
                act.dma_start(identity[:, :], ident).then_inc(constants_in, 16)
                act.dma_start(band_f[:, :, :], band).then_inc(constants_in, 16)
                for g in range(4):
                    act.wait_ge(x_turned, g + 1)
                    act.copy(xb[:, 1 + 512 * g:1 + 512 * g + 512], turn[:, g % 2, :]).then_inc(x_laid, 1)
                act.wait_ge(weights_in, 16 * 7)

                def step(i, odd, mix_next, weigh, finish):
                    m, p, e = i + 1, 1 - odd, i - 1
                    if mix_next:
                        act.wait_ge(s_low_mix, m + 1)
                        act.activation(mix[:, :], low_mix[0], ACT.Tanh).then_inc(s_mix, 1)
                        act.activation(mix_last[:, :], low_mix[1], ACT.Tanh).then_inc(s_mix, 1)
                    if finish:
                        act.wait_ge(s_yturn, e + 1)
                        act.copy(y_t[:, :], y_turned).then_inc(s_yt, 1)
                    if weigh:
                        act.wait_ge(s_level, i * 8 + 8)
                        act.copy(coef[0:32, :, 32:64], level_32[0:32, :, :]).then_inc(s_coef_far, 1)
                        act.copy(coef[64:96, :, 96:128], level_32[64:96, :, :]).then_inc(s_coef_far, 1)
                        act.copy(coef[0:64, :, 64:128], level_64[0:64, :, :]).then_inc(s_coef_far, 1)
                    if mix_next:
                        act.wait_ge(s_lora1, m + 1)
                        act.activation(low[:, :], lora_low, ACT.Tanh).then_inc(s_lora_t, 1)
                        act.wait_ge(s_vg, m + 1)
                        after(act, s_su, m - 1)
                        act.copy(v_tok[p][:, :], proj_b[:, 1, 0:DIM]).then_inc(s_v, 1)
                        after(act, s_gate, m)
                        act.activation(gate_t[:, :], proj_b[:, 1, DIM:2 * DIM], ACT.Tanh, scale=0.5).then_inc(s_gt, 1)
                    if weigh:
                        act.wait_ge(s_kturn, i + 1)
                        act.copy(k_tok[:, :], k_turned).then_inc(s_ktok, 1)
                    if mix_next:
                        act.wait_ge(s_lora2, m + 1)
                        after(act, s_decay, m)
                        act.activation(rate[:, :], lora_rate, ACT.Exp, bias=vec[:, V_DECAY:V_DECAY + 1]).then_inc(s_rate, 1)
                        act.wait_ge(s_rate, m + 1)
                        act.activation(decay_one[p][:, :], rate[:, :], ACT.Exp, scale=-1.0).then_inc(s_decay, 1)
                    if finish:
                        act.wait_ge(s_oturn, e + 1)
                        act.copy(xa[:, bass.ds(e * TILE + 1, TILE)], x_one_turned).then_inc(s_done, 1)

                run(act, step)

            @block.vector
            def _(dve):
                dve.memset(xa[:, 0:1], 0.0).then_inc(cleared, 1)
                dve.memset(xb[:, 0:1], 0.0).then_inc(cleared, 1)
                dve.memset(coef[:, :, :], 0.0).then_inc(cleared, 1)
                dve.memset(state[:, :], 0.0).then_inc(cleared, 1)
                dve.wait_ge(constants_in, 32)
                dve.tensor_copy(identity_bf[:, :], identity[:, :]).then_inc(converted, 1)
                dve.tensor_copy(band_bf[:, :, :], band_f[:, :, :]).then_inc(converted, 1)
                dve.wait_ge(weights_in, 16 * 7)
                dve.wait_ge(cleared, 4)
                dve.wait_ge(x_laid, 4)
                maa = vec[:, V_MAA:V_MAA + MIXES].unsqueeze(2).broadcast_to([128, MIXES, TILE])

                def scale_level(c, j, odd):
                    b = 1 << j
                    r_v, k_v = levels_of(rf[odd], b), levels_of(kf[odd], b)
                    pairs = TILE // (2 * b)
                    d_v = (decay[j - 1] if j else decay_one[odd])[:, :].rearrange("p (m two) -> p m two", two=2)
                    dve.wait_ge(s_level, c * 8 + j + 2)
                    if j:
                        dve.wait_ge(s_scaled, c * 3 * LEVELS + 3 * j)
                    else:
                        dve.wait_ge(s_decay, c + 1)
                        dve.wait_ge(s_k, c + 1)
                        after(dve, s_state, c * R_HEADS)
                    dve.tensor_tensor(r_v[:, :, 1, :], r_v[:, :, 1, :],
                                      d_v[:, :, 0:1].broadcast_to([128, pairs, b]), ALU.mult).then_inc(s_scaled, 1)
                    dve.tensor_tensor(k_v[:, :, 0, :], k_v[:, :, 0, :],
                                      d_v[:, :, 1:2].broadcast_to([128, pairs, b]), ALU.mult).then_inc(s_scaled, 1)
                    dve.tensor_tensor(decay[j][:, :], d_v[:, :, 0], d_v[:, :, 1], ALU.mult).then_inc(s_scaled, 1)

                def step(i, odd, mix_next, weigh, finish):
                    m, p, e = i + 1, 1 - odd, i - 1
                    here = xb[:, bass.ds(m * TILE + 1, TILE)] if mix_next else None

                    def add_levels(blocks):
                        dve.wait_ge(s_cut, i + 1)
                        for q in blocks:
                            part = slice(WINDOW * q, WINDOW * q + WINDOW)
                            dve.tensor_reduce(coef[part, :, part], cut[part, :, :, :].rearrange("p h l t -> p h t l"),
                                              AX.X, ALU.add).then_inc(s_coef, 1)

                    if weigh:
                        scale_level(i, 0, odd)
                    if finish:
                        dve.wait_ge(s_y, e + 1)
                        for h in range(R_HEADS):
                            dve.bn_stats(stats[:, h, :], turn[:, 0, R_HEAD * h:R_HEAD * h + R_HEAD]).then_inc(s_stat, 1)
                    if mix_next:
                        dve.tensor_tensor(xx[:, :], xb[:, bass.ds(m * TILE, TILE)], here, ALU.subtract).then_inc(s_xx, 1)
                    if finish:
                        dve.wait_ge(s_stat, e * 2 + 2)
                        stand_alone(dve, passed)
                        for h in range(R_HEADS):
                            dve.bn_aggr(moments[:, h, :], stats[:, h, :]).then_inc(s_mom, 1)
                    if mix_next:
                        dve.wait_ge(s_xx, m + 1)
                        dve.scalar_tensor_tensor(x_mixed[:, :], xx[:, :], vec[:, V_MAA_X:V_MAA_X + 1], here,
                                                 ALU.mult, ALU.add).then_inc(s_xmix, 1)
                    if finish:
                        for h in range(R_HEADS):
                            dve.wait_ge(s_mom, e * 2 + h + 1)
                            dve.tensor_scalar(var_eps[:, h:h + 1], moments[:, h, 1:2], GROUP_EPS, None,
                                              ALU.add).then_inc(s_ve, 1)
                    if weigh:
                        scale_level(i, 1, odd)
                        scale_level(i, 2, odd)
                    if finish:
                        dve.wait_ge(s_pow, e + 1)
                        for h in range(R_HEADS):
                            part = slice(R_HEAD * h, R_HEAD * h + R_HEAD)
                            dve.tensor_scalar(y_n[:, part], turn[:, 0, part], moments[:, h, 0:1], rstd[:, h:h + 1],
                                              ALU.subtract, ALU.mult).then_inc(s_yn, 1)
                        dve.wait_ge(s_yn, e * 2 + 2)
                        dve.tensor_tensor(y_w[:, :], y_n[:, :], norm_rows[:, 0, :], ALU.mult).then_inc(s_yw, 1)
                        dve.wait_ge(s_yw, e + 1)
                        dve.tensor_tensor(y_b[:, :], y_w[:, :], norm_rows[:, 1, :], ALU.add).then_inc(s_yb, 1)
                        dve.wait_ge(s_yb, e + 1)
                        dve.wait_ge(s_gate, e + 1)
                        dve.tensor_tensor(y_g[:, :], y_b[:, :], gate[p][:, :], ALU.mult).then_inc(s_yg, 1)
                    if weigh:
                        scale_level(i, 3, odd)
                    if mix_next:
                        dve.wait_ge(s_mix_up, m + 1)
                        wide = proj_a[:, :, :].rearrange("p a b -> p (a b)")[:, 0:MIXES * TILE].rearrange(
                            "p (s t) -> p s t", s=MIXES)
                        dve.tensor_tensor(share[:, :, :], wide, maa, ALU.add).then_inc(s_add, 1)
                    if weigh:
                        scale_level(i, 4, odd)
                        after(dve, s_coef, i * BLOCKS)
                        dve.tensor_tensor(cut[:, :, :, :],
                                          att[:, :, 0:192].rearrange("p h (l t) -> p h l t", t=WINDOW),
                                          masks[:, :, :].unsqueeze(1).broadcast_to([128, R_HEADS, len(MASKED), WINDOW]),
                                          ALU.mult).then_inc(s_cut, 1)
                    if finish:
                        dve.wait_ge(s_out, e + 1)
                        dve.tensor_tensor(res[:, :], projected, x_tok[:, e, :], ALU.add).then_inc(s_res, 1)
                    if mix_next:
                        dve.wait_ge(s_add, m + 1)
                        dve.tensor_tensor(shift_part[:, :, :], share[:, :, :],
                                          xx[:, :].unsqueeze(1).broadcast_to([128, MIXES, TILE]),
                                          ALU.mult).then_inc(s_mul, 1)
                    if weigh:
                        scale_level(i, 5, odd)
                        add_levels((0, 1))
                    if finish:
                        dve.wait_ge(s_res, e + 1)
                        dve.bn_stats(stats2[:, :], res[:, :]).then_inc(s_stat2, 1)
                    if mix_next:
                        dve.wait_ge(s_mul, m + 1)
                        after(dve, s_vg, m)
                        dve.tensor_tensor(streams[:, :, :], shift_part[:, :, :],
                                          here.unsqueeze(1).broadcast_to([128, MIXES, TILE]),
                                          ALU.add).then_inc(s_streams, 1)
                    if finish:
                        dve.wait_ge(s_stat2, e + 1)
                        stand_alone(dve, passed)
                        dve.bn_aggr(moments2[:, :], stats2[:, :]).then_inc(s_mom2, 1)
                    if weigh:
                        scale_level(i, 6, odd)
                    if finish:
                        dve.wait_ge(s_mom2, e + 1)
                        dve.tensor_scalar(var_eps2[:, :], moments2[:, 1:2], LN_EPS, None, ALU.add).then_inc(s_ve2, 1)
                    if weigh:
                        add_levels((2, 3))
                    if mix_next:
                        dve.wait_ge(s_rk, m + 1)
                        after(dve, s_su, m - 1)
                        stand_alone(dve, passed)
                        dve.tensor_copy(rf[p][:, :], proj_b[:, 0, 0:TILE]).then_inc(s_r, 1)
                        dve.tensor_scalar(rf_bonus[p][:, :], proj_b[:, 0, 0:TILE], vec[:, V_BONUS:V_BONUS + 1], None,
                                          ALU.mult).then_inc(s_rb, 1)
                        dve.tensor_copy(kf[p][:, :], proj_b[:, 0, TILE:2 * TILE]).then_inc(s_k, 1)
                    if finish:
                        dve.wait_ge(s_pow2, e + 1)
                        after(dve, s_oturn, e)
                        after(dve, s_keep, e)
                        dve.tensor_scalar(x_one[:, :], res[:, :], moments2[:, 0:1], rstd2[:, 0:1],
                                          ALU.subtract, ALU.mult).then_inc(s_one, 1)
                    if mix_next:
                        dve.wait_ge(s_gt, m + 1)
                        after(dve, s_gate, m)
                        dve.tensor_scalar(gate_s[:, :], gate_t[:, :], 0.5, 0.5, ALU.mult, ALU.add).then_inc(s_gs, 1)
                        dve.wait_ge(s_gs, m + 1)
                        after(dve, s_yg, m - 1)
                        dve.tensor_tensor(gate[p][:, :], gate_s[:, :], proj_b[:, 1, DIM:2 * DIM], ALU.mult)\
                            .then_inc(s_gate, 1)
                    if finish:
                        dve.wait_ge(s_one, e + 1)
                        stand_alone(dve, passed)
                        dve.tensor_copy(x_tok[:, e, :], x_one[:, :]).then_inc(s_keep, 1)
                    if weigh:
                        dve.wait_ge(s_su, i + 1)
                        dve.wait_ge(s_scaled, i * 3 * LEVELS + 3 * LEVELS)
                        for h in range(R_HEADS):
                            part = slice(R_HEAD * h, R_HEAD * h + R_HEAD)
                            dve.scalar_tensor_tensor(state[part, part], state[part, part], decay[LEVELS - 1][part, 0:1],
                                                     state_add[part, part],
                                                     ALU.mult, ALU.add).then_inc(s_state, 1)

                run(dve, step)

            @block.tensor
            def _(pe):
                pe.wait_ge(constants_in, 32)
                for g in range(4):
                    pe.wait_ge(x_in[g], 16)
                    if g >= 2:
                        pe.wait_ge(x_laid, g - 1)
                    for j in range(4):
                        mm = pe.transpose(turn[:, g % 2, TILE * j:TILE * j + TILE], x_tok[:, 4 * g + j, :], identity[:, :])
                    mm.then_inc(x_turned, 1)
                pe.wait_ge(x_laid, 4)
                pe.wait_ge(weights_in, 16 * 7)
                pe.wait_ge(w2_in, 16 * MIXES)

                def level(j, r_buffer, odd):
                    for h in range(R_HEADS):
                        rows = slice(R_HEAD * h, R_HEAD * h + R_HEAD)
                        for q in range(BLOCKS):
                            cols = slice(WINDOW * q, WINDOW * q + WINDOW)
                            mm = pe.matmul(att[cols, h, WINDOW * j:WINDOW * j + WINDOW], kf[odd][rows, cols],
                                           r_buffer[rows, cols], start=True, stop=True)
                    mm.then_inc(s_level, 1)

                def near_level(i, j, odd):
                    pe.wait_ge(s_scaled, i * 3 * LEVELS + 3 * (j - 1))
                    stand_alone(pe, passed)
                    level(j, rf[odd], odd)

                def step(i, odd, mix_next, weigh, finish):
                    m, p, e = i + 1, 1 - odd, i - 1
                    if weigh:
                        pe.wait_ge(s_rb, i + 1)
                        pe.wait_ge(s_k, i + 1)
                        stand_alone(pe, passed)
                        level(0, rf_bonus[odd], odd)
                        level(1, rf[odd], odd)
                        near_level(i, 2, odd)

                    def mix_up(streams_now):
                        for j in streams_now:
                            if j < 4:
                                pe.matmul(proj_a[:, 0, TILE * j:TILE * j + TILE], w2_wide[:, j, :], mix[:, :],
                                          start=True, stop=True)
                            else:
                                pe.matmul(proj_a[:, 1, 0:TILE], w2_wide[0:LORA, 4, :], mix_last[:, :],
                                          start=True, stop=True).then_inc(s_mix_up, 1)

                    if mix_next:
                        pe.wait_ge(s_xmix, m + 1)
                        after(pe, s_rate, m)
                        pe.matmul(low_mix[0], w1[:, 0:128], x_mixed[:, :], start=True, stop=True)
                        pe.matmul(low_mix[1], w1[:, 128:160], x_mixed[:, :], start=True, stop=True)\
                            .then_inc(s_low_mix, 1)
                    if weigh:
                        near_level(i, 3, odd)
                    if mix_next:
                        pe.wait_ge(s_mix, m * 2 + 2)
                        mix_up((0, 1))
                    if weigh:
                        near_level(i, 4, odd)
                    if mix_next:
                        mix_up((2, 3, 4))
                    if finish:
                        pe.wait_ge(s_yg, e + 1)
                        after(pe, s_done, e)
                        pe.transpose(y_turned, y_g[:, :], identity[:, :]).then_inc(s_yturn, 1)
                    if weigh:
                        near_level(i, 5, odd)
                    if finish:
                        pe.wait_ge(s_yt, e + 1)
                        pe.matmul(projected, y_t[:, :], wr[:, 4, :], start=True, stop=True).then_inc(s_out, 1)
                    if weigh:
                        pe.wait_ge(s_scaled, i * 3 * LEVELS + 15)
                        after(pe, s_yn, i * R_HEADS)
                        after(pe, s_state, i * R_HEADS)
                        if finish:
                            pe.wait_ge(s_res, e + 1)
                        stand_alone(pe, passed)
                        for h in range(R_HEADS):
                            rows = slice(R_HEAD * h, R_HEAD * h + R_HEAD)
                            for q in (0, 2):
                                now = slice(WINDOW * q, WINDOW * q + WINDOW)
                                later = slice(WINDOW * q + WINDOW, WINDOW * q + 2 * WINDOW)
                                mm = pe.matmul(level_32[now, h, :], kf[odd][rows, now], rf[odd][rows, later],
                                               start=True, stop=True)
                        mm.then_inc(s_level, 1)
                        pe.wait_ge(s_scaled, i * 3 * LEVELS + 18)
                        stand_alone(pe, passed)
                        for h in range(R_HEADS):
                            rows = slice(R_HEAD * h, R_HEAD * h + R_HEAD)
                            mm = pe.matmul(level_64[0:64, h, :], kf[odd][rows, 0:64], rf[odd][rows, 64:128],
                                           start=True, stop=True)
                        mm.then_inc(s_level, 1)
                    if mix_next:
                        pe.wait_ge(s_streams, m + 1)
                        after(pe, s_k, m)
                        after(pe, s_gate, m)
                        pe.matmul(lora_low, dw1[:, :], streams[:, 0, :], start=True, stop=True).then_inc(s_lora1, 1)
                        pe.matmul(proj_b[:, 0, 0:TILE], wr[:, 0, :], streams[:, 3, :], start=True, stop=True)
                        pe.matmul(proj_b[:, 0, TILE:2 * TILE], wr[:, 1, :], streams[:, 1, :],
                                  start=True, stop=True).then_inc(s_rk, 1)
                        pe.matmul(proj_b[:, 1, 0:DIM], streams[:, 2, :], wr[:, 2, :], start=True, stop=True)
                        pe.matmul(proj_b[:, 1, DIM:2 * DIM], streams[:, 4, :], wr[:, 3, :],
                                  start=True, stop=True).then_inc(s_vg, 1)
                    if weigh:
                        pe.wait_ge(s_scaled, i * 3 * LEVELS + 21)
                        pe.wait_ge(s_cut, i + 1)
                        pe.transpose(k_turned, kf[odd][:, :], identity[:, :]).then_inc(s_kturn, 1)
                    if mix_next:
                        pe.wait_ge(s_lora_t, m + 1)
                        pe.matmul(lora_rate, dw2[:, :], low[:, :], start=True, stop=True).then_inc(s_lora2, 1)
                    if finish:
                        pe.wait_ge(s_one, e + 1)
                        if weigh:
                            pe.wait_ge(s_coef_far, i * 3 + 3)
                        pe.transpose(x_one_turned, x_one[:, :], identity[:, :]).then_inc(s_oturn, 1)
                    if weigh:
                        pe.wait_ge(s_coef, i * BLOCKS + BLOCKS)
                        pe.wait_ge(s_v, i + 1)
                        pe.wait_ge(s_coef_far, i * 3 + 3)
                        pe.matmul(y_sum, rf[odd][:, :], state[:, :], start=True, stop=False)
                        for h in range(R_HEADS):
                            part = slice(R_HEAD * h, R_HEAD * h + R_HEAD)
                            mm = pe.matmul(turn[:, 0, part], coef[:, h, :], v_tok[odd][:, part],
                                           start=False, stop=(h == 1))
                        mm.then_inc(s_y, 1)
                        pe.wait_ge(s_ktok, i + 1)
                        pe.matmul(state_add, k_tok[:, :], v_tok[odd][:, :], start=True, stop=True).then_inc(s_su, 1)

                run(pe, step)


def layers(nc, ctx, given):
    w_qkv, w_o, w_ffn, where, carry_scale, scales = (
        given[k] for k in ("w_qkv", "w_o", "w_ffn", "where", "carry_scale", "scales"))
    tables_in, q_in, k_in, v_in, wo_in, ffn_in = (
        given[k] for k in ("tables_in", "q_in", "k_in", "v_in", "wo_in", "ffn_in"))
    load_projection, load_wo, load_ffn = (given[k] for k in ("load_projection", "load_wo", "load_ffn"))
    xa, xb, identity, identity_bf, band_bf, averager, ones, minus_half = (
        given[k] for k in ("xa", "xb", "identity", "identity_bf", "band_bf", "averager", "ones", "minus_half"))
    proj_a, proj_b, att, turn = (given[k] for k in ("proj_a", "proj_b", "att", "turn"))
    constants_in, passed = given["constants_in"], given["passed"]

    with ExitStack() as own:
        def sb(name, shape, dtype=F32):
            return own.enter_context(nc.sbuf_tensor(name, shape, dtype))

        def sem(name):
            return ctx.enter_context(nc.semaphore(name))

        shift_a = [sb(f"shift_a{i}", [128, TILE]) for i in range(2)]
        turns = [sb(f"turns{i}", [128, 4, HEAD]) for i in range(2)]
        squares = [sb(f"squares{i}", [128, HEADS, HEAD]) for i in range(2)]
        sums = sb("sums", [128, 2, HEADS])
        sums_min = sb("sums_min", [128, 2, HEADS])
        inv_norm = sb("inv_norm", [128, 2, HEADS])
        root_work = [sb(f"root_work{i}", [128, 2, HEADS]) for i in range(2)]
        raw = [sb(f"raw{i}", [128, HEADS, HEAD]) for i in range(2)]
        unit = [sb(f"unit{i}", [128, HEADS, HEAD]) for i in range(2)]
        along = [sb(f"along{i}", [128, HEADS, HEAD]) for i in range(2)]
        across = [sb(f"across{i}", [128, HEADS, HEAD]) for i in range(2)]
        rotated = [sb(f"rotated{i}", [128, HEADS, HEAD]) for i in range(2)]
        q_t = sb("q_t", [128, PAIRS, TILE])
        k_t = sb("k_t", [128, PAIRS, WINDOW + TILE])
        v_tok = [sb(f"val{i}", [128, 2, PAIRS, HEAD]) for i in range(2)]
        v_win = sb("v_win", [128, BLOCKS, PAIRS * HEAD])
        row_max = sb("row_max", [128, HEADS])
        logits = sb("logits", [128, 2, PAIRS, 2 * WINDOW])
        probs = sb("probs", [128, PAIRS, 2, 2 * WINDOW])
        mass = sb("mass", [128, HEADS])
        inv_mass = sb("inv_mass", [128, HEADS])
        p_t = sb("p_t", [128, PAIRS, TILE])
        heads_out = sb("heads_out", [128, PAIRS, 2, HEAD])
        o_t = sb("o_t", [128, PAIRS, TILE])
        shift_f = sb("shift_f", [128, TILE])
        dev = sb("dev", [128, TILE])
        dev_sq = sb("dev_sq", [128, TILE])
        var_f = sb("var_f", [128, 1])
        rstd_f = sb("rstd_f", [128, 1])
        rstd_diag = sb("rstd_diag", [128, TILE])
        norm_g = sb("norm_g", [128, TILE])
        normed = sb("normed", [128, TILE])
        gelu = sb("gelu", [128, NC_, TILE])
        hidden = sb("hidden", [128, NC_, TILE])

        cleared = sem("cleared")
        shifted = sem("shifted")
        table_made = sem("table_made")
        q_projected, k_projected, v_projected = sem("q_projected"), sem("k_projected"), sem("v_projected")
        raw_kept = [sem("q_kept"), sem("k_kept")]
        squared = [sem("q_squared"), sem("k_squared")]
        summed = [sem("q_summed"), sem("k_summed")]
        bounded, rooted = sem("bounded"), sem("rooted")
        united = [sem("q_united"), sem("k_united")]
        alonged = [sem("q_alonged"), sem("k_alonged")]
        acrossed = [sem("q_acrossed"), sem("k_acrossed")]
        rotated_in = [sem("q_rotated"), sem("k_rotated")]
        q_turned, q_laid = sem("q_turned"), sem("q_laid")
        k_turned, k_laid, k_carried = sem("k_turned"), sem("k_laid"), sem("k_carried")
        v_laid, v_spread = sem("v_laid"), sem("v_spread")
        scored, maxed, centred, weighed = sem("scored"), sem("maxed"), sem("centred"), sem("weighed")
        massed, mass_inverted = sem("massed"), sem("mass_inverted")
        p_turned, p_laid, mixed, scaled_out = sem("p_turned"), sem("p_laid"), sem("mixed"), sem("scaled_out")
        o_turned, o_laid, attended, xb_ready = sem("o_turned"), sem("o_laid"), sem("attended"), sem("xb_ready")
        f_shifted, mean_made, deviated, dev_squared = (
            sem(k) for k in ("f_shifted", "mean_made", "deviated", "dev_squared"))
        var_made, var_kept, rstd_made, rstd_laid, rstd_spread, scaled_f, normed_f = (
            sem(k) for k in ("var_made", "var_kept", "rstd_made", "rstd_laid", "rstd_spread", "scaled_f", "normed_f"))
        widened, gelued, gated, narrowed, xa_ready = (
            sem(k) for k in ("widened", "gelued", "gated", "narrowed", "xa_ready"))

        slots = [proj_a, proj_b]

        def by_head(slot):
            return slot[:, :, :].rearrange("p a (h e) -> p (a h) e", e=HEAD)

        def halves(buffer):
            return buffer[:, :, :].rearrange("p h (two e) -> p h two e", two=2)

        def turn_along(engine, j, m, p):
            engine.wait_ge(table_made, m + 1)
            engine.wait_ge(raw_kept[j], m + 1)
            after(engine, rotated_in[j], m)
            engine.tensor_tensor(along[j][:, :, :], raw[j][:, :, :],
                              turns[p][:, 2 * j, :].unsqueeze(1).broadcast_to([128, HEADS, HEAD]),
                              ALU.mult).then_inc(alonged[j], 1)

        def run(engine, step):
            step(-1, 1, False, True, False)
            step(0, 0, True, True, False)
            with engine.Fori(0, (STEPS - 2) // 2) as i:
                step(i * 2 + 1, 1, True, True, True)
                step(i * 2 + 2, 0, True, True, True)
            step(STEPS - 1, 1, True, False, True)
            step(STEPS, 0, False, False, True)

        with nc.Block() as block:
            @block.sync
            def _(sp):
                def spread(m, odd):
                    now, old = v_tok[odd], v_tok[1 - odd]
                    sp.wait_ge(v_laid, m + 1)
                    stand_alone(sp, passed)
                    after(sp, mixed, 2 * m)
                    stand_alone(sp, passed)
                    for par in range(2):
                        base = 2 * WINDOW * par
                        own_rows = slice(base + WINDOW, base + 2 * WINDOW)
                        flat = [v[:, par, :, :].rearrange("p a e -> p (a e)") for v in (now, old)]
                        for w in range(BLOCKS):
                            sp.dma_start(v_win[own_rows, w, :],
                                         flat[0][WINDOW * w:WINDOW * w + WINDOW, :]).then_inc(v_spread, 16)
                            before = flat[0][WINDOW * (w - 1):WINDOW * w, :] if w else flat[1][TILE - WINDOW:TILE, :]
                            sp.dma_start(v_win[base:base + WINDOW, w, :], before).then_inc(v_spread, 16)

                def spread_pairs(first, last, base):
                    with sp.Fori(first // 2, last // 2) as i:
                        spread(base + i * 2, 0)
                        spread(base + i * 2 + 1, 1)

                sp.wait_ge(cleared, 2)
                spread_pairs(0, TILES - 2, 0)
                spread(TILES - 2, 0)
                with sp.Fori(1, DEPTH) as layer:
                    first = layer * TILES
                    sp.wait_ge(q_projected, first)
                    stand_alone(sp, passed)
                    load_projection(sp, layer, 0)
                    sp.wait_ge(k_projected, first)
                    stand_alone(sp, passed)
                    load_projection(sp, layer, 1)
                    sp.wait_ge(v_projected, 2 * first)
                    stand_alone(sp, passed)
                    load_projection(sp, layer, 2)
                    spread(first - 1, 1)
                    sp.wait_ge(attended, first)
                    stand_alone(sp, passed)
                    load_wo(sp, layer)
                    spread(first, 0)
                    sp.wait_ge(xa_ready, first)
                    stand_alone(sp, passed)
                    load_ffn(sp, layer)
                    spread(first + 1, 1)
                    spread_pairs(2, TILES - 2, first)
                    spread(first + TILES - 2, 0)
                spread(STEPS - 1, 1)

            @block.gpsimd
            def _(pool):
                pool.wait_ge(tables_in, 48)

                def step(n, odd, attend, project, feed):
                    m, p = n + 1, 1 - odd

                    def invert_deviation():
                        pool.wait_ge(var_kept, n)
                        pool.tensor_tensor(rstd_f[:, :], var_f[:, :], minus_half[:, 0:1], ALU.pow).then_inc(rstd_made, 1)

                    if not project:
                        invert_deviation()
                        return
                    after(pool, alonged[1], m - 1)
                    after(pool, acrossed[1], 2 * (m - 1))
                    pool.tensor_tensor(turns[p][:, :, :], where[:, tile_of(m), :, :], scales[:, layer_of(m), :, :],
                                       ALU.mult).then_inc(table_made, 1)
                    pool.wait_ge(table_made, m + 1)
                    for j in range(2):
                        pool.wait_ge(raw_kept[j], m + 1)
                        after(pool, rotated_in[j], m)
                        u, a = halves(raw[j]), halves(across[j])
                        for half in range(2):
                            table = turns[p][:, 2 * j + 1, 32 * half:32 * half + 32].unsqueeze(1).broadcast_to(
                                [128, HEADS, 32])
                            pool.tensor_tensor(a[:, :, 1 - half, :], u[:, :, half, :], table,
                                               ALU.mult).then_inc(acrossed[j], 1)
                            if feed and j == half == 0:
                                invert_deviation()
                        if j == 0:
                            turn_along(pool, 0, m, p)
                        pool.wait_ge(alonged[j], m + 1)
                        pool.wait_ge(acrossed[j], 2 * m + 2)
                        after(pool, united[j], m)
                        pool.tensor_tensor(rotated[j][:, :, :], along[j][:, :, :], across[j][:, :, :],
                                           ALU.add).then_inc(rotated_in[j], 1)

                run(pool, step)

            @block.scalar
            def _(act):
                def step(n, odd, attend, project, feed):
                    m, p, f = n + 1, 1 - odd, n - 1
                    if attend:
                        for j in range(2):
                            act.wait_ge(q_turned, 2 * n + j + 1)
                            after(act, scored, 2 * n)
                            act.copy(q_t[:, 4 * j:4 * j + 4, :], turn[:, j, :].rearrange("p (a t) -> p a t", t=TILE))\
                                .then_inc(q_laid, 1)
                        for j in range(2):
                            act.wait_ge(k_turned, 2 * n + j + 1)
                            after(act, k_carried, n)
                            act.copy(k_t[:, 4 * j:4 * j + 4, WINDOW:], turn[:, j, :].rearrange("p (a t) -> p a t", t=TILE))\
                                .then_inc(k_laid, 1)

                    def keep_raw(j):
                        act.wait_ge((q_projected, k_projected)[j], m + 1)
                        after(act, alonged[j], m)
                        after(act, acrossed[j], 2 * m)
                        act.copy(raw[j][:, :, :], by_head(slots[j])).then_inc(raw_kept[j], 1)

                    def square(j):
                        after(act, summed[j], m)
                        act.activation(squares[j][:, :, :], by_head(slots[j]), ACT.Square).then_inc(squared[j], 1)

                    if project:
                        keep_raw(0)
                        square(0)
                    if attend:
                        for par in range(2):
                            act.wait_ge(centred, 2 * n + par + 1)
                            after(act, p_turned, 2 * n)
                            after(act, massed, n)
                            act.activation(probs[:, :, par, :], logits[:, par, :, :], ACT.Exp).then_inc(weighed, 1)
                    if project:
                        keep_raw(1)
                    if attend:
                        for j in range(2):
                            act.wait_ge(p_turned, 2 * n + j + 1)
                            after(act, mixed, 2 * n)
                            act.copy(p_t[:, 4 * j:4 * j + 4, :], att[:, j, :].rearrange("p (a t) -> p a t", t=TILE))\
                                .then_inc(p_laid, 1)
                    if project:
                        square(1)
                    if feed:
                        act.wait_ge(widened, f + 1)
                        act.wait_ge(ffn_in, (layer_of(f) + 1) * 16)
                        after(act, gated, NC_ * f)
                        for i, (_, size) in enumerate(CHUNKS):
                            act.activation(gelu[0:size, i, :], turn[0:size, 1, TILE * i:TILE * i + TILE], ACT.Gelu,
                                           bias=w_ffn[0:size, F_B1G + i:F_B1G + i + 1]).then_inc(gelued, 1)
                    if attend:
                        for j in range(2):
                            act.wait_ge(o_turned, 2 * n + j + 1)
                            after(act, attended, n)
                            act.copy(o_t[:, 4 * j:4 * j + 4, :],
                                     att[:, j, :].rearrange("p (a t) -> p a t", t=TILE)).then_inc(o_laid, 1)
                    if project:
                        act.wait_ge(v_projected, 2 * m + 2)
                        after(act, v_spread, 256 * m)
                        act.copy(v_tok[p][:, :, :, :], proj_a[:, :, :].rearrange("p a (h e) -> p a h e", e=HEAD))\
                            .then_inc(v_laid, 1)

                run(act, step)

            @block.vector
            def _(dve):
                dve.memset(k_t[:, :, 0:WINDOW], 0.0).then_inc(cleared, 1)
                dve.memset(v_tok[1][TILE - WINDOW:TILE, :, :, :], 0.0).then_inc(cleared, 1)
                dve.wait_ge(cleared, 2)
                dve.wait_ge(tables_in, 48)

                def unite(j, m):
                    dve.wait_ge(rotated_in[j], m + 1)
                    dve.wait_ge(rooted, ROOT_OPS * m + ROOT_OPS)
                    after(dve, (q_turned, k_turned)[j], 2 * m)
                    dve.tensor_tensor(unit[j][:, :, :], rotated[j][:, :, :],
                                      inv_norm[:, j, :].unsqueeze(2).broadcast_to([128, HEADS, HEAD]),
                                      ALU.mult).then_inc(united[j], 1)

                def root(ops, m):
                    inverse_root(dve, ops, sums_min[:, :, :], inv_norm[:, :, :], [w[:, :, :] for w in root_work],
                                 rooted, ROOT_OPS * m)

                def sum_squares(j, m):
                    dve.wait_ge(squared[j], m + 1)
                    after(dve, bounded, m)
                    dve.tensor_reduce(sums[:, j, :], squares[j][:, :, :], AX.X, ALU.add).then_inc(summed[j], 1)

                def divide_out(par, n):
                    dve.wait_ge(mixed, 2 * n + par + 1)
                    dve.wait_ge(mass_inverted, n + 1)
                    after(dve, o_turned, 2 * n)
                    dve.tensor_tensor(heads_out[:, :, par, :], att[:, par, :].rearrange("p (a e) -> p a e", e=HEAD),
                                      inv_mass[:, :].rearrange("p (a b) -> p a b", b=2)[:, :, par].unsqueeze(2)
                                      .broadcast_to([128, PAIRS, HEAD]), ALU.mult).then_inc(scaled_out, 1)

                def shift_layer_input(m, p):
                    after(dve, v_projected, 2 * (m - 1))
                    after(dve, xa_ready, m - 3)
                    stand_alone(dve, passed)
                    dve.tensor_copy(shift_a[p][0:64, :], xa[0:64, columns(m)]).then_inc(shifted, 1)
                    dve.tensor_copy(shift_a[p][64:128, :], xa[64:128, columns_before(m)]).then_inc(shifted, 1)

                def step(n, odd, attend, project, feed):
                    m, p, f = n + 1, 1 - odd, n - 1

                    def spread_rstd():
                        dve.wait_ge(rstd_made, f + 1)
                        dve.tensor_scalar(rstd_diag[:, :], identity[:, :], rstd_f[:, 0:1], None,
                                          ALU.mult).then_inc(rstd_laid, 1)

                    def keep_variance():
                        dve.wait_ge(var_made, f + 1)
                        dve.tensor_scalar(var_f[:, :], turn[:, 0, 0:1], LN_EPS, None, ALU.add).then_inc(var_kept, 1)

                    if isinstance(n, int) and n == -1:
                        shift_layer_input(0, 0)
                    if feed:
                        after(dve, xb_ready, f + 1)
                        after(dve, deviated, f)
                        stand_alone(dve, passed)
                        dve.tensor_copy(shift_f[0:64, :], xb[0:64, columns(f)]).then_inc(f_shifted, 1)
                        dve.tensor_copy(shift_f[64:128, :], xb[64:128, columns_before(f)]).then_inc(f_shifted, 1)
                        dve.wait_ge(mean_made, f + 1)
                        dve.wait_ge(f_shifted, 2 * f + 2)
                        after(dve, scaled_f, f)
                        dve.tensor_tensor(dev[:, :], shift_f[:, :], att[:, 1, 0:TILE], ALU.subtract).then_inc(deviated, 1)
                        dve.wait_ge(deviated, f + 1)
                        dve.tensor_tensor(dev_sq[:, :], dev[:, :], dev[:, :], ALU.mult).then_inc(dev_squared, 1)
                    if attend:
                        for par in range(2):
                            heads = slice(PAIRS * par, PAIRS * par + PAIRS)
                            scores = att[:, par, :].rearrange("p (a c) -> p a c", a=PAIRS)
                            dve.wait_ge(scored, 2 * n + par + 1)
                            dve.tensor_reduce(row_max[:, heads], scores, AX.X, ALU.max).then_inc(maxed, 1)
                            if feed and par == 0:
                                keep_variance()
                            dve.wait_ge(maxed, 2 * n + par + 1)
                            after(dve, weighed, 2 * n)
                            dve.tensor_tensor(logits[:, par, :, :], scores,
                                              row_max[:, heads].unsqueeze(2).broadcast_to([128, PAIRS, 2 * WINDOW]),
                                              ALU.subtract).then_inc(centred, 1)
                            if par == 0:
                                if feed:
                                    spread_rstd()
                                if project:
                                    sum_squares(0, m)
                        dve.tensor_scalar(k_t[:, :, 0:WINDOW], k_t[:, :, TILE:TILE + WINDOW], carry_scale[:, 0:1], None,
                                          ALU.mult).then_inc(k_carried, 1)
                    else:
                        if feed:
                            keep_variance()
                            spread_rstd()
                        if project:
                            sum_squares(0, m)
                    if feed:
                        dve.wait_ge(rstd_spread, f + 1)
                        dve.wait_ge(ffn_in, (layer_of(f) + 1) * 16)
                        dve.scalar_tensor_tensor(norm_g[:, :], dev[:, :], w_ffn[:, F_G:F_G + 1], turn[:, 1, 0:TILE],
                                                 ALU.mult, ALU.mult).then_inc(scaled_f, 1)
                        dve.wait_ge(scaled_f, f + 1)
                        after(dve, widened, f)
                        dve.tensor_scalar(normed[:, :], norm_g[:, :], w_ffn[:, F_B:F_B + 1], None,
                                          ALU.add).then_inc(normed_f, 1)
                    if attend:
                        dve.wait_ge(weighed, 2 * n + 2)
                        dve.tensor_reduce(mass[:, :], probs[:, :, :, :].rearrange("p a b c -> p (a b) c"), AX.X,
                                          ALU.add).then_inc(massed, 1)
                    if project:
                        turn_along(dve, 1, m, p)
                        sum_squares(1, m)
                    if attend:
                        dve.wait_ge(massed, n + 1)
                        after(dve, scaled_out, 2 * n)
                        dve.reciprocal(inv_mass[:, :], mass[:, :]).then_inc(mass_inverted, 1)
                    if project:
                        for j in range(2):
                            dve.wait_ge(summed[j], m + 1)
                        dve.tensor_scalar(sums_min[:, :, :], sums[:, :, :], 1e-24, None, ALU.max).then_inc(bounded, 1)
                    if attend:
                        divide_out(0, n)
                    if project:
                        dve.wait_ge(bounded, m + 1)
                        after(dve, united[1], m)
                        root([0], m)
                    if feed:
                        for i, (_, size) in enumerate(CHUNKS):
                            dve.wait_ge(gelued, NC_ * f + i + 1)
                            after(dve, narrowed, f)
                            dve.scalar_tensor_tensor(hidden[0:size, i, :], turn[0:size, 0, TILE * i:TILE * i + TILE],
                                                     w_ffn[0:size, F_B1A + i:F_B1A + i + 1], gelu[0:size, i, :],
                                                     ALU.add, ALU.mult).then_inc(gated, 1)
                            if project:
                                root([i + 1], m)
                            if attend and i == 0:
                                divide_out(1, n)
                    elif attend:
                        divide_out(1, n)
                    if project:
                        root(range(NC_ + 1 if feed else 1, ROOT_OPS), m)
                    if feed:
                        dve.wait_ge(narrowed, f + 1)
                        dve.scalar_tensor_tensor(xa[:, columns(f)], turn[:, 1, 0:TILE], w_ffn[:, F_B2:F_B2 + 1],
                                                 xb[:, columns(f)], ALU.add, ALU.add).then_inc(xa_ready, 1)
                    if project:
                        unite(0, m)
                        shift_layer_input(m + 1, odd)
                        unite(1, m)
                    if attend:
                        dve.wait_ge(attended, n + 1)
                        dve.tensor_tensor(xb[:, columns(n)], att[:, 0, 0:TILE], xa[:, columns(n)], ALU.add)\
                            .then_inc(xb_ready, 1)

                run(dve, step)

            @block.tensor
            def _(pe):
                mask_first, mask_other = 0, 1

                def transposes(bank, source, count, signal):
                    for j in range(4):
                        mm = pe.transpose(bank[:, TILE * j:TILE * j + TILE], source(count * 4 + j), identity[:, :])
                    mm.then_inc(signal, 1)

                def project_values(par, m, p):
                    values = w_qkv[:, 2 * INNER:].rearrange("i (a b e) -> i b a e", a=PAIRS, b=2)
                    pe.matmul(proj_a[:, par, :].rearrange("p (a e) -> p a e", a=PAIRS), shift_a[p][:, :],
                              values[:, par, :, :], start=True, stop=True).then_inc(v_projected, 1)

                def step(n, odd, attend, project, feed):
                    m, p, f = n + 1, 1 - odd, n - 1

                    def pair(buffer):
                        return lambda a: buffer[:, 2 * a:2 * a + 2, :].rearrange("p h e -> p (h e)")

                    def variance():
                        pe.wait_ge(dev_squared, f + 1)
                        if attend:
                            pe.wait_ge(k_laid, 2 * n + 1)
                        pe.matmul(turn[:, 0, 0:1], dev_sq[:, :], averager[:, 0:1], start=True, stop=True)\
                            .then_inc(var_made, 1)

                    def project_half(j, half):
                        if half == 0:
                            if j == 0:
                                pe.wait_ge(shifted, 2 * m + 2)
                                pe.wait_ge(q_in, (layer_of(m) + 1) * 16)
                                after(pe, v_laid, m)
                            else:
                                pe.wait_ge(k_in, (layer_of(m) + 1) * 16)
                                after(pe, squared[1], m)
                            stand_alone(pe, passed)
                        base = INNER * j + 512 * half
                        mm = pe.matmul(slots[j][:, half, :], shift_a[p][:, :], w_qkv[:, base:base + 512],
                                       start=True, stop=True)
                        if half == 1:
                            mm.then_inc((q_projected, k_projected)[j], 1)

                    if attend:
                        pe.wait_ge(united[0], n + 1)
                        for j in range(2):
                            if j:
                                after(pe, xa_ready, n - 1)
                            transposes(turn[:, j, :], pair(unit[0]), j, q_turned)
                    if project:
                        project_half(0, 0)
                    if attend:
                        for j in range(2):
                            pe.wait_ge(united[1], n + 1)
                            pe.wait_ge(q_laid, 2 * n + j + 1)
                            transposes(turn[:, j, :], pair(unit[1]), j, k_turned)
                    if project:
                        project_half(0, 1)
                    if feed:
                        pe.wait_ge(f_shifted, 2 * f + 2)
                        pe.matmul(att[:, 1, 0:TILE], averager[:, :], shift_f[:, :], start=True, stop=True)\
                            .then_inc(mean_made, 1)
                    if attend:
                        which = (mask_first if n == 0 else mask_other) if isinstance(n, int) else (tile_of(n) + 15) // 16
                        band = band_bf[:, which, :].unsqueeze(1).broadcast_to([128, PAIRS, 2 * WINDOW])
                        for par in range(2):
                            pe.wait_ge(k_laid, 2 * n + 2)
                            if par == 0:
                                after(pe, xb_ready, n)
                            elif feed:
                                pe.wait_ge(deviated, f + 1)
                            rows = slice(HEAD * par, HEAD * par + HEAD)
                            pe.matmul(att[:, par, :].rearrange("p (a c) -> p a c", a=PAIRS), identity_bf[:, :], band,
                                      start=True, stop=False, skip_group_check=True)
                            for a in range(PAIRS):
                                for w in range(BLOCKS):
                                    mm = pe.matmul(att[WINDOW * w:WINDOW * w + WINDOW, par, HEAD * a:HEAD * a + HEAD],
                                                   q_t[rows, a, WINDOW * w:WINDOW * w + WINDOW],
                                                   k_t[rows, a, WINDOW * w:WINDOW * w + 2 * WINDOW],
                                                   start=False, stop=True, skip_group_check=True)
                            mm.then_inc(scored, 1)
                            if par == 0 and feed:
                                variance()
                            if par == 0 and project:
                                project_half(1, 0)
                    else:
                        if feed:
                            variance()
                        if project:
                            project_half(1, 0)
                    if project:
                        project_half(1, 1)
                    if feed:
                        pe.wait_ge(rstd_laid, f + 1)
                        pe.matmul(turn[:, 1, 0:TILE], ones[:, :], rstd_diag[:, :], start=True, stop=True)\
                            .then_inc(rstd_spread, 1)
                    if project:
                        pe.wait_ge(squared[0], m + 1)
                        pe.wait_ge(v_in, (layer_of(m) + 1) * 16)
                        project_values(0, m, p)
                    if attend:
                        pe.wait_ge(weighed, 2 * n + 2)
                        for j in range(2):
                            transposes(att[:, j, :], lambda a: probs[:, a, :, :].rearrange("p b c -> p (b c)"), j, p_turned)
                    if feed:
                        pe.wait_ge(normed_f, f + 1)
                        pe.wait_ge(ffn_in, (layer_of(f) + 1) * 16)
                        for half in (1, 0):
                            for i, (at, size) in enumerate(CHUNKS):
                                col = F_W1 + FFN * half + at
                                mm = pe.matmul(turn[0:size, half, TILE * i:TILE * i + TILE], w_ffn[:, col:col + size],
                                               normed[:, :], start=True, stop=True)
                        mm.then_inc(widened, 1)
                    if attend:
                        for par in range(2):
                            if par == 0:
                                pe.wait_ge(p_laid, 2 * n + 2)
                                pe.wait_ge(v_spread, 256 * n + 256)
                                stand_alone(pe, passed)
                            rows = slice(HEAD * par, HEAD * par + HEAD)
                            for a in range(PAIRS):
                                for w in range(BLOCKS):
                                    mm = pe.matmul(att[WINDOW * w:WINDOW * w + WINDOW, par, HEAD * a:HEAD * a + HEAD],
                                                   p_t[rows, a, WINDOW * w:WINDOW * w + WINDOW],
                                                   v_win[rows, w, HEAD * a:HEAD * a + HEAD], start=True, stop=True)
                            mm.then_inc(mixed, 1)
                    if project:
                        project_values(1, m, p)
                    if attend:
                        turned = lambda a: heads_out[:, a, :, :].rearrange("p b e -> p (b e)")
                        pe.wait_ge(scaled_out, 2 * n + 2)
                        for j in range(2):
                            transposes(att[:, j, :], turned, j, o_turned)
                    if feed:
                        pe.wait_ge(gated, NC_ * f + NC_)
                        for i, (_, size) in enumerate(CHUNKS):
                            mm = pe.matmul(turn[:, 1, 0:TILE], w_ffn[0:size, F_W2 + DIM * i:F_W2 + DIM * i + DIM],
                                           hidden[0:size, i, :], start=(i == 0), stop=(i == NC_ - 1))
                        mm.then_inc(narrowed, 1)
                    if attend:
                        pe.wait_ge(wo_in, (layer_of(n) + 1) * 16)
                        for a in range(PAIRS):
                            if a % 4 == 0:
                                pe.wait_ge(o_laid, 2 * n + a // 4 + 1)
                            mm = pe.matmul(att[:, 0, 0:TILE], w_o[:, a, :], o_t[:, a, :],
                                           start=(a == 0), stop=(a == PAIRS - 1))
                        mm.then_inc(attended, 1)

                run(pe, step)


def last_norm(nc, ctx, given):
    xa, x_tok, identity, out, att, turn = (given[k] for k in ("xa", "x_tok", "identity", "out", "att", "turn"))
    minus_half = given["minus_half"]
    GROUP = 4
    with ExitStack() as own:
        def sb(name, shape, dtype=F32):
            return own.enter_context(nc.sbuf_tensor(name, shape, dtype))

        def sem(name):
            return ctx.enter_context(nc.semaphore(name))

        total = sb("total", [128, TILES, DIM])
        stat = sb("stat", [128, TILES, 6])
        moment = sb("moment", [128, TILES, 2])
        var_l = sb("var_l", [128, TILES])
        rstd_l = sb("rstd_l", [128, TILES])
        final = sb("final", [128, TILES, DIM])
        l_turned, l_added, l_stat, l_moment, l_var, l_rstd, l_final, stored = (
            sem(k) for k in ("l_turned", "l_added", "l_stat", "l_moment", "l_var", "l_rstd", "l_final", "stored"))
        banks = [turn[:, 0, :], turn[:, 1, :], att[:, 0, :], att[:, 1, :]]
        with nc.Block() as block:
            @block.tensor
            def _(pe):
                for g in range(TILES // GROUP):
                    for j in range(GROUP):
                        t = GROUP * g + j
                        mm = pe.transpose(banks[g][:, DIM * j:DIM * j + DIM], xa[:, 1 + TILE * t:1 + TILE * t + TILE],
                                          identity[:, :])
                    mm.then_inc(l_turned, 1)

            @block.vector
            def _(dve):
                for g in range(TILES // GROUP):
                    tiles = slice(GROUP * g, GROUP * g + GROUP)
                    dve.wait_ge(l_turned, g + 1)
                    dve.tensor_tensor(total[:, tiles, :], banks[g].rearrange("p (t c) -> p t c", t=GROUP),
                                      x_tok[:, tiles, :], ALU.add).then_inc(l_added, 1)
                    dve.wait_ge(l_added, g + 1)
                    for t in range(GROUP * g, GROUP * g + GROUP):
                        dve.bn_stats(stat[:, t, :], total[:, t, :]).then_inc(l_stat, 1)
                    for t in range(GROUP * g, GROUP * g + GROUP):
                        dve.wait_ge(l_stat, t + 1)
                        dve.bn_aggr(moment[:, t, :], stat[:, t, :]).then_inc(l_moment, 1)
                    dve.wait_ge(l_moment, GROUP * g + GROUP)
                    dve.tensor_scalar(var_l[:, tiles], moment[:, tiles, 1], LN_EPS, None, ALU.add).then_inc(l_var, 1)
                for g in range(TILES // GROUP):
                    dve.wait_ge(l_rstd, g + 1)
                    for t in range(GROUP * g, GROUP * g + GROUP):
                        dve.tensor_scalar(final[:, t, :], total[:, t, :], moment[:, t, 0:1], rstd_l[:, t:t + 1],
                                          ALU.subtract, ALU.mult).then_inc(l_final, 1)

            @block.gpsimd
            def _(pool):
                for g in range(TILES // GROUP):
                    tiles = slice(GROUP * g, GROUP * g + GROUP)
                    pool.wait_ge(l_var, g + 1)
                    pool.tensor_tensor(rstd_l[:, tiles], var_l[:, tiles], minus_half[:, 0:GROUP], ALU.pow)\
                        .then_inc(l_rstd, 1)

            @block.sync
            def _(sp):
                for g in range(TILES // GROUP):
                    tiles = slice(GROUP * g, GROUP * g + GROUP)
                    sp.wait_ge(l_final, GROUP * g + GROUP)
                    sp.dma_start(out[0, 512 * g:512 * g + 512, :].rearrange("(t p) c -> p t c", p=TILE),
                                 final[:, tiles, :]).then_inc(stored, 16)
                sp.wait_ge(stored, 16 * (TILES // GROUP))


def position_tables():
    half = np.arange(0, HEAD, 2, dtype=np.float64)
    freq = 1.0 / 10000.0 ** (half / HEAD)
    t = np.arange(TOKENS, dtype=np.float64)
    angle = t[:, None] * freq[None, :]
    base = (half + 0.4 * HEAD) / (1.4 * HEAD)
    power = ((t % TILE) - TILE // 2) / (WINDOW // 2)
    scale = base[None, :] ** power[:, None]
    cos, sin = np.cos(angle), np.sin(angle)
    sign = np.concatenate([np.ones(HEAD // 2), -np.ones(HEAD // 2)])
    both = lambda a: np.concatenate([a, a], -1)
    tables = np.stack([both(cos * scale) * QK_SCALE, both(sin * scale) * sign * QK_SCALE,
                       both(cos / scale), both(sin / scale) * sign], 1)
    tables = tables.reshape(TILES, TILE, 4, HEAD).transpose(1, 0, 2, 3)
    carry = np.tile(np.concatenate([base, base]) ** (TILE // (WINDOW // 2)), 2)[:, None]
    return np.ascontiguousarray(tables, np.float32), np.ascontiguousarray(carry, np.float32)


def band_masks():
    a = np.arange(TILE)[:, None]
    c = np.arange(2 * WINDOW)[None, :]
    i = a % WINDOW
    hidden = (c - WINDOW > i) | (i > c)
    first = hidden | ((a < WINDOW) & (c < WINDOW))
    return np.stack([first, hidden], 1).astype(np.float32) * np.float32(MASKED_BIT)


def level_cuts():
    s = (np.arange(128) % WINDOW)[:, None]
    t = np.arange(WINDOW)[None, :]
    cuts = [(s == t) if b == 0 else ((t // b) % 2 == 1) & (s // b == t // b - 1) for b in MASKED]
    return np.stack(cuts, 1).astype(np.float32)


def kernel(**inputs):
    import concourse.bacc as bacc
    from concourse.bass_utils import run_bass_kernel_spmd

    a = {k.removeprefix("L0_"): np.ascontiguousarray(v) for k, v in inputs.items()}
    maa = [a["attn_time_maa_" + k] for k in "xwkvrg"]
    vectors = np.stack(maa + [a["attn_time_decay"], a["attn_time_faaaa"].reshape(-1)], 1)
    r_weights = np.stack([a["attn_W" + k] for k in "rkvgo"])
    r_norm = np.stack([a["attn_ln_w"], a["attn_ln_b"]])
    qk = np.stack([a["ffn_q_scale"], a["ffn_q_scale"], a["ffn_k_scale"], a["ffn_k_scale"]], 1)

    def rows(v, lead):
        wide = np.zeros((DEPTH, NC_ * 128) + v.shape[2:], v.dtype)
        wide[:, :FFN] = v
        return wide.reshape((DEPTH, NC_, 128) + v.shape[2:]).swapaxes(1, 2)

    ffn = np.concatenate([
        a["ffn_W1"],
        rows(a["ffn_W2"], DIM).reshape(DEPTH, 128, NC_ * DIM),
        a["ffn_ln_g"][:, :, None], a["ffn_ln_b"][:, :, None],
        rows(a["ffn_b1"][:, :FFN], 1), rows(a["ffn_b1"][:, FFN:], 1),
        a["ffn_b2"][:, :, None]], 2)
    tables, carry = position_tables()
    arrays = {
        "x": a["attn_x"], "vectors": vectors, "mix_w1": a["attn_time_maa_w1"], "mix_w2": a["attn_time_maa_w2"],
        "decay_w1": a["attn_time_decay_w1"], "decay_w2": a["attn_time_decay_w2"], "r_weights": r_weights,
        "r_norm": r_norm, "wqkv": a["ffn_Wqkv"], "wo": a["ffn_Wo"], "ffn": ffn, "qk_scales": qk,
        "positions": tables, "carry": carry, "ident": np.eye(128, dtype=np.float32), "band": band_masks(),
        "level_masks": level_cuts(),
    }
    arrays = {k + "_dram": np.ascontiguousarray(v) for k, v in arrays.items()}

    nc = bacc.Bacc("TRN2", target_bir_lowering=False, num_devices=1)
    args = [nc.dram_tensor(k, v.shape, mybir.dt.from_np(v.dtype), kind="ExternalInput").ap() for k, v in arrays.items()]
    out = nc.dram_tensor("out_dram", (1, TOKENS, DIM), F32, kind="ExternalOutput").ap()
    build(nc, *args, out)
    result = run_bass_kernel_spmd(nc, [arrays], core_ids=[0])
    return result.results[0]["out_dram"]
```
